# Optimizing a Trainium2 kernel written in Bass

```python
import numpy as np
import jax
import jax.numpy as jnp

def _softmax(x, axis=-1):
    return jax.nn.softmax(x, axis=axis)

def _gelu(x):
    return jax.nn.gelu(x, approximate=True)

def _silu(x):
    return jax.nn.silu(x)

def _sigmoid(x):
    return jax.nn.sigmoid(x)

def _layernorm(x, axis=-1, eps=1e-05):
    m = jnp.mean(x, axis=axis, keepdims=True)
    v = jnp.var(x, axis=axis, keepdims=True)
    return (x - m) / jnp.sqrt(v + eps)

def _scatter_add(tgt, idx, src, axis=0):
    return tgt.at[idx].add(src)

def _segment_sum(src, seg, n):
    return jax.ops.segment_sum(src, seg, n)
kernel_name = 'mk_lm_tower_d2_tok_ids256_r4_272980'

def setup_inputs(seed: int=0):
    np.random.seed(seed)
    _w = jnp.asarray

    def _rec_inputs():
        import jax
        import jax.numpy as jnp
        _rk = jax.random.key(seed)
        x = jax.random.randint(jax.random.fold_in(_rk, 1), (8, 512), 0, 100001, jnp.int32)
        return x
    x = _rec_inputs()

    def _L0_tok_setup():
        import jax, jax.numpy as jnp
        import numpy as np
        NUM_ITEMS = 25000
        D = 64
        FOURIER_DIM = 64
        VISIT_DIM = 24
        RESIDUAL_SCALE = 0.1
        LN_EPS = 1e-05

        def _layer_norm(x, gamma, beta):
            mu = jnp.mean(x, axis=-1, keepdims=True)
            var = jnp.mean(jnp.square(x - mu), axis=-1, keepdims=True)
            return (x - mu) * jax.lax.rsqrt(var + LN_EPS) * gamma + beta
        key = jax.random.key(seed)
        ks = jax.random.split(key, 12)
        item_ids = jax.random.randint(ks[0], (128, 512), 0, NUM_ITEMS + 1)
        emb_table = 0.02 * jax.random.normal(ks[1], (NUM_ITEMS + 1, D), dtype=jnp.float32)
        emb_table = emb_table.at[0].set(0.0)
        geo_table = jax.random.normal(ks[2], (NUM_ITEMS + 1, FOURIER_DIM), dtype=jnp.float32)
        visit_table = jax.random.uniform(ks[3], (NUM_ITEMS + 1, VISIT_DIM), dtype=jnp.float32)

        def xavier(k, fan_in, fan_out):
            lim = np.sqrt(6.0 / (fan_in + fan_out))
            return jax.random.uniform(k, (fan_in, fan_out), jnp.float32, -lim, lim)
        w_item = xavier(ks[4], D, D)
        b_item = jnp.zeros((D,), jnp.float32)
        w_geo = xavier(ks[5], FOURIER_DIM, D)
        b_geo = jnp.zeros((D,), jnp.float32)
        w_visit = xavier(ks[6], VISIT_DIM, D)
        b_visit = jnp.zeros((D,), jnp.float32)
        w_fuse = xavier(ks[7], 3 * D, D)
        b_fuse = jnp.zeros((D,), jnp.float32)
        ln_gamma = jnp.ones((D,), jnp.float32)
        ln_beta = jnp.zeros((D,), jnp.float32)
        return dict(item_ids=item_ids, emb_table=emb_table, geo_table=geo_table, visit_table=visit_table, w_item=w_item, b_item=b_item, w_geo=w_geo, b_geo=b_geo, w_visit=w_visit, b_visit=b_visit, w_fuse=w_fuse, b_fuse=b_fuse, ln_gamma=ln_gamma, ln_beta=ln_beta)
    _L0_tok_all = _L0_tok_setup()
    _L0_tok_in = {k: v for k, v in _L0_tok_all.items() if k in ('emb_table', 'geo_table', 'visit_table', 'w_item', 'b_item', 'w_geo', 'b_geo', 'w_visit', 'b_visit', 'w_fuse', 'b_fuse', 'ln_gamma', 'ln_beta')}
    del _L0_tok_all

    def _L0_attn_setup():
        import jax, jax.numpy as jnp
        import numpy as np
        DIM = 64
        HEADS = 4
        HEAD_DIM = DIM // HEADS
        SCALE = HEAD_DIM ** (-0.5)
        key = jax.random.key(seed)
        ks = jax.random.split(key, 9)
        B, N, C = (2, 1024, DIM)
        x = jax.random.normal(ks[0], (B, N, C), dtype=jnp.float32)
        lim = np.sqrt(6.0 / (C + C)).astype(np.float32)

        def w(k):
            return jax.random.uniform(k, (C, C), dtype=jnp.float32, minval=-lim, maxval=lim)
        return {'x': x, 'Wq': w(ks[1]), 'bq': jnp.zeros((C,), jnp.float32), 'Wk': w(ks[2]), 'bk': jnp.zeros((C,), jnp.float32), 'Wv': w(ks[3]), 'bv': jnp.zeros((C,), jnp.float32), 'Wo': w(ks[4]), 'bo': jnp.zeros((C,), jnp.float32)}
    _L0_attn_all = _L0_attn_setup()
    _L0_attn_in = {k: v for k, v in _L0_attn_all.items() if k in ('Wq', 'bq', 'Wk', 'bk', 'Wv', 'bv', 'Wo', 'bo')}
    del _L0_attn_all

    def _L0_ffn_setup():
        import jax, jax.numpy as jnp
        import numpy as np
        B, S, D, F, E, K = (8, 512, 64, 256, 8, 2)
        key = jax.random.key(seed)
        ks = jax.random.split(key, 10)
        s = 0.02
        return {'x': jax.random.normal(ks[0], (B, S, D), dtype=jnp.float32), 'Wr': jax.random.normal(ks[1], (D, E), dtype=jnp.float32) * s, 'W1s': jax.random.normal(ks[2], (D, F), dtype=jnp.float32) * s, 'b1s': jnp.zeros((F,), dtype=jnp.float32), 'W2s': jax.random.normal(ks[3], (F, D), dtype=jnp.float32) * s, 'b2s': jnp.zeros((D,), dtype=jnp.float32), 'W1p': jax.random.normal(ks[4], (E, D, F), dtype=jnp.float32) * s, 'b1p': jnp.zeros((E, F), dtype=jnp.float32), 'W2p': jax.random.normal(ks[5], (E, F, D), dtype=jnp.float32) * s, 'b2p': jnp.zeros((E, D), dtype=jnp.float32)}
    _L0_ffn_all = _L0_ffn_setup()
    _L0_ffn_in = {k: v for k, v in _L0_ffn_all.items() if k in ('Wr', 'W1s', 'b1s', 'W2s', 'b2s', 'W1p', 'b1p', 'W2p', 'b2p')}
    del _L0_ffn_all

    def _L1_attn_setup():
        import jax, jax.numpy as jnp
        import numpy as np
        from jax import lax
        B_, L_, D_ = (4, 512, 64)
        DI, NS, DC, DTR = (128, 16, 4, 16)
        DFF = 4 * D_

        def _layer_norm(x, g, b, eps=1e-05):
            m = jnp.mean(x, -1, keepdims=True)
            v = jnp.mean((x - m) ** 2, -1, keepdims=True)
            return (x - m) / jnp.sqrt(v + eps) * g + b

        def _mamba(x, in_proj_w, in_proj_b, conv_w, conv_b, x_proj_w, dt_proj_w, dt_proj_b, A_log, D_ssm, out_proj_w, out_proj_b):
            B, L, D = x.shape
            xz = x @ in_proj_w.T + in_proj_b
            xi, z = jnp.split(xz, 2, axis=-1)
            xc = jnp.transpose(xi, (0, 2, 1))
            xc = lax.conv_general_dilated(xc, conv_w[:, None, :], (1,), [(DC - 1, 0)], dimension_numbers=('NCH', 'OIH', 'NCH'), feature_group_count=DI)
            xi = jax.nn.silu(jnp.transpose(xc + conv_b[None, :, None], (0, 2, 1)))
            x_dbl = xi @ x_proj_w.T
            dt, Bs, Cs = jnp.split(x_dbl, [DTR, DTR + NS], axis=-1)
            dt = jax.nn.softplus(dt @ dt_proj_w.T + dt_proj_b)
            A = -jnp.exp(A_log)
            dA = jnp.exp(dt[..., None] * A)
            dBu = dt[..., None] * Bs[:, :, None, :] * xi[..., None]
            dA_t = jnp.moveaxis(dA, 1, 0)
            dBu_t = jnp.moveaxis(dBu, 1, 0)
            C_t = jnp.moveaxis(Cs, 1, 0)

            def step(h, inp):
                a, bu, c = inp
                h = a * h + bu
                y = jnp.einsum('bdn,bn->bd', h, c)
                return (h, y)
            h0 = jnp.zeros((B, DI, NS), x.dtype)
            _, ys = lax.scan(step, h0, (dA_t, dBu_t, C_t))
            y = jnp.moveaxis(ys, 0, 1) + xi * D_ssm
            y = y * jax.nn.silu(z)
            return y @ out_proj_w.T + out_proj_b
        key = jax.random.key(seed)
        ks = jax.random.split(key, 20)
        rn = lambda k, s, sc=0.02: jax.random.normal(k, s, jnp.float32) * sc
        return {'x': jax.random.normal(ks[0], (B_, L_, D_), jnp.float32), 'in_proj_w': rn(ks[1], (2 * DI, D_)), 'in_proj_b': jnp.zeros((2 * DI,), jnp.float32), 'conv_w': rn(ks[2], (DI, DC), 0.1), 'conv_b': jnp.zeros((DI,), jnp.float32), 'x_proj_w': rn(ks[3], (DTR + 2 * NS, DI)), 'dt_proj_w': rn(ks[4], (DI, DTR), 0.1), 'dt_proj_b': rn(ks[5], (DI,), 0.5), 'A_log': jnp.log(jnp.tile(jnp.arange(1, NS + 1, dtype=jnp.float32), (DI, 1))), 'D_ssm': jnp.ones((DI,), jnp.float32), 'out_proj_w': rn(ks[6], (D_, DI)), 'out_proj_b': jnp.zeros((D_,), jnp.float32), 'ln1_g': jnp.ones((D_,), jnp.float32), 'ln1_b': jnp.zeros((D_,), jnp.float32), 'fc1_w': rn(ks[7], (DFF, D_)), 'fc1_b': jnp.zeros((DFF,), jnp.float32), 'fc2_w': rn(ks[8], (D_, DFF)), 'fc2_b': jnp.zeros((D_,), jnp.float32), 'ln2_g': jnp.ones((D_,), jnp.float32), 'ln2_b': jnp.zeros((D_,), jnp.float32)}
    _L1_attn_all = _L1_attn_setup()
    _L1_attn_in = {k: v for k, v in _L1_attn_all.items() if k in ('in_proj_w', 'in_proj_b', 'conv_w', 'conv_b', 'x_proj_w', 'dt_proj_w', 'dt_proj_b', 'A_log', 'D_ssm', 'out_proj_w', 'out_proj_b', 'ln1_g', 'ln1_b', 'fc1_w', 'fc1_b', 'fc2_w', 'fc2_b', 'ln2_g', 'ln2_b')}
    del _L1_attn_all

    def _L1_ffn_setup():
        import jax, jax.numpy as jnp
        import numpy as np
        E = 8
        K = 2
        D = 64
        H = 128
        DOUT = 64
        EPS = 1e-05
        key = jax.random.key(seed)
        ks = jax.random.split(key, 9)
        s = 0.02
        return {'x': jax.random.normal(ks[0], (4, 2048, D), jnp.float32), 'gamma': 1.0 + 0.05 * jax.random.normal(ks[1], (D,), jnp.float32), 'beta': 0.05 * jax.random.normal(ks[2], (D,), jnp.float32), 'Wr': 0.01 * jax.random.normal(ks[3], (D, E), jnp.float32), 'br': jnp.zeros((E,), jnp.float32), 'W1': s * jax.random.normal(ks[4], (E, D, H), jnp.float32), 'b1': s * jax.random.normal(ks[5], (E, H), jnp.float32), 'W2': s * jax.random.normal(ks[6], (E, H, DOUT), jnp.float32), 'b2': s * jax.random.normal(ks[7], (E, DOUT), jnp.float32)}
    _L1_ffn_all = _L1_ffn_setup()
    _L1_ffn_in = {k: v for k, v in _L1_ffn_all.items() if k in ('gamma', 'beta', 'Wr', 'br', 'W1', 'b1', 'W2', 'b2')}
    del _L1_ffn_all
    return {'x': x, 'L0_tok_emb_table': _L0_tok_in['emb_table'], 'L0_tok_geo_table': _L0_tok_in['geo_table'], 'L0_tok_visit_table': _L0_tok_in['visit_table'], 'L0_tok_w_item': _L0_tok_in['w_item'], 'L0_tok_b_item': _L0_tok_in['b_item'], 'L0_tok_w_geo': _L0_tok_in['w_geo'], 'L0_tok_b_geo': _L0_tok_in['b_geo'], 'L0_tok_w_visit': _L0_tok_in['w_visit'], 'L0_tok_b_visit': _L0_tok_in['b_visit'], 'L0_tok_w_fuse': _L0_tok_in['w_fuse'], 'L0_tok_b_fuse': _L0_tok_in['b_fuse'], 'L0_tok_ln_gamma': _L0_tok_in['ln_gamma'], 'L0_tok_ln_beta': _L0_tok_in['ln_beta'], 'L0_attn_Wq': _L0_attn_in['Wq'], 'L0_attn_bq': _L0_attn_in['bq'], 'L0_attn_Wk': _L0_attn_in['Wk'], 'L0_attn_bk': _L0_attn_in['bk'], 'L0_attn_Wv': _L0_attn_in['Wv'], 'L0_attn_bv': _L0_attn_in['bv'], 'L0_attn_Wo': _L0_attn_in['Wo'], 'L0_attn_bo': _L0_attn_in['bo'], 'L0_ffn_Wr': _L0_ffn_in['Wr'], 'L0_ffn_W1s': _L0_ffn_in['W1s'], 'L0_ffn_b1s': _L0_ffn_in['b1s'], 'L0_ffn_W2s': _L0_ffn_in['W2s'], 'L0_ffn_b2s': _L0_ffn_in['b2s'], 'L0_ffn_W1p': _L0_ffn_in['W1p'], 'L0_ffn_b1p': _L0_ffn_in['b1p'], 'L0_ffn_W2p': _L0_ffn_in['W2p'], 'L0_ffn_b2p': _L0_ffn_in['b2p'], 'L1_attn_in_proj_w': _L1_attn_in['in_proj_w'], 'L1_attn_in_proj_b': _L1_attn_in['in_proj_b'], 'L1_attn_conv_w': _L1_attn_in['conv_w'], 'L1_attn_conv_b': _L1_attn_in['conv_b'], 'L1_attn_x_proj_w': _L1_attn_in['x_proj_w'], 'L1_attn_dt_proj_w': _L1_attn_in['dt_proj_w'], 'L1_attn_dt_proj_b': _L1_attn_in['dt_proj_b'], 'L1_attn_A_log': _L1_attn_in['A_log'], 'L1_attn_D_ssm': _L1_attn_in['D_ssm'], 'L1_attn_out_proj_w': _L1_attn_in['out_proj_w'], 'L1_attn_out_proj_b': _L1_attn_in['out_proj_b'], 'L1_attn_ln1_g': _L1_attn_in['ln1_g'], 'L1_attn_ln1_b': _L1_attn_in['ln1_b'], 'L1_attn_fc1_w': _L1_attn_in['fc1_w'], 'L1_attn_fc1_b': _L1_attn_in['fc1_b'], 'L1_attn_fc2_w': _L1_attn_in['fc2_w'], 'L1_attn_fc2_b': _L1_attn_in['fc2_b'], 'L1_attn_ln2_g': _L1_attn_in['ln2_g'], 'L1_attn_ln2_b': _L1_attn_in['ln2_b'], 'L1_ffn_gamma': _L1_ffn_in['gamma'], 'L1_ffn_beta': _L1_ffn_in['beta'], 'L1_ffn_Wr': _L1_ffn_in['Wr'], 'L1_ffn_br': _L1_ffn_in['br'], 'L1_ffn_W1': _L1_ffn_in['W1'], 'L1_ffn_b1': _L1_ffn_in['b1'], 'L1_ffn_W2': _L1_ffn_in['W2'], 'L1_ffn_b2': _L1_ffn_in['b2']}

def reference(x, L0_tok_emb_table, L0_tok_geo_table, L0_tok_visit_table, L0_tok_w_item, L0_tok_b_item, L0_tok_w_geo, L0_tok_b_geo, L0_tok_w_visit, L0_tok_b_visit, L0_tok_w_fuse, L0_tok_b_fuse, L0_tok_ln_gamma, L0_tok_ln_beta, L0_attn_Wq, L0_attn_bq, L0_attn_Wk, L0_attn_bk, L0_attn_Wv, L0_attn_bv, L0_attn_Wo, L0_attn_bo, L0_ffn_Wr, L0_ffn_W1s, L0_ffn_b1s, L0_ffn_W2s, L0_ffn_b2s, L0_ffn_W1p, L0_ffn_b1p, L0_ffn_W2p, L0_ffn_b2p, L1_attn_in_proj_w, L1_attn_in_proj_b, L1_attn_conv_w, L1_attn_conv_b, L1_attn_x_proj_w, L1_attn_dt_proj_w, L1_attn_dt_proj_b, L1_attn_A_log, L1_attn_D_ssm, L1_attn_out_proj_w, L1_attn_out_proj_b, L1_attn_ln1_g, L1_attn_ln1_b, L1_attn_fc1_w, L1_attn_fc1_b, L1_attn_fc2_w, L1_attn_fc2_b, L1_attn_ln2_g, L1_attn_ln2_b, L1_ffn_gamma, L1_ffn_beta, L1_ffn_Wr, L1_ffn_br, L1_ffn_W1, L1_ffn_b1, L1_ffn_W2, L1_ffn_b2):
    import jax
    import jax.numpy as jnp

    def _L0_tok_ref(item_ids, emb_table, geo_table, visit_table, w_item, b_item, w_geo, b_geo, w_visit, b_visit, w_fuse, b_fuse, ln_gamma, ln_beta):
        import jax, jax.numpy as jnp
        import numpy as np
        NUM_ITEMS = 25000
        D = 64
        FOURIER_DIM = 64
        VISIT_DIM = 24
        RESIDUAL_SCALE = 0.1
        LN_EPS = 1e-05

        def _layer_norm(x, gamma, beta):
            mu = jnp.mean(x, axis=-1, keepdims=True)
            var = jnp.mean(jnp.square(x - mu), axis=-1, keepdims=True)
            return (x - mu) * jax.lax.rsqrt(var + LN_EPS) * gamma + beta
        gelu = lambda x: jax.nn.gelu(x, approximate=False)
        safe_ids = jnp.clip(item_ids, 0, emb_table.shape[0] - 1)
        item_emb = emb_table[safe_ids]
        fourier_feat = geo_table[safe_ids]
        visit_feat = visit_table[safe_ids]
        item_h = gelu(item_emb @ w_item + b_item)
        geo_h = gelu(fourier_feat @ w_geo + b_geo)
        visit_h = gelu(visit_feat @ w_visit + b_visit)
        cat = jnp.concatenate([item_h, geo_h, visit_h], axis=-1)
        fused = _layer_norm(gelu(cat @ w_fuse + b_fuse), ln_gamma, ln_beta)
        valid_mask = (item_ids != 0)[..., None].astype(fused.dtype)
        fused = fused * valid_mask
        return item_emb + RESIDUAL_SCALE * fused

    def _L0_attn_ref(x, Wq, bq, Wk, bk, Wv, bv, Wo, bo):
        import jax, jax.numpy as jnp
        import numpy as np
        DIM = 64
        HEADS = 4
        HEAD_DIM = DIM // HEADS
        SCALE = HEAD_DIM ** (-0.5)
        B, N, C = x.shape
        x = jnp.clip(x, -10000.0, 10000.0)

        def heads(t):
            return t.reshape(B, N, HEADS, HEAD_DIM).transpose(0, 2, 1, 3)
        q = heads((x @ Wq.T + bq).astype(jnp.float32))
        k = heads((x @ Wk.T + bk).astype(jnp.float32))
        v = heads((x @ Wv.T + bv).astype(jnp.float32))
        attn = jnp.einsum('bhnd,bhmd->bhnm', q, k) * SCALE
        attn = jax.nn.softmax(attn, axis=-1)
        out = jnp.einsum('bhnm,bhmd->bhnd', attn, v)
        out = out.transpose(0, 2, 1, 3).reshape(B, N, C)
        out = out.astype(jnp.bfloat16).astype(jnp.float32)
        return out @ Wo.T + bo

    def _L0_ffn_ref(x, Wr, W1s, b1s, W2s, b2s, W1p, b1p, W2p, b2p):
        import jax, jax.numpy as jnp
        import numpy as np
        B, S, D, F, E, K = (8, 512, 64, 256, 8, 2)
        gelu = lambda t: jax.nn.gelu(t, approximate=False)
        shared = gelu(x @ W1s + b1s) @ W2s + b2s
        rw = jax.nn.softmax(x @ Wr, axis=-1)
        topw, topi = jax.lax.top_k(rw, K)
        topw = topw / jnp.sum(topw, axis=-1, keepdims=True)
        mask = jnp.sum(jax.nn.one_hot(topi, E, dtype=topw.dtype) * topw[..., None], axis=-2)
        h = gelu(jnp.einsum('bsd,edf->bsef', x, W1p) + b1p)
        priv = jnp.einsum('bsef,efd->bsed', h, W2p) + b2p
        routed = jnp.einsum('bsed,bse->bsd', priv, mask)
        return shared + routed

    def _L1_attn_ref(x, in_proj_w, in_proj_b, conv_w, conv_b, x_proj_w, dt_proj_w, dt_proj_b, A_log, D_ssm, out_proj_w, out_proj_b, ln1_g, ln1_b, fc1_w, fc1_b, fc2_w, fc2_b, ln2_g, ln2_b):
        import jax, jax.numpy as jnp
        import numpy as np
        from jax import lax
        B_, L_, D_ = (4, 512, 64)
        DI, NS, DC, DTR = (128, 16, 4, 16)
        DFF = 4 * D_

        def _layer_norm(x, g, b, eps=1e-05):
            m = jnp.mean(x, -1, keepdims=True)
            v = jnp.mean((x - m) ** 2, -1, keepdims=True)
            return (x - m) / jnp.sqrt(v + eps) * g + b

        def _mamba(x, in_proj_w, in_proj_b, conv_w, conv_b, x_proj_w, dt_proj_w, dt_proj_b, A_log, D_ssm, out_proj_w, out_proj_b):
            B, L, D = x.shape
            xz = x @ in_proj_w.T + in_proj_b
            xi, z = jnp.split(xz, 2, axis=-1)
            xc = jnp.transpose(xi, (0, 2, 1))
            xc = lax.conv_general_dilated(xc, conv_w[:, None, :], (1,), [(DC - 1, 0)], dimension_numbers=('NCH', 'OIH', 'NCH'), feature_group_count=DI)
            xi = jax.nn.silu(jnp.transpose(xc + conv_b[None, :, None], (0, 2, 1)))
            x_dbl = xi @ x_proj_w.T
            dt, Bs, Cs = jnp.split(x_dbl, [DTR, DTR + NS], axis=-1)
            dt = jax.nn.softplus(dt @ dt_proj_w.T + dt_proj_b)
            A = -jnp.exp(A_log)
            dA = jnp.exp(dt[..., None] * A)
            dBu = dt[..., None] * Bs[:, :, None, :] * xi[..., None]
            dA_t = jnp.moveaxis(dA, 1, 0)
            dBu_t = jnp.moveaxis(dBu, 1, 0)
            C_t = jnp.moveaxis(Cs, 1, 0)

            def step(h, inp):
                a, bu, c = inp
                h = a * h + bu
                y = jnp.einsum('bdn,bn->bd', h, c)
                return (h, y)
            h0 = jnp.zeros((B, DI, NS), x.dtype)
            _, ys = lax.scan(step, h0, (dA_t, dBu_t, C_t))
            y = jnp.moveaxis(ys, 0, 1) + xi * D_ssm
            y = y * jax.nn.silu(z)
            return y @ out_proj_w.T + out_proj_b
        gelu = lambda t: jax.nn.gelu(t, approximate=False)
        ssm = _mamba(x, in_proj_w, in_proj_b, conv_w, conv_b, x_proj_w, dt_proj_w, dt_proj_b, A_log, D_ssm, out_proj_w, out_proj_b)
        y = _layer_norm(x + ssm, ln1_g, ln1_b)
        ffn = gelu(gelu(y @ fc1_w.T + fc1_b) @ fc2_w.T + fc2_b)
        return _layer_norm(y + ffn, ln2_g, ln2_b)

    def _L1_ffn_ref(x, gamma, beta, Wr, br, W1, b1, W2, b2):
        import jax, jax.numpy as jnp
        import numpy as np
        E = 8
        K = 2
        D = 64
        H = 128
        DOUT = 64
        EPS = 1e-05
        mu = jnp.mean(x, axis=-1, keepdims=True)
        var = jnp.mean(jnp.square(x - mu), axis=-1, keepdims=True)
        xn = (x - mu) * jax.lax.rsqrt(var + EPS) * gamma + beta
        logits = jnp.einsum('bsd,de->bse', xn, Wr) + br
        top_vals, top_idx = jax.lax.top_k(logits, K)
        w = jax.nn.softmax(top_vals, axis=-1)
        w_full = jnp.einsum('bsk,bske->bse', w, jax.nn.one_hot(top_idx, E, dtype=w.dtype))
        y = jnp.zeros(x.shape[:-1] + (DOUT,), x.dtype)
        for e in range(E):
            h = jax.nn.gelu(jnp.einsum('bsd,dh->bsh', xn, W1[e]) + b1[e], approximate=False)
            y_e = jnp.einsum('bsh,hd->bsd', h, W2[e]) + b2[e]
            y = y + y_e * w_full[..., e, None]
        return y
    h = _L0_tok_ref(x, L0_tok_emb_table, L0_tok_geo_table, L0_tok_visit_table, L0_tok_w_item, L0_tok_b_item, L0_tok_w_geo, L0_tok_b_geo, L0_tok_w_visit, L0_tok_b_visit, L0_tok_w_fuse, L0_tok_b_fuse, L0_tok_ln_gamma, L0_tok_ln_beta)
    h = h + _L0_attn_ref(_layernorm(h, axis=-1), L0_attn_Wq, L0_attn_bq, L0_attn_Wk, L0_attn_bk, L0_attn_Wv, L0_attn_bv, L0_attn_Wo, L0_attn_bo)
    h = h + _L0_ffn_ref(_layernorm(h, axis=-1), L0_ffn_Wr, L0_ffn_W1s, L0_ffn_b1s, L0_ffn_W2s, L0_ffn_b2s, L0_ffn_W1p, L0_ffn_b1p, L0_ffn_W2p, L0_ffn_b2p)
    h = h + _L1_attn_ref(_layernorm(h, axis=-1), L1_attn_in_proj_w, L1_attn_in_proj_b, L1_attn_conv_w, L1_attn_conv_b, L1_attn_x_proj_w, L1_attn_dt_proj_w, L1_attn_dt_proj_b, L1_attn_A_log, L1_attn_D_ssm, L1_attn_out_proj_w, L1_attn_out_proj_b, L1_attn_ln1_g, L1_attn_ln1_b, L1_attn_fc1_w, L1_attn_fc1_b, L1_attn_fc2_w, L1_attn_fc2_b, L1_attn_ln2_g, L1_attn_ln2_b)
    h = h + _L1_ffn_ref(_layernorm(h, axis=-1), L1_ffn_gamma, L1_ffn_beta, L1_ffn_Wr, L1_ffn_br, L1_ffn_W1, L1_ffn_b1, L1_ffn_W2, L1_ffn_b2)
    return h

_drawn_inputs = setup_inputs


def setup_inputs(seed=0):
    import zlib

    import numpy as np

    out = dict(_drawn_inputs(seed))
    spreads = {'L0_tok_b_item': (0.0, 0.1),
     'L0_tok_b_geo': (0.0, 0.1),
     'L0_tok_b_visit': (0.0, 0.1),
     'L0_tok_b_fuse': (0.0, 0.1),
     'L0_tok_ln_gamma': (1.0, 0.2),
     'L0_tok_ln_beta': (0.0, 0.1),
     'L0_attn_bq': (0.0, 0.661),
     'L0_attn_bk': (0.0, 2.0),
     'L0_attn_bv': (0.0, 0.1),
     'L0_attn_bo': (0.0, 0.1),
     'L0_ffn_b1s': (0.0, 0.392),
     'L0_ffn_b2s': (0.0, 0.1),
     'L0_ffn_b1p': (0.0, 0.603),
     'L0_ffn_b2p': (0.0, 0.1),
     'L1_attn_in_proj_b': (0.0, 0.8),
     'L1_attn_conv_b': (0.0, 0.8),
     'L1_attn_D_ssm': (1.0, 0.6),
     'L1_attn_out_proj_b': (0.0, 2.0),
     'L1_attn_ln1_g': (1.0, 0.2),
     'L1_attn_ln1_b': (0.0, 0.1),
     'L1_attn_fc1_b': (0.0, 0.8),
     'L1_attn_fc2_b': (0.0, 0.284),
     'L1_attn_ln2_g': (1.0, 0.2),
     'L1_attn_ln2_b': (0.0, 0.1),
     'L1_ffn_br': (0.0, 0.8)}
    factors = {'L0_tok_w_item': 2.805,
     'L0_ffn_W1p': 2.795,
     'L1_attn_in_proj_w': 8.0,
     'L1_attn_conv_w': 8.0,
     'L1_attn_x_proj_w': 8.0,
     'L1_attn_dt_proj_w': 8.0,
     'L1_attn_dt_proj_b': 8.0,
     'L1_attn_A_log': 8.0,
     'L1_attn_out_proj_w': 8.0,
     'L1_attn_fc1_w': 8.0,
     'L1_attn_fc2_w': 6.774,
     'L1_ffn_gamma': 8.0,
     'L1_ffn_beta': 8.0,
     'L1_ffn_Wr': 8.0,
     'L1_ffn_W1': 7.394,
     'L1_ffn_b1': 23.628,
     'L1_ffn_W2': 8.0,
     'L1_ffn_b2': 29.894}
    for name, (base, spread) in spreads.items():
        noise = np.random.default_rng([zlib.crc32(name.encode()), seed]).standard_normal(out[name].shape)
        drawn = base * np.exp(spread * noise) if base else spread * noise
        out[name] = jnp.asarray(drawn.astype(out[name].dtype))
    for name, factor in factors.items():
        out[name] = (out[name] * factor).astype(out[name].dtype)
    return out
```

```python
from contextlib import ExitStack

import numpy as np
import concourse.bass as bass
from concourse import mybir

NB, S, D = 8, 512, 64
HALF = S // 2
NT = S // 128
NH, DH = 4, 16
F0, E, F1 = 256, 8, 128
DI, NS, DC, DTR = 128, 16, 4, 16
VIS = 24
ROW = 2 * D + VIS
LN_EPS = 1e-5
NLN = 8
GROUPS = DI * NS // 128
N_ITEMS = 25001

WIDTHS = [
    ("w_eg", 128), ("w_vis", 64), ("w_f1", 64), ("w_f2", 64),
    ("w_qk", 128), ("w_v", 128), ("bv", S), ("w_o", 64),
    ("wr0", E), ("w1_0", 9 * F0), ("w2_0", 18 * D),
    ("w_inx", 128), ("w_inz", 128), ("w_xdt", 16), ("w_xb", 128), ("w_xc", 128), ("w_dt", 128), ("w_out", 64),
    ("fc1", 256), ("fc2", 128), ("wr1", E), ("br1", NT * E), ("w1_1", E * F1), ("w2_1", E * D),
    ("iota", NT * E),
    ("b_eg", 1), ("b_vis", 1), ("b_f", 1), ("g_t", 1), ("be_t", 1), ("b_qk", 1), ("b_o", 1),
    ("b1_0", 18), ("b2_0", 9), ("b_inx", 1), ("b_inz", 1), ("conv_w", DC), ("conv_b", 1), ("b_dt", 1),
    ("a_log", GROUPS), ("d_ssm", 1), ("b_out", 1), ("g1", 1), ("be1", 1), ("b_fc1", 2), ("b_fc2", 1),
    ("g2", 1), ("be2", 1), ("g_m", 1), ("be_m", 1), ("b1_1", E), ("b2_1", E),
]
AT = {name: (sum(w for _, w in WIDTHS[:n]), width) for n, (name, width) in enumerate(WIDTHS)}
WCOLS = sum(w for _, w in WIDTHS)

PER = {
    "ids_clipped": 1, "valid_ready": 1, "rows_in": 16 * NT, "tok_transposed": 1, "eg_ready": 1, "vis_ready": 1,
    "embp_ready": 1, "feat_done": 1, "cat_ready": 2, "fuse_done": 1, "fuse_act": 1, "valid_bc": 1,
    "tok_affine": 1, "tok_masked": 1, "h0_ready": 1,
    "ln_centred": NLN, "ln_squared": NLN, "ln_kept": NLN, "ln_var": NLN, "ln_vareps": NLN, "ln_rstd": NLN,
    "ln_bc": NLN, "ln_out": NLN,
    "qk_done": 1, "v_done": 1, "qk_full": 1, "qk_hi": 1, "qk_r": 1, "qk_mid": 1, "qk_lo": 1, "v_ready": 1,
    "stack_in": 16 * 12 * NH, "s1_done": 8, "max_done": 8, "max_split": 5, "max_turned": 1, "max_in": 1,
    "s2_done": 8, "exp_done": 8, "pv_done": NT, "o_ready": 1, "den_done": 1, "rec_ready": 1, "o_bf": 1,
    "wo_done": 1, "h1_ready": 1,
    "lg0_done": 1, "lg0_in": 1, "gate0": 1, "top0": NT, "idx0": NT, "r0": 9, "e0": 1, "mask0": 1, "mbc0_done": 1, "mbc0_in": 1,
    "lg1_done": 1, "lg1_in": 1, "gate1": 1, "top1": NT, "idx1": NT, "r1": 9, "e1": 1, "mask1": 1, "mbc1_done": 2, "mbc1_in": 2,
    "hid0_done": 9, "gelu0": 18, "w2_0_done": 9, "y0": 9, "acc0": 8,
    "in_done": 1, "xi_ready": 1, "sz_ready": 1, "conv": 4, "u_ready": 1, "xp_done": 1, "dtl_ready": 1, "br_ready": 1,
    "cr_ready": 1, "dtp_done": 1, "sp_abs": 1, "sp_exp": 1, "sp_relu": 1, "sp_u1": 1, "sp_ln": 1, "sp_r": 1, "sp_t": 1,
    "dt_ready": 1, "dx_ready": 1, "spread": GROUPS, "da_ready": GROUPS, "dbu_ready": GROUPS, "scanned": GROUPS,
    "hc_ready": GROUPS, "y_sum": 4, "y1": 1, "y2": 1, "out_done": 1, "s_ready": 1, "yln": 1,
    "fc1_done": 1, "fc1_act": 2, "fc2_done": 1, "ff_ready": 1, "s2_ready": 1, "yy": 1, "h3_ready": 1, "x6_ready": 1,
    "hid1_done": E // 2, "gelu1": E, "w2_1_done": E // 2, "y1e": E, "acc1": E, "out_turned": 1, "out_ready": 1, "stored": 32,
}


def build_tower(nc: bass.Bass, ids: bass.AP, table: bass.AP, weights: bass.AP, out: bass.AP):
    fp32, bf16 = mybir.dt.float32, mybir.dt.bfloat16
    i32, u32 = mybir.dt.int32, mybir.dt.uint32
    ALU, ACT, AX = mybir.AluOpType, mybir.ActivationFunctionType, mybir.AxisListType

    ctx = ExitStack()
    with ctx:
        def sb(name, shape, dt=fp32):
            return ctx.enter_context(nc.sbuf_tensor(name, shape, dt))

        wts = sb("wts", [128, WCOLS])

        def w(name, rows=slice(0, 128), cols=None):
            at, width = AT[name]
            lo, hi = cols if cols else (0, width)
            return wts[rows, at + lo:at + hi]

        ident = sb("ident", [128, 128])
        identb = sb("identb", [128, 128], bf16)
        centre = sb("centre", [128, 128])
        halfmean = sb("halfmean", [128, 2])
        sel_den = sb("sel_den", [128, 128])
        sel_dn = sb("sel_dn", [128, 4, 128])
        sel_y = sb("sel_y", [128, 4, 32])
        wo3 = sb("wo3", [128, 3, 64], bf16)
        wo_r = sb("wo_r", [128, 2, 64])
        neg_half = sb("neg_half", [128, 4])
        e_base = sb("e_base", [128, 4])
        a_neg = sb("a_neg", [128, GROUPS])
        a_exp = sb("a_exp", [128, GROUPS])
        gate = sb("gate", [128, 2])
        gpool = sb("gpool", [128, 4])
        ids_all = sb("ids_all", [128, NB * NT], i32)

        ids_c = sb("ids_c", [128, NT], i32)
        valid = sb("valid", [128, NT])
        rows = sb("rows", [128, NT, ROW])
        eg = sb("eg", [128, S])
        vis = sb("vis", [VIS, S])
        embp = sb("embp", [128, HALF])
        cat1 = sb("cat1", [128, S])
        cat2 = sb("cat2", [64, S])
        f0 = sb("f0", [128, HALF])
        tok_a = sb("tok_a", [128, HALF])
        tok_m = sb("tok_m", [128, HALF])
        h0, h1, h2, h3, h4 = (sb(f"h{i}", [128, HALF]) for i in range(5))
        ln_sq = sb("ln_sq", [128, 2, HALF])
        ln_xc = sb("ln_xc", [128, 2, HALF])
        ln_ve = sb("ln_ve", [128, 2, NT])
        ln_rs = sb("ln_rs", [128, 2, NT])
        ln_o = sb("ln_o", [128, NLN, HALF])
        qkf = sb("qkf", [128, S])
        qkr = sb("qkr", [128, S])
        part = sb("part", [128, 3, S], bf16)
        QS = sb("QS", [128, NH, S], bf16)
        KS = sb("KS", [128, NH, S], bf16)
        vsb = sb("vsb", [128, NT, 128])
        nmax = sb("nmax", [128, 4 * NH])
        nmax_r = sb("nmax_r", [128, 2, 4 * NH])
        M = sb("M", [128, 4 * NH, 32], bf16)
        P = sb("P", [128, 4, 2, S])
        osb, rec = qkr, qkf
        obf = sb("obf", [128, S], bf16)
        lg = sb("lg", [128, 2, NT, E])
        top = sb("top", [128, 2, NT, 8])
        idx = sb("idx", [128, 2, NT, 8], u32)
        idxf = sb("idxf", [128, 2, NT, 2])
        eq = sb("eq", [128, 2, 2, NT, E])
        dlt = sb("dlt", [128, 2, NT])
        ex2 = sb("ex2", [128, 2, NT])
        ssum = sb("ssum", [128, 2, NT])
        w12 = sb("w12", [128, 2, 2, NT])
        mk = sb("mk", [128, 2, 3, NT, E])
        mbc = sb("mbc", [128, 2, E, HALF])
        hid = sb("hid", [128, 4, 2, HALF])
        ye = sb("ye", [128, 2, HALF])
        acc = sb("acc", [128, 2, HALF])
        hidb = sb("hidb", [128, 4, 2, HALF])
        yeb = sb("yeb", [128, 2, HALF])
        accb = sb("accb", [128, 2, HALF])
        xip = sb("xip", [128, DC - 1 + S])
        sz = sb("sz", [128, S])
        cv = sb("cv", [128, 2, S])
        u = sb("u", [128, S])
        dtl = sb("dtl", [DTR, S])
        Br = sb("Br", [128, S])
        Cr = sb("Cr", [128, S])
        sp = sb("sp", [128, 6, S])
        dt = sb("dt", [128, S])
        dx = sb("dx", [128, S])
        dA = sb("dA", [128, 2, S])
        dBu = sb("dBu", [128, 2, S])
        hst = sb("hst", [128, 2, S])
        hc = sb("hc", [128, 4, S])
        y1, y2 = sp[:, 2, :], sp[:, 3, :]
        sres = sb("sres", [128, HALF])
        yl = sb("yl", [128, HALF])
        ff = sb("ff", [128, HALF])
        s2 = sb("s2", [128, HALF])
        yy = sb("yy", [128, HALF])
        x6 = sb("x6", [128, HALF])
        outs = sb("outs", [128, 2, 128])

        F = ctx.enter_context(nc.psum_tensor("F", [128, 5, 512], fp32))
        G = ctx.enter_context(nc.psum_tensor("G", [128, 3, 512], fp32))
        turned = F[:, 0:2, :].bitcast(bf16).rearrange("p k (i q) -> p (k i) q", q=S)

        sem = {name: ctx.enter_context(nc.semaphore(name)) for name in PER}
        s_w = ctx.enter_context(nc.semaphore("weights_in"))
        s_ids = ctx.enter_context(nc.semaphore("ids_in"))
        s_c = ctx.enter_context(nc.semaphore("consts_pool"))
        s_v = ctx.enter_context(nc.semaphore("consts_dve"))
        s_ae = ctx.enter_context(nc.semaphore("a_exp_ready"))
        made = {}
        block = ctx.enter_context(nc.Block())

        def nth(name, b, k=None):
            return PER[name] * b + (PER[name] if k is None else k)

        def not_first(b):
            return not (isinstance(b, int) and b == 0)

        def half(x):
            return slice(64 * x, 64 * x + 64)

        def ln_bank(j):
            return F[:, 4, :] if j < 3 else G[:, 2, :]

        @block.sync
        def _(sp_):
            sp_.dma_start(ids_all[:, :], ids).then_inc(s_ids, 16)
            sp_.dma_start(wts[:, :], weights).then_inc(s_w, 16)

            def row(b):
                for n, (qp, kp) in enumerate(((0, 0), (1, 0), (0, 1), (1, 1), (2, 0), (0, 2))):
                    for h in range(NH):
                        if n == 0 and h == 0:
                            sp_.wait_ge(sem["qk_lo"], nth("qk_lo", b))
                        sp_.dma_start(QS[16 * n:16 * n + 16, h, :], part[16 * h:16 * h + 16, qp, :]).then_inc(sem["stack_in"], 16)
                        sp_.dma_start(KS[16 * n:16 * n + 16, h, :], part[64 + 16 * h:80 + 16 * h, kp, :]).then_inc(sem["stack_in"], 16)
                sp_.wait_ge(sem["out_ready"], nth("out_ready", b))
                bs = bass.ds(b, 1) if not isinstance(b, int) else slice(b, b + 1)
                for c in range(2):
                    dst = out[bs, :, :].rearrange("o (x c p) d -> c p (o x) d", x=2, c=2)[c]
                    sp_.dma_start(dst, outs[:, c, :].rearrange("p (x d) -> p x d", x=2)).then_inc(sem["stored"], 16)

            row(0)
            with sp_.Fori(1, NB) as b:
                row(b)
            sp_.wait_ge(sem["stored"], 32 * NB)

        @block.gpsimd
        def _(g):
            cnt = [0]

            def link(ins):
                cnt[0] += 1
                ins.then_inc(s_c, 1)
                g.wait_ge(s_c, cnt[0])

            def select(t, fill, base, pattern, mult):
                link(g.affine_select(out=t, in_=t, compare_op=ALU.not_equal, fill=fill, base=base,
                                     pattern=pattern, channel_multiplier=mult))

            link(g.memset(ident[:, :], 0.0))
            select(ident[:, :], 1.0, 0, [[-1, 128]], 1)
            link(g.memset(centre[:, :], 0.0))
            for x in range(2):
                link(g.memset(centre[half(x), half(x)], -1.0 / D))
            select(centre[:, :], 1.0 - 1.0 / D, 0, [[-1, 128]], 1)
            link(g.memset(halfmean[:, :], 0.0))
            for x in range(2):
                link(g.memset(halfmean[half(x), x:x + 1], 1.0 / D))
            link(g.memset(sel_den[:, :], 0.0))
            v = sel_den[:, :].rearrange("p (h i) -> p h i", i=32)
            select(v, 1.0, -16, [[-32, 4], [0, 32]], 1)
            link(g.memset(sel_dn[:, :, :], 0.0))
            for r in range(4):
                q = slice(32 * r, 32 * r + 32)
                v = sel_dn[q, :, :].rearrange("p s (j n) -> p s j n", n=NS)
                select(v, 1.0, 0, [[-8, 4], [-1, 8], [0, NS]], 1)
            link(g.memset(sel_y[:, :, :], 0.0))
            link(g.memset(neg_half[:, :], -0.5))
            link(g.memset(e_base[:, :], float(np.e)))
            link(g.memset(M[:, :, :], 0.0))
            link(g.memset(KS[96:128, :, :], 1.0))
            link(g.memset(xip[:, 0:DC - 1], 0.0))
            link(g.memset(gpool[:, :], 0.0))
            made["pool"] = cnt[0]

            def rstd(j, b):
                g.wait_ge(sem["ln_vareps"], nth("ln_vareps", b, j + 1))
                n = j % 2
                g.tensor_tensor(ln_rs[:, n, :], ln_ve[:, n, :], neg_half[:, :], ALU.pow).then_inc(sem["ln_rstd"], 1)

            def row(b):
                if not_first(b):
                    g.wait_ge(sem["tok_transposed"], nth("tok_transposed", b, 0))
                g.wait_ge(sem["ids_clipped"], nth("ids_clipped", b))
                g.tensor_tensor(gpool[:, :], neg_half[:, :], neg_half[:, :], ALU.add)
                for t in range(NT):
                    g.indirect_dma_start(rows[:, t, :], None, table[:, :], bass.IndirectOffsetOnAxis(ap=ids_c[:, t:t + 1], axis=0)).then_inc(sem["rows_in"], 16)
                rstd(0, b)
                rstd(1, b)
                rstd(2, b)
                router(0, b)
                for e in range(8):
                    g.wait_ge(sem["y0"], nth("y0", b, e + 2))
                    if e:
                        g.wait_ge(sem["acc0"], nth("acc0", b, e))
                    o = h2[:, :] if e == 7 else acc[:, (e + 1) % 2, :]
                    g.tensor_tensor(o, acc[:, e % 2, :], ye[:, e % 2, :], ALU.add).then_inc(sem["acc0"], 1)
                rstd(3, b)
                for k in range(GROUPS):
                    g.wait_ge(sem["scanned"], nth("scanned", b, k + 1))
                    if k == 0:
                        g.wait_ge(sem["cr_ready"], nth("cr_ready", b))
                        if not_first(b):
                            g.wait_ge(sem["y_sum"], nth("y_sum", b, 0))
                    if k >= 4:
                        g.wait_ge(sem["y_sum"], nth("y_sum", b, k // 4))
                    g.tensor_tensor(hc[:, k % 4, :], hst[:, k % 2, :], Cr[:, :], ALU.mult).then_inc(sem["hc_ready"], 1)
                for j in range(4, 8):
                    rstd(j, b)
                router(1, b)
                for e in range(8):
                    g.wait_ge(sem["y1e"], nth("y1e", b, e + 1))
                    if e:
                        g.wait_ge(sem["acc1"], nth("acc1", b, e))
                    o = h4[:, :] if e == 7 else accb[:, (e + 1) % 2, :]
                    i = h3[:, :] if e == 0 else accb[:, e % 2, :]
                    g.tensor_tensor(o, i, yeb[:, e % 2, :], ALU.add).then_inc(sem["acc1"], 1)

            def router(n, b):
                g.wait_ge(sem[f"r{n}"], nth(f"r{n}", b, 1))
                g.tensor_tensor(ex2[:, n, :], e_base[:, :], dlt[:, n, :], ALU.pow).then_inc(sem[f"e{n}"], 1)

            row(0)
            with g.Fori(1, NB) as b:
                row(b)

        @block.scalar
        def _(a):
            act = nc.scalar.activation
            a.wait_ge(s_w, 16)
            act(a_exp[:, :], w("a_log"), ACT.Exp).then_inc(s_ae, 1)

            def ln(j, b):
                bank = ln_bank(j)
                n = j % 2
                a.wait_ge(sem["ln_centred"], nth("ln_centred", b, j + 1))
                act(ln_xc[:, n, :], bank[:, 0:HALF], ACT.Copy).then_inc(sem["ln_kept"], 1)
                act(ln_sq[:, n, :], bank[:, 0:HALF], ACT.Square).then_inc(sem["ln_squared"], 1)

            def row(b):
                a.wait_ge(sem["tok_transposed"], nth("tok_transposed", b))
                act(eg[:, :], F[:, 0, :], ACT.Copy).then_inc(sem["eg_ready"], 1)
                a.wait_ge(sem["feat_done"], nth("feat_done", b))
                act(cat1[:, :], F[:, 3, :], ACT.Gelu, bias=w("b_eg")).then_inc(sem["cat_ready"], 1)
                act(cat2[:, :], F[0:64, 4, :], ACT.Gelu, bias=w("b_vis", slice(0, 64))).then_inc(sem["cat_ready"], 1)
                a.wait_ge(sem["fuse_done"], nth("fuse_done", b))
                act(f0[:, :], F[:, 1, 0:HALF], ACT.Gelu, bias=w("b_f")).then_inc(sem["fuse_act"], 1)
                ln(0, b)
                ln(1, b)
                a.wait_ge(sem["qk_done"], nth("qk_done", b))
                act(qkf[:, :].rearrange("p (x c) -> p x c", x=2), F[:, 0:2, 0:HALF], ACT.Identity, bias=w("b_qk")).then_inc(sem["qk_full"], 1)
                if not_first(b):
                    a.wait_ge(sem["stack_in"], nth("stack_in", b, 0))
                a.wait_ge(sem["qk_full"], nth("qk_full", b))
                act(part[:, 0, :], qkf[:, :], ACT.Copy).then_inc(sem["qk_hi"], 1)
                a.wait_ge(sem["qk_r"], nth("qk_r", b))
                act(part[:, 1, :], qkr[:, :], ACT.Copy).then_inc(sem["qk_mid"], 1)
                for n in range(8):
                    a.wait_ge(sem["s2_done"], nth("s2_done", b, n + 1))
                    if n >= 4:
                        a.wait_ge(sem["pv_done"], nth("pv_done", b, (n - 4) // 2 + 1))
                    act(P[:, n % 4, :, :], F[:, 2 * (n % 2):2 * (n % 2) + 2, :], ACT.Exp, scale=DH ** -0.5).then_inc(sem["exp_done"], 1)
                ln(2, b)
                a.wait_ge(sem["mbc0_done"], nth("mbc0_done", b))
                act(mbc[:, 0, :, :], F[:, 0:4, :].rearrange("p k (i c) -> p (k i) c", i=2), ACT.Copy).then_inc(sem["mbc0_in"], 1)
                for e in range(9):
                    a.wait_ge(sem["hid0_done"], nth("hid0_done", b, e + 1))
                    for ch in range(2):
                        if e >= 2 and ch == 0:
                            a.wait_ge(sem["w2_0_done"], nth("w2_0_done", b, e - 1))
                        p = 2 * (e % 2)
                        act(hid[:, p + ch, :, :], F[:, p:p + 2, HALF * ch:HALF * ch + HALF], ACT.Gelu,
                            bias=w("b1_0", cols=(2 * e + ch, 2 * e + ch + 1))).then_inc(sem["gelu0"], 1)
                ln(3, b)
                a.wait_ge(sem["in_done"], nth("in_done", b))
                act(xip[:, DC - 1:].rearrange("p (x c) -> p x c", x=2), G[:, 0:2, 0:HALF], ACT.Identity, bias=w("b_inx")).then_inc(sem["xi_ready"], 1)
                act(sz[:, :].rearrange("p (x c) -> p x c", x=2), G[:, 0:2, HALF:S], ACT.Silu, bias=w("b_inz")).then_inc(sem["sz_ready"], 1)
                a.wait_ge(sem["conv"], nth("conv", b))
                act(u[:, :], cv[:, 1, :], ACT.Silu, bias=w("conv_b")).then_inc(sem["u_ready"], 1)
                a.wait_ge(sem["xp_done"], nth("xp_done", b))
                act(dtl[:, :], G[0:DTR, 0, :], ACT.Copy).then_inc(sem["dtl_ready"], 1)
                act(Br[:, :], G[:, 1, :], ACT.Copy).then_inc(sem["br_ready"], 1)
                a.wait_ge(sem["dtp_done"], nth("dtp_done", b))
                act(sp[:, 0, :], G[:, 0, :], ACT.Abs, bias=w("b_dt")).then_inc(sem["sp_abs"], 1)
                act(sp[:, 1, :], G[:, 0, :], ACT.Relu, bias=w("b_dt")).then_inc(sem["sp_relu"], 1)
                a.wait_ge(sem["sp_abs"], nth("sp_abs", b))
                act(sp[:, 2, :], sp[:, 0, :], ACT.Exp, scale=-1.0).then_inc(sem["sp_exp"], 1)
                a.wait_ge(sem["sp_u1"], nth("sp_u1", b))
                act(sp[:, 4, :], sp[:, 3, :], ACT.Ln).then_inc(sem["sp_ln"], 1)
                for k in range(GROUPS):
                    g_ = 4 * (k % 4) + k // 4
                    a.wait_ge(sem["spread"], nth("spread", b, k + 1))
                    if k >= 2:
                        a.wait_ge(sem["scanned"], nth("scanned", b, k - 1))
                    act(dA[:, k % 2, :], G[:, 0, :], ACT.Exp, scale=a_neg[:, g_:g_ + 1]).then_inc(sem["da_ready"], 1)
                ln(4, b)
                a.wait_ge(sem["fc1_done"], nth("fc1_done", b))
                for ch in range(2):
                    act(hidb[:, ch, :, :], G[:, 0:2, HALF * ch:HALF * ch + HALF], ACT.Gelu, bias=w("b_fc1", cols=(ch, ch + 1))).then_inc(sem["fc1_act"], 1)
                a.wait_ge(sem["fc2_done"], nth("fc2_done", b))
                act(ff[:, :], G[:, 2, 0:HALF], ACT.Gelu, bias=w("b_fc2")).then_inc(sem["ff_ready"], 1)
                ln(5, b)
                ln(6, b)
                ln(7, b)
                for i in range(2):
                    a.wait_ge(sem["mbc1_done"], nth("mbc1_done", b, i + 1))
                    act(mbc[:, 1, 4 * i:4 * i + 4, :], G[:, 0:2, :].rearrange("p k (i c) -> p (k i) c", i=2), ACT.Copy).then_inc(sem["mbc1_in"], 1)
                for e in range(E):
                    i, n = e // 2, e % 2
                    a.wait_ge(sem["hid1_done"], nth("hid1_done", b, i + 1))
                    if i >= 2 and n == 0:
                        a.wait_ge(sem["w2_1_done"], nth("w2_1_done", b, i - 1))
                    act(hidb[:, 2 * (i % 2) + n, :, :], G[:, 0:2, HALF * n:HALF * n + HALF], ACT.Gelu,
                        bias=w("b1_1", cols=(e, e + 1))).then_inc(sem["gelu1"], 1)

            row(0)
            with a.Fori(1, NB) as b:
                row(b)

        @block.vector
        def _(v):
            tt, ts, stt = nc.vector.tensor_tensor, nc.vector.tensor_scalar, nc.vector.scalar_tensor_tensor
            cnt = [0]

            def link(ins):
                cnt[0] += 1
                ins.then_inc(s_v, 1)
                v.wait_ge(s_v, cnt[0])

            v.wait_ge(s_c, made["pool"])
            link(v.tensor_copy(identb[:, :], ident[:, :]))
            v.wait_ge(s_w, 16)
            link(v.tensor_copy(wo3[:, 0, :], w("w_o")))
            link(tt(wo_r[:, 0, :], w("w_o"), wo3[:, 0, :], ALU.subtract))
            link(v.tensor_copy(wo3[:, 1, :], wo_r[:, 0, :]))
            link(tt(wo_r[:, 1, :], wo_r[:, 0, :], wo3[:, 1, :], ALU.subtract))
            link(v.tensor_copy(wo3[:, 2, :], wo_r[:, 1, :]))
            for s in range(4):
                link(v.tensor_reduce(sel_y[:, s, 8 * s:8 * s + 8], ident[:, :].rearrange("p (j n) -> p j n", n=NS), AX.X, ALU.add))
            v.wait_ge(s_ae, 1)
            link(ts(a_neg[:, :], a_exp[:, :], -1.0, None, ALU.mult))
            made["dve"] = cnt[0]

            def ln(j, b, out_=None):
                bank = ln_bank(j)
                n = j % 2
                v.wait_ge(sem["ln_var"], nth("ln_var", b, j + 1))
                ts(ln_ve[:, n, :], bank[:, HALF:HALF + NT], LN_EPS, None, ALU.add).then_inc(sem["ln_vareps"], 1)
                v.wait_ge(sem["ln_bc"], nth("ln_bc", b, j + 1))
                v.wait_ge(sem["ln_kept"], nth("ln_kept", b, j + 1))
                tt(ln_o[:, j, :], bank[:, HALF:S], ln_xc[:, n, :], ALU.mult).then_inc(sem["ln_out"], 1)

            def router(n, b, bank, bias):
                v.wait_ge(sem[f"lg{n}_done"], nth(f"lg{n}_done", b))
                lgn = lg[:, n, :, :]
                src = bank.rearrange("p x (c e) -> p x c e", e=E)
                dst = lgn.rearrange("p (x c) e -> p x c e", x=2)
                if bias is None:
                    v.tensor_copy(dst, src).then_inc(sem[f"lg{n}_in"], 1)
                else:
                    tt(dst, src, bias.rearrange("p (x c e) -> p x c e", x=2, e=E), ALU.add).then_inc(sem[f"lg{n}_in"], 1)
                v.wait_ge(sem[f"lg{n}_in"], nth(f"lg{n}_in", b))
                v.memset(gate[:, 0:1], 0.0)
                for t in range(NT):
                    v.max(top[:, n, t, :], lgn[:, t, :]).then_inc(sem[f"top{n}"], 1)
                v.wait_ge(sem[f"top{n}"], nth(f"top{n}", b))
                v.memset(gate[:, 1:2], 0.0)
                for t in range(NT):
                    v.max_index(idx[:, n, t, :], top[:, n, t, :], lgn[:, t, :]).then_inc(sem[f"idx{n}"], 1)
                r = f"r{n}"
                tt(dlt[:, n, :], top[:, n, :, 1], top[:, n, :, 0], ALU.subtract).then_inc(sem[r], 1)
                v.wait_ge(sem[f"idx{n}"], nth(f"idx{n}", b))
                v.tensor_copy(idxf[:, n, :, :], idx[:, n, :, 0:2]).then_inc(sem[r], 1)
                v.wait_ge(sem[r], nth(r, b, 2))
                iota = w("iota").rearrange("p (t e) -> p t e", e=E)
                for i in range(2):
                    tt(eq[:, n, i, :, :], iota, idxf[:, n, :, i:i + 1].to_broadcast([128, NT, E]), ALU.is_equal).then_inc(sem[r], 1)
                v.wait_ge(sem[f"e{n}"], nth(f"e{n}", b))
                ts(ssum[:, n, :], ex2[:, n, :], 1.0, None, ALU.add).then_inc(sem[r], 1)
                v.wait_ge(sem[r], nth(r, b, 5))
                v.reciprocal(w12[:, n, 0, :], ssum[:, n, :]).then_inc(sem[r], 1)
                v.wait_ge(sem[r], nth(r, b, 6))
                tt(w12[:, n, 1, :], w12[:, n, 0, :], ex2[:, n, :], ALU.mult).then_inc(sem[r], 1)
                tt(mk[:, n, 0, :, :], eq[:, n, 0, :, :], w12[:, n, 0, :].unsqueeze(2).to_broadcast([128, NT, E]), ALU.mult).then_inc(sem[r], 1)
                v.wait_ge(sem[r], nth(r, b, 7))
                tt(mk[:, n, 1, :, :], eq[:, n, 1, :, :], w12[:, n, 1, :].unsqueeze(2).to_broadcast([128, NT, E]), ALU.mult).then_inc(sem[r], 1)
                v.wait_ge(sem[r], nth(r, b, 9))
                tt(mk[:, n, 2, :, :], mk[:, n, 0, :, :], mk[:, n, 1, :, :], ALU.add).then_inc(sem[f"mask{n}"], 1)

            def row(b):
                src = ids_all[:, bass.ds(b * NT, NT)] if not isinstance(b, int) else ids_all[:, b * NT:b * NT + NT]
                if not_first(b):
                    v.wait_ge(sem["rows_in"], nth("rows_in", b, 0))
                ts(ids_c[:, :], src, 0, N_ITEMS - 1, ALU.max, ALU.min).then_inc(sem["ids_clipped"], 1)
                ts(valid[:, :], src, 0, None, ALU.not_equal).then_inc(sem["valid_ready"], 1)
                v.wait_ge(sem["tok_transposed"], nth("tok_transposed", b))
                v.tensor_copy(vis[:, :], F[0:VIS, 1, :]).then_inc(sem["vis_ready"], 1)
                v.tensor_copy(embp[:, :], F[:, 2, 0:HALF]).then_inc(sem["embp_ready"], 1)
                ln(0, b)
                v.wait_ge(sem["ln_out"], nth("ln_out", b, 1))
                ts(tok_a[:, :], ln_o[:, 0, :], w("g_t"), w("be_t"), ALU.mult, ALU.add).then_inc(sem["tok_affine"], 1)
                v.wait_ge(sem["valid_bc"], nth("valid_bc", b))
                v.wait_ge(sem["tok_affine"], nth("tok_affine", b))
                tt(tok_m[:, :], F[:, 2, 0:HALF], tok_a[:, :], ALU.mult).then_inc(sem["tok_masked"], 1)
                v.wait_ge(sem["tok_masked"], nth("tok_masked", b))
                stt(out=h0[:, :], in0=tok_m[:, :], scalar=0.1, in1=embp[:, :], op0=ALU.mult, op1=ALU.add).then_inc(sem["h0_ready"], 1)
                ln(1, b)
                v.wait_ge(sem["v_done"], nth("v_done", b))
                tt(vsb[:, :, :].rearrange("p (x c) n -> p x (c n)", x=2), F[:, 2:4, 0:HALF], w("bv").rearrange("p (x c) -> p x c", x=2), ALU.add).then_inc(sem["v_ready"], 1)
                v.wait_ge(sem["qk_hi"], nth("qk_hi", b))
                tt(qkr[:, :], qkf[:, :], part[:, 0, :], ALU.subtract).then_inc(sem["qk_r"], 1)
                v.wait_ge(sem["qk_mid"], nth("qk_mid", b))
                tt(part[:, 2, :], qkr[:, :], part[:, 1, :], ALU.subtract).then_inc(sem["qk_lo"], 1)
                for n in range(8):
                    v.wait_ge(sem["s1_done"], nth("s1_done", b, n + 1))
                    p = 2 * (n % 2)
                    v.tensor_reduce(nmax[:, 2 * n:2 * n + 2], F[:, p:p + 2, :], AX.X, ALU.max, negate=True).then_inc(sem["max_done"], 1)
                v.wait_ge(sem["max_done"], nth("max_done", b))
                v.tensor_copy(M[:, :, 0], nmax[:, :]).then_inc(sem["max_split"], 1)
                v.wait_ge(sem["max_split"], nth("max_split", b, 1))
                tt(nmax_r[:, 0, :], nmax[:, :], M[:, :, 0], ALU.subtract).then_inc(sem["max_split"], 1)
                v.wait_ge(sem["max_split"], nth("max_split", b, 2))
                v.tensor_copy(M[:, :, 1], nmax_r[:, 0, :]).then_inc(sem["max_split"], 1)
                v.wait_ge(sem["max_split"], nth("max_split", b, 3))
                tt(nmax_r[:, 1, :], nmax_r[:, 0, :], M[:, :, 1], ALU.subtract).then_inc(sem["max_split"], 1)
                v.wait_ge(sem["max_split"], nth("max_split", b, 4))
                v.tensor_copy(M[:, :, 2], nmax_r[:, 1, :]).then_inc(sem["max_split"], 1)
                v.wait_ge(sem["max_turned"], nth("max_turned", b))
                v.tensor_copy(QS[96:128, :, :], turned[96:128, :, :]).then_inc(sem["max_in"], 1)
                v.wait_ge(sem["pv_done"], nth("pv_done", b))
                v.tensor_copy(osb[:, :], F[:, 4, :]).then_inc(sem["o_ready"], 1)
                v.wait_ge(sem["den_done"], nth("den_done", b))
                v.reciprocal(rec[:, :], F[:, 0, :]).then_inc(sem["rec_ready"], 1)
                v.wait_ge(sem["rec_ready"], nth("rec_ready", b))
                tt(obf[:, :], osb[:, :], rec[:, :], ALU.mult).then_inc(sem["o_bf"], 1)
                v.wait_ge(sem["wo_done"], nth("wo_done", b))
                stt(out=h1[:, :], in0=F[:, 1, 0:HALF], scalar=w("b_o"), in1=h0[:, :], op0=ALU.add, op1=ALU.add).then_inc(sem["h1_ready"], 1)
                ln(2, b)
                router(0, b, F[:, 0:2, 0:2 * E], None)
                for e in range(9):
                    v.wait_ge(sem["w2_0_done"], nth("w2_0_done", b, e + 1))
                    src = F[:, 4, 0:HALF]
                    bias = w("b2_0", cols=(e, e + 1))
                    if e == 0:
                        v.wait_ge(sem["h1_ready"], nth("h1_ready", b))
                        stt(out=acc[:, 0, :], in0=src, scalar=bias, in1=h1[:, :], op0=ALU.add, op1=ALU.add).then_inc(sem["y0"], 1)
                    else:
                        if e == 1:
                            v.wait_ge(sem["mbc0_in"], nth("mbc0_in", b))
                        if e >= 3:
                            v.wait_ge(sem["acc0"], nth("acc0", b, e - 2))
                        stt(out=ye[:, (e - 1) % 2, :], in0=src, scalar=bias, in1=mbc[:, 0, e - 1, :], op0=ALU.add, op1=ALU.mult).then_inc(sem["y0"], 1)
                ln(3, b)
                v.wait_ge(sem["xi_ready"], nth("xi_ready", b))
                cw = [w("conv_w", cols=(i, i + 1)) for i in range(DC)]
                ts(cv[:, 0, :], xip[:, 0:S], cw[0], None, ALU.mult).then_inc(sem["conv"], 1)
                for i in range(1, DC):
                    v.wait_ge(sem["conv"], nth("conv", b, i))
                    stt(out=cv[:, i % 2, :], in0=xip[:, i:i + S], scalar=cw[i], in1=cv[:, (i - 1) % 2, :], op0=ALU.mult, op1=ALU.add).then_inc(sem["conv"], 1)
                v.wait_ge(sem["xp_done"], nth("xp_done", b))
                v.tensor_copy(Cr[:, :], G[:, 2, :]).then_inc(sem["cr_ready"], 1)
                v.wait_ge(sem["sp_exp"], nth("sp_exp", b))
                ts(sp[:, 3, :], sp[:, 2, :], 1.0, None, ALU.add).then_inc(sem["sp_u1"], 1)
                v.wait_ge(sem["sp_u1"], nth("sp_u1", b))
                stt(out=sp[:, 5, :], in0=sp[:, 3, :], scalar=1.0, in1=sp[:, 2, :], op0=ALU.subtract, op1=ALU.subtract).then_inc(sem["sp_r"], 1)
                v.wait_ge(sem["sp_r"], nth("sp_r", b))
                v.wait_ge(sem["sp_relu"], nth("sp_relu", b))
                tt(sp[:, 0, :], sp[:, 1, :], sp[:, 5, :], ALU.subtract).then_inc(sem["sp_t"], 1)
                v.wait_ge(sem["sp_ln"], nth("sp_ln", b))
                v.wait_ge(sem["sp_t"], nth("sp_t", b))
                tt(dt[:, :], sp[:, 4, :], sp[:, 0, :], ALU.add).then_inc(sem["dt_ready"], 1)
                v.wait_ge(sem["u_ready"], nth("u_ready", b))
                v.wait_ge(sem["dt_ready"], nth("dt_ready", b))
                tt(dx[:, :], dt[:, :], u[:, :], ALU.mult).then_inc(sem["dx_ready"], 1)
                for k in range(GROUPS):
                    v.wait_ge(sem["spread"], nth("spread", b, k + 1))
                    if k == 0:
                        v.wait_ge(sem["br_ready"], nth("br_ready", b))
                    if k >= 2:
                        v.wait_ge(sem["scanned"], nth("scanned", b, k - 1))
                    tt(dBu[:, k % 2, :], G[:, 1, :], Br[:, :], ALU.mult).then_inc(sem["dbu_ready"], 1)
                    v.wait_ge(sem["dbu_ready"], nth("dbu_ready", b, k + 1))
                    v.wait_ge(sem["da_ready"], nth("da_ready", b, k + 1))
                    if k >= 2:
                        v.wait_ge(sem["hc_ready"], nth("hc_ready", b, k - 1))
                    v.tensor_tensor_scan(hst[:, k % 2, :], dA[:, k % 2, :], dBu[:, k % 2, :], 0.0, ALU.mult, ALU.add).then_inc(sem["scanned"], 1)
                v.wait_ge(sem["y_sum"], nth("y_sum", b))
                stt(out=y1, in0=u[:, :], scalar=w("d_ssm"), in1=G[:, 2, :], op0=ALU.mult, op1=ALU.add).then_inc(sem["y1"], 1)
                v.wait_ge(sem["y1"], nth("y1", b))
                v.wait_ge(sem["sz_ready"], nth("sz_ready", b))
                tt(y2, y1, sz[:, :], ALU.mult).then_inc(sem["y2"], 1)
                v.wait_ge(sem["out_done"], nth("out_done", b))
                stt(out=sres[:, :], in0=G[:, 0, 0:HALF], scalar=w("b_out"), in1=ln_o[:, 3, :], op0=ALU.add, op1=ALU.add).then_inc(sem["s_ready"], 1)
                ln(4, b)
                v.wait_ge(sem["ln_out"], nth("ln_out", b, 5))
                ts(yl[:, :], ln_o[:, 4, :], w("g1"), w("be1"), ALU.mult, ALU.add).then_inc(sem["yln"], 1)
                v.wait_ge(sem["yln"], nth("yln", b))
                v.wait_ge(sem["ff_ready"], nth("ff_ready", b))
                tt(s2[:, :], yl[:, :], ff[:, :], ALU.add).then_inc(sem["s2_ready"], 1)
                ln(5, b)
                v.wait_ge(sem["ln_out"], nth("ln_out", b, 6))
                ts(yy[:, :], ln_o[:, 5, :], w("g2"), w("be2"), ALU.mult, ALU.add).then_inc(sem["yy"], 1)
                v.wait_ge(sem["yy"], nth("yy", b))
                v.wait_ge(sem["acc0"], nth("acc0", b))
                tt(h3[:, :], yy[:, :], h2[:, :], ALU.add).then_inc(sem["h3_ready"], 1)
                ln(6, b)
                ln(7, b)
                v.wait_ge(sem["ln_out"], nth("ln_out", b, 8))
                ts(x6[:, :], ln_o[:, 7, :], w("g_m"), w("be_m"), ALU.mult, ALU.add).then_inc(sem["x6_ready"], 1)
                router(1, b, G[:, 0:2, 0:2 * E], w("br1"))
                for e in range(E):
                    v.wait_ge(sem["w2_1_done"], nth("w2_1_done", b, e // 2 + 1))
                    if e == 0:
                        v.wait_ge(sem["mbc1_in"], nth("mbc1_in", b))
                    if e >= 2:
                        v.wait_ge(sem["acc1"], nth("acc1", b, e - 1))
                    stt(out=yeb[:, e % 2, :], in0=G[:, 2, HALF * (e % 2):HALF * (e % 2) + HALF], scalar=w("b2_1", cols=(e, e + 1)),
                        in1=mbc[:, 1, e, :], op0=ALU.add, op1=ALU.mult).then_inc(sem["y1e"], 1)
                v.wait_ge(sem["out_turned"], nth("out_turned", b))
                if not_first(b):
                    v.wait_ge(sem["stored"], nth("stored", b, 0))
                v.tensor_copy(outs[:, :, :], G[:, 0, 0:256].rearrange("p (c n) -> p c n", c=2)).then_inc(sem["out_ready"], 1)

            v.wait_ge(s_ids, 16)
            row(0)
            with v.Fori(1, NB) as b:
                row(b)

        @block.tensor
        def _(pe):
            mm = nc.tensor.matmul
            pe.wait_ge(s_w, 16)
            pe.wait_ge(s_c, made["pool"])
            pe.wait_ge(s_v, made["dve"])

            def ln(j, b, x):
                bank = ln_bank(j)
                n = j % 2
                mm(bank[:, 0:HALF], centre[:, :], x, start=True, stop=True).then_inc(sem["ln_centred"], 1)
                pe.wait_ge(sem["ln_squared"], nth("ln_squared", b, j + 1))
                for c in range(2):
                    last = mm(bank[:, HALF + 2 * c:HALF + 2 * c + 2], ln_sq[:, n, 128 * c:128 * c + 128], halfmean[:, :], start=True, stop=True)
                last.then_inc(sem["ln_var"], 1)
                pe.wait_ge(sem["ln_rstd"], nth("ln_rstd", b, j + 1))
                for c in range(2):
                    for x_ in range(2):
                        last = mm(bank[half(x_), HALF + 128 * c:HALF + 128 * c + 128],
                                  ln_rs[:, n, 2 * c + x_:2 * c + x_ + 1].to_broadcast([128, 64]), ident[:, :], start=True, stop=True)
                last.then_inc(sem["ln_bc"], 1)

            def logits(n, b, x, wr, banks):
                for x_ in range(2):
                    for c in range(2):
                        last = mm(banks[:, x_, E * c:E * c + E], x[half(x_), 128 * c:128 * c + 128], wr[half(x_), :], start=True, stop=True)
                last.then_inc(sem[f"lg{n}_done"], 1)

            def mask_bc(n, e, out_):
                for c in range(2):
                    for x_ in range(2):
                        last = mm(out_[half(x_), 128 * c:128 * c + 128], mk[:, n, 2, 2 * x_ + c, e:e + 1].to_broadcast([128, 64]),
                                  ident[:, :], start=True, stop=True)
                return last

            def row(b):
                pe.wait_ge(sem["rows_in"], nth("rows_in", b))
                for x_ in range(2):
                    for c in range(2):
                        t = 2 * x_ + c
                        at = 128 * t
                        nc.tensor.transpose(F[:, 0, at:at + 128], rows[:, t, 0:128], ident[:, :])
                        nc.tensor.transpose(F[0:VIS, 1, at:at + 128], rows[:, t, 128:ROW], ident[:, :])
                for c in range(2):
                    for x_ in range(2):
                        last = mm(F[half(x_), 2, 128 * c:128 * c + 128], rows[:, 2 * x_ + c, 0:64], ident[:, :], start=True, stop=True)
                last.then_inc(sem["tok_transposed"], 1)
                pe.wait_ge(sem["eg_ready"], nth("eg_ready", b))
                mm(F[:, 3, :], w("w_eg"), eg[:, :], start=True, stop=True)
                pe.wait_ge(sem["vis_ready"], nth("vis_ready", b))
                mm(F[0:64, 4, :], w("w_vis", slice(0, VIS)), vis[:, :], start=True, stop=True).then_inc(sem["feat_done"], 1)
                pe.wait_ge(sem["embp_ready"], nth("embp_ready", b))
                pe.wait_ge(sem["valid_ready"], nth("valid_ready", b))
                for c in range(2):
                    for x_ in range(2):
                        t = 2 * x_ + c
                        last = mm(F[half(x_), 2, 128 * c:128 * c + 128], valid[:, t:t + 1].to_broadcast([128, 64]), ident[:, :], start=True, stop=True)
                last.then_inc(sem["valid_bc"], 1)
                pe.wait_ge(sem["cat_ready"], nth("cat_ready", b))
                for x_ in range(2):
                    mm(F[half(x_), 1, 0:HALF], w("w_f1"), cat1[:, HALF * x_:HALF * x_ + HALF], start=True, stop=False)
                for x_ in range(2):
                    last = mm(F[half(x_), 1, 0:HALF], w("w_f2", slice(0, 64)), cat2[:, HALF * x_:HALF * x_ + HALF], start=False, stop=True)
                last.then_inc(sem["fuse_done"], 1)
                pe.wait_ge(sem["fuse_act"], nth("fuse_act", b))
                ln(0, b, f0[:, :])
                pe.wait_ge(sem["h0_ready"], nth("h0_ready", b))
                ln(1, b, h0[:, :])
                x1 = ln_o[:, 1, :]
                pe.wait_ge(sem["ln_out"], nth("ln_out", b, 2))
                for x_ in range(2):
                    last = mm(F[:, x_, 0:HALF], w("w_qk", half(x_)), x1[half(x_), :], start=True, stop=True)
                last.then_inc(sem["qk_done"], 1)
                for x_ in range(2):
                    for c in range(2):
                        last = mm(F[:, 2 + x_, 128 * c:128 * c + 128], x1[half(x_), 128 * c:128 * c + 128], w("w_v", half(x_)), start=True, stop=True)
                last.then_inc(sem["v_done"], 1)
                pe.wait_ge(sem["stack_in"], nth("stack_in", b))
                for n in range(8):
                    if n == 0:
                        pe.wait_ge(sem["qk_full"], nth("qk_full", b))
                    if n == 1:
                        pe.wait_ge(sem["v_ready"], nth("v_ready", b))
                    if n >= 2:
                        pe.wait_ge(sem["max_done"], nth("max_done", b, n - 1))
                    for i in range(2):
                        h = 2 * (n % 2) + i
                        last = mm(F[:, 2 * (n % 2) + i, :], QS[0:96, h, 128 * (n // 2):128 * (n // 2) + 128], KS[0:96, h, :], start=True, stop=True)
                    last.then_inc(sem["s1_done"], 1)
                pe.wait_ge(sem["max_split"], nth("max_split", b))
                for t in range(NT):
                    for h in range(NH):
                        last = nc.tensor.transpose(turned[96:128, h, 128 * t:128 * t + 128], M[:, NH * t + h, :], identb[:, :])
                last.then_inc(sem["max_turned"], 1)
                def pv(kt):
                    pe.wait_ge(sem["exp_done"], nth("exp_done", b, 2 * kt + 2))
                    for h in range(NH):
                        n = 2 * kt + h // 2
                        last = mm(F[32 * h:32 * h + 32, 4, :], vsb[:, kt, 32 * h:32 * h + 32], P[:, n % 4, h % 2, :], start=(kt == 0), stop=(kt == NT - 1))
                    last.then_inc(sem["pv_done"], 1)
                for n in range(8):
                    if n == 0:
                        pe.wait_ge(sem["max_in"], nth("max_in", b))
                    if n >= 2:
                        pe.wait_ge(sem["exp_done"], nth("exp_done", b, n - 1))
                    for i in range(2):
                        h = 2 * (n % 2) + i
                        kt = n // 2
                        last = mm(F[:, 2 * (n % 2) + i, :], KS[:, h, 128 * kt:128 * kt + 128], QS[:, h, :], start=True, stop=True)
                    last.then_inc(sem["s2_done"], 1)
                    if n >= 3 and n % 2 == 1:
                        pv((n - 3) // 2)
                pv(NT - 1)
                pe.wait_ge(sem["o_ready"], nth("o_ready", b))
                mm(F[:, 0, :], sel_den[:, :], osb[:, :], start=True, stop=True).then_inc(sem["den_done"], 1)
                pe.wait_ge(sem["o_bf"], nth("o_bf", b))
                for p in range(3):
                    for x_ in range(2):
                        last = mm(F[half(x_), 1, 0:HALF], wo3[:, p, :], obf[:, HALF * x_:HALF * x_ + HALF], start=(p == 0), stop=(p == 2))
                last.then_inc(sem["wo_done"], 1)
                pe.wait_ge(sem["h1_ready"], nth("h1_ready", b))
                ln(2, b, h1[:, :])
                x2 = ln_o[:, 2, :]
                pe.wait_ge(sem["ln_out"], nth("ln_out", b, 3))
                logits(0, b, x2, w("wr0"), F[:, 0:2, :])
                pe.wait_ge(sem["mask0"], nth("mask0", b))
                for e in range(E):
                    last = mask_bc(0, e, F[:, e // 2, HALF * (e % 2):HALF * (e % 2) + HALF])
                last.then_inc(sem["mbc0_done"], 1)

                def down0(e):
                    pe.wait_ge(sem["gelu0"], nth("gelu0", b, 2 * e + 2))
                    if e >= 1:
                        pe.wait_ge(sem["y0"], nth("y0", b, e))
                    for ch in range(2):
                        for x_ in range(2):
                            last = mm(F[half(x_), 4, 0:HALF], w("w2_0", cols=(64 * (2 * e + ch), 64 * (2 * e + ch) + 64)),
                                      hid[:, 2 * (e % 2) + ch, x_, :], start=(ch == 0), stop=(ch == 1), skip_group_check=True)
                    last.then_inc(sem["w2_0_done"], 1)
                for e in range(9):
                    if e == 0:
                        pe.wait_ge(sem["mbc0_in"], nth("mbc0_in", b))
                    if e >= 2:
                        pe.wait_ge(sem["gelu0"], nth("gelu0", b, 2 * (e - 1)))
                    for ch in range(2):
                        for x_ in range(2):
                            last = mm(F[:, 2 * (e % 2) + x_, HALF * ch:HALF * ch + HALF], w("w1_0", half(x_), (128 * (2 * e + ch), 128 * (2 * e + ch) + 128)),
                                      x2[half(x_), :], start=True, stop=True)
                    last.then_inc(sem["hid0_done"], 1)
                    if e:
                        down0(e - 1)
                down0(8)
                pe.wait_ge(sem["acc0"], nth("acc0", b))
                ln(3, b, h2[:, :])
                x3 = ln_o[:, 3, :]
                pe.wait_ge(sem["ln_out"], nth("ln_out", b, 4))
                for x_ in range(2):
                    mm(G[:, x_, 0:HALF], w("w_inx", half(x_)), x3[half(x_), :], start=True, stop=True)
                    last = mm(G[:, x_, HALF:S], w("w_inz", half(x_)), x3[half(x_), :], start=True, stop=True)
                last.then_inc(sem["in_done"], 1)
                pe.wait_ge(sem["sz_ready"], nth("sz_ready", b))
                pe.wait_ge(sem["u_ready"], nth("u_ready", b))
                mm(G[0:DTR, 0, :], w("w_xdt"), u[:, :], start=True, stop=True)
                mm(G[:, 1, :], w("w_xb"), u[:, :], start=True, stop=True)
                mm(G[:, 2, :], w("w_xc"), u[:, :], start=True, stop=True).then_inc(sem["xp_done"], 1)
                pe.wait_ge(sem["dtl_ready"], nth("dtl_ready", b))
                mm(G[:, 0, :], w("w_dt", slice(0, DTR)), dtl[:, :], start=True, stop=True).then_inc(sem["dtp_done"], 1)

                def ysum(s):
                    pe.wait_ge(sem["hc_ready"], nth("hc_ready", b, 4 * s + 4))
                    for r in range(4):
                        last = mm(G[32 * r:32 * r + 32, 2, :], sel_y[:, s, :], hc[:, r, :], start=(s == 0), stop=(s == 3))
                    last.then_inc(sem["y_sum"], 1)
                for k in range(GROUPS):
                    r, s = k % 4, k // 4
                    q = slice(32 * r, 32 * r + 32)
                    if k == 0:
                        pe.wait_ge(sem["br_ready"], nth("br_ready", b))
                        pe.wait_ge(sem["cr_ready"], nth("cr_ready", b))
                        pe.wait_ge(sem["sp_relu"], nth("sp_relu", b))
                        pe.wait_ge(sem["dx_ready"], nth("dx_ready", b))
                    else:
                        pe.wait_ge(sem["da_ready"], nth("da_ready", b, k))
                        pe.wait_ge(sem["dbu_ready"], nth("dbu_ready", b, k))
                    mm(G[:, 0, :], sel_dn[q, s, :], dt[q, :], start=True, stop=True)
                    mm(G[:, 1, :], sel_dn[q, s, :], dx[q, :], start=True, stop=True).then_inc(sem["spread"], 1)
                    if k >= 5 and k % 4 == 1:
                        ysum((k - 5) // 4)
                ysum(3)
                pe.wait_ge(sem["y2"], nth("y2", b))
                for x_ in range(2):
                    last = mm(G[half(x_), 0, 0:HALF], w("w_out"), sp[:, 3, HALF * x_:HALF * x_ + HALF], start=True, stop=True)
                last.then_inc(sem["out_done"], 1)
                pe.wait_ge(sem["s_ready"], nth("s_ready", b))
                ln(4, b, sres[:, :])
                pe.wait_ge(sem["yln"], nth("yln", b))
                for ch in range(2):
                    for x_ in range(2):
                        last = mm(G[:, x_, HALF * ch:HALF * ch + HALF], w("fc1", half(x_), (128 * ch, 128 * ch + 128)), yl[half(x_), :], start=True, stop=True)
                last.then_inc(sem["fc1_done"], 1)
                pe.wait_ge(sem["fc1_act"], nth("fc1_act", b))
                for ch in range(2):
                    for x_ in range(2):
                        last = mm(G[half(x_), 2, 0:HALF], w("fc2", cols=(64 * ch, 64 * ch + 64)), hidb[:, ch, x_, :], start=(ch == 0), stop=(ch == 1))
                last.then_inc(sem["fc2_done"], 1)
                pe.wait_ge(sem["s2_ready"], nth("s2_ready", b))
                ln(5, b, s2[:, :])
                pe.wait_ge(sem["h3_ready"], nth("h3_ready", b))
                ln(6, b, h3[:, :])
                pe.wait_ge(sem["ln_out"], nth("ln_out", b, 7))
                ln(7, b, ln_o[:, 6, :])
                pe.wait_ge(sem["x6_ready"], nth("x6_ready", b))
                logits(1, b, x6[:, :], w("wr1"), G[:, 0:2, :])
                pe.wait_ge(sem["mask1"], nth("mask1", b))
                for i in range(2):
                    if i:
                        pe.wait_ge(sem["mbc1_in"], nth("mbc1_in", b, 1))
                    for e in range(4):
                        last = mask_bc(1, 4 * i + e, G[:, e // 2, HALF * (e % 2):HALF * (e % 2) + HALF])
                    last.then_inc(sem["mbc1_done"], 1)

                def down1(i):
                    pe.wait_ge(sem["gelu1"], nth("gelu1", b, 2 * i + 2))
                    if i >= 1:
                        pe.wait_ge(sem["y1e"], nth("y1e", b, 2 * i))
                    for n in range(2):
                        e = 2 * i + n
                        for x_ in range(2):
                            last = mm(G[half(x_), 2, HALF * n:HALF * n + HALF], w("w2_1", cols=(64 * e, 64 * e + 64)),
                                      hidb[:, 2 * (i % 2) + n, x_, :], start=True, stop=True)
                    last.then_inc(sem["w2_1_done"], 1)
                for i in range(E // 2):
                    if i == 0:
                        pe.wait_ge(sem["mbc1_in"], nth("mbc1_in", b))
                    else:
                        pe.wait_ge(sem["gelu1"], nth("gelu1", b, 2 * i))
                    for n in range(2):
                        e = 2 * i + n
                        for x_ in range(2):
                            last = mm(G[:, x_, HALF * n:HALF * n + HALF], w("w1_1", half(x_), (128 * e, 128 * e + 128)), x6[half(x_), :], start=True, stop=True)
                    last.then_inc(sem["hid1_done"], 1)
                    if i:
                        down1(i - 1)
                down1(E // 2 - 1)
                pe.wait_ge(sem["acc1"], nth("acc1", b))
                for c in range(2):
                    last = nc.tensor.transpose(G[:, 0, 128 * c:128 * c + 128], h4[:, 128 * c:128 * c + 128], ident[:, :])
                last.then_inc(sem["out_turned"], 1)

            row(0)
            with pe.Fori(1, NB) as b:
                row(b)


def kernel(**inputs):
    import concourse.bacc as bacc
    from concourse.bass_utils import run_bass_kernel_spmd

    p = {k: np.asarray(v) for k, v in inputs.items()}
    wts = np.zeros((128, WCOLS), np.float32)

    def put(name, a, row=0, col=0):
        a = a if a.ndim == 2 else a[:, None]
        at = AT[name][0] + col
        wts[row:row + a.shape[0], at:at + a.shape[1]] = a

    def twice(name, a, col=0):
        put(name, a, 0, col)
        put(name, a, 64, col)

    put("w_eg", p["L0_tok_w_item"]); put("w_eg", p["L0_tok_w_geo"], 64, 64)
    put("b_eg", p["L0_tok_b_item"]); put("b_eg", p["L0_tok_b_geo"], 64)
    put("w_vis", p["L0_tok_w_visit"]); put("b_vis", p["L0_tok_b_visit"])
    put("w_f1", p["L0_tok_w_fuse"][:128]); put("w_f2", p["L0_tok_w_fuse"][128:])
    twice("b_f", p["L0_tok_b_fuse"]); twice("g_t", p["L0_tok_ln_gamma"]); twice("be_t", p["L0_tok_ln_beta"])
    twice("w_qk", p["L0_attn_Wq"].T); twice("w_qk", p["L0_attn_Wk"].T, 64)
    put("b_qk", p["L0_attn_bq"]); put("b_qk", p["L0_attn_bk"], 64)
    for h in range(NH):
        hs = slice(DH * h, DH * h + DH)
        twice("w_v", p["L0_attn_Wv"][hs].T, 32 * h)
        put("w_o", p["L0_attn_Wo"][:, hs].T, 32 * h)
        for t in range(NT):
            put("bv", np.tile(p["L0_attn_bv"][hs], (128, 1)), 0, 128 * t + 32 * h)
            put("bv", np.ones((128, 1), np.float32), 0, 128 * t + 32 * h + DH)
    twice("b_o", p["L0_attn_bo"])
    twice("wr0", p["L0_ffn_Wr"]); twice("wr1", p["L1_ffn_Wr"])
    for e in range(9):
        w1 = p["L0_ffn_W1s"] if e == 0 else p["L0_ffn_W1p"][e - 1]
        b1 = p["L0_ffn_b1s"] if e == 0 else p["L0_ffn_b1p"][e - 1]
        w2 = p["L0_ffn_W2s"] if e == 0 else p["L0_ffn_W2p"][e - 1]
        b2 = p["L0_ffn_b2s"] if e == 0 else p["L0_ffn_b2p"][e - 1]
        twice("w1_0", w1, F0 * e)
        for ch in range(2):
            put("w2_0", w2[128 * ch:128 * ch + 128], 0, 64 * (2 * e + ch))
            put("b1_0", b1[128 * ch:128 * ch + 128], 0, 2 * e + ch)
        twice("b2_0", b2, e)
    twice("w_inx", p["L1_attn_in_proj_w"][:DI].T); twice("w_inz", p["L1_attn_in_proj_w"][DI:].T)
    put("b_inx", p["L1_attn_in_proj_b"][:DI]); put("b_inz", p["L1_attn_in_proj_b"][DI:])
    put("conv_w", p["L1_attn_conv_w"]); put("conv_b", p["L1_attn_conv_b"])
    xp = p["L1_attn_x_proj_w"]
    put("w_xdt", xp[:DTR].T)
    put("w_xb", np.tile(xp[DTR:DTR + NS].T, (1, 8))); put("w_xc", np.tile(xp[DTR + NS:].T, (1, 8)))
    put("w_dt", p["L1_attn_dt_proj_w"].T); put("b_dt", p["L1_attn_dt_proj_b"])
    put("a_log", p["L1_attn_A_log"].reshape(GROUPS, 8, NS).transpose(1, 2, 0).reshape(128, GROUPS))
    put("d_ssm", p["L1_attn_D_ssm"]); put("w_out", p["L1_attn_out_proj_w"].T); twice("b_out", p["L1_attn_out_proj_b"])
    twice("g1", p["L1_attn_ln1_g"]); twice("be1", p["L1_attn_ln1_b"])
    twice("g2", p["L1_attn_ln2_g"]); twice("be2", p["L1_attn_ln2_b"])
    twice("fc1", p["L1_attn_fc1_w"].T)
    for ch in range(2):
        put("fc2", p["L1_attn_fc2_w"].T[128 * ch:128 * ch + 128], 0, 64 * ch)
        put("b_fc1", p["L1_attn_fc1_b"][128 * ch:128 * ch + 128], 0, ch)
    twice("b_fc2", p["L1_attn_fc2_b"])
    twice("g_m", p["L1_ffn_gamma"]); twice("be_m", p["L1_ffn_beta"])
    put("br1", np.tile(p["L1_ffn_br"], (128, NT)))
    put("iota", np.tile(np.arange(E, dtype=np.float32), (128, NT)))
    for e in range(E):
        twice("w1_1", p["L1_ffn_W1"][e], F1 * e)
        put("w2_1", p["L1_ffn_W2"][e], 0, 64 * e)
        put("b1_1", p["L1_ffn_b1"][e], 0, e)
        twice("b2_1", p["L1_ffn_b2"][e], e)
    arrays = {
        "ids": np.ascontiguousarray(p["x"].reshape(NB * NT, 128).T),
        "table": np.concatenate([p["L0_tok_emb_table"], p["L0_tok_geo_table"], p["L0_tok_visit_table"]], axis=1),
        "weights": wts,
    }
    nc = bacc.Bacc("TRN2", target_bir_lowering=False, num_devices=1)
    args = [nc.dram_tensor(f"in_{n}", a.shape, mybir.dt.from_np(a.dtype), kind="ExternalInput").ap() for n, a in arrays.items()]
    args.append(nc.dram_tensor("out_h", (NB, S, D), mybir.dt.float32, kind="ExternalOutput").ap())
    build_tower(nc, *args)
    r = run_bass_kernel_spmd(nc, [{f"in_{n}": a for n, a in arrays.items()}], core_ids=[0])
    return r.results[0]["out_h"]
```

```python
from contextlib import ExitStack

import numpy as np
import concourse.bass as bass
from concourse import mybir

NB, S, D = 8, 512, 64
HALF = S // 2
NT = S // 128
NH, DH = 4, 16
F0, E, F1 = 256, 8, 128
DI, NS, DC, DTR = 128, 16, 4, 16
VIS = 24
ROW = 2 * D + VIS
LN_EPS = 1e-5
NLN = 8
GROUPS = DI * NS // 128
N_ITEMS = 25001

WIDTHS = [
    ("w_eg", 128), ("w_vis", 64), ("w_f1", 64), ("w_f2", 64),
    ("w_qk", 128), ("w_v", 128), ("bv", 128), ("w_o", 64),
    ("wr0", E), ("w1_0", 9 * F0), ("w2_0", 18 * D),
    ("w_inx", 128), ("w_inz", 128), ("w_xdt", 16), ("w_xb", 128), ("w_xc", 128), ("w_dt", 128), ("w_out", 64),
    ("fc1", 256), ("fc2", 128), ("wr1", E), ("br1", NT * E), ("w1_1", E * F1), ("w2_1", E * D),
    ("iota", NT * E),
    ("b_eg", 1), ("b_vis", 1), ("b_f", 1), ("g_t", 1), ("be_t", 1), ("b_qk", 1), ("b_o", 1),
    ("b1_0", 18), ("b2_0", 9), ("b_inx", 1), ("b_inz", 1), ("conv_w", DC), ("conv_b", 1), ("b_dt", 1),
    ("a_log", GROUPS), ("d_ssm", 1), ("b_out", 1), ("g1", 1), ("be1", 1), ("b_fc1", 2), ("b_fc2", 1),
    ("g2", 1), ("be2", 1), ("g_m", 1), ("be_m", 1), ("b1_1", E), ("b2_1", E),
]
AT = {name: (sum(w for _, w in WIDTHS[:n]), width) for n, (name, width) in enumerate(WIDTHS)}
WCOLS = sum(w for _, w in WIDTHS)

PER = {
    "ids_clipped": 1, "valid_ready": 1, "rows_in": 16 * NT, "tok_transposed": 1, "eg_ready": 1, "vis_ready": 1,
    "embp_ready": 1, "feat_done": 1, "cat_ready": 2, "fuse_done": 1, "fuse_act": 1, "valid_bc": 1,
    "tok_affine": 1, "tok_masked": 1, "h0_ready": 1,
    "lnF_centred": 3, "lnF_squared": 3, "lnF_kept": 3, "lnF_var": 3, "lnF_vareps": 3, "lnF_rstd": 3, "lnF_bc": 3, "lnF_out": 3,
    "lnB_centred": 5, "lnB_squared": 5, "lnB_kept": 5, "lnB_var": 5, "lnB_vareps": 5, "lnB_rstd": 5, "lnB_bc": 5, "lnB_out": 5,
    "qk_done": 1, "v_done": 1, "qk_full": 1, "qk_hi": 1, "qk_r": 1, "qk_mid": 1, "qk_lo": 1, "v_ready": 1,
    "parts_out": 32, "stack_in": 96, "s1_done": 8, "max_done": 8, "max_split": 5, "max_turned": 1, "max_in": 1,
    "s2_done": 8, "exp_done": 8, "pv_done": NT, "o_ready": 1, "den_done": 1, "rec_ready": 1, "o_bf": 1,
    "wo_done": 1, "h1_ready": 1,
    "lg0_done": 1, "lg0_in": 1, "top0": NT, "idx0": NT, "r0": 9, "e0": 1, "mask0": 1, "mp0": 5, "mt0_done": 1, "mt0_in": 1, "mbc0_done": 1, "mbc0_in": 1,
    "lg1_done": 1, "lg1_in": 1, "top1": NT, "idx1": NT, "r1": 9, "e1": 1, "mask1": 1, "mp1": 5, "mt1_done": 1, "mt1_in": 1, "mbc1_done": 2, "mbc1_in": 2,
    "hid0_done": 9, "gelu0": 18, "w2_0_done": 9, "y0": 9, "acc0": 8,
    "h2_taken": 1,
    "in_done": 1, "xi_ready": 1, "sz_ready": 1, "conv": 4, "u_ready": 1, "xp_done": 1, "dtl_ready": 1, "br_ready": 1,
    "cr_ready": 1, "dtp_done": 1, "sp_abs": 1, "sp_exp": 1, "sp_relu": 1, "sp_u1": 1, "sp_ln": 1, "sp_r": 1, "sp_t": 1,
    "dt_ready": 1, "dx_ready": 1, "d_hi": 2, "d_r": 2, "d_mid": 2, "d_lo": 2, "dparts_out": 16, "dstack_in": 16,
    "spread": GROUPS, "da_ready": GROUPS, "dbu_ready": GROUPS, "scanned": GROUPS,
    "hc_ready": GROUPS, "y_sum": 4, "y1": 1, "y2": 1, "out_done": 1, "s_ready": 1, "yln": 1,
    "fc1_done": 1, "fc1_act": 2, "fc2_done": 1, "ff_ready": 1, "s2_ready": 1, "yy": 1, "h3_ready": 1, "x6_ready": 1,
    "hid1_done": E // 2, "gelu1": E, "w2_1_done": E // 2, "y1e": E, "acc1": E, "out_turned": 1, "out_ready": 1, "stored": 32,
}

FRONT = (["gather", "tok", "feat", "fuse", "ln0a", "ln0b", "ln0c", "ln1a", "ln1b", "ln1c", "qkv", "split"]
         + [f"s1_{n}" for n in range(8)] + ["msplit"] + [f"s2_{n}" for n in range(8)] + ["den", "wo"]
         + ["ln2a", "ln2b", "ln2c", "logit0", "router0", "mask0"] + [f"ffn_{e}" for e in range(10)])
BACK = (["take", "ln3a", "ln3b", "ln3c", "inproj", "conv", "xproj", "dtproj", "softplus", "dsplit"]
        + [f"grp_{k}" for k in range(GROUPS + 1)] + ["yout", "ln4a", "ln4b", "ln4c", "fc1", "fc2", "ln5a", "ln5b", "ln5c"]
        + ["ln6a", "ln6b", "ln6c", "ln7a", "ln7b", "ln7c", "logit1", "router1", "mask1"] + [f"exp_{i}" for i in range(E // 2 + 1)] + ["turn"])
MERGE = [0, 1, 2, 3, 4, 5, 7, 8, 9, 10, 11, 12, 13, 14, 15, 16, 17, 18, 20, 21, 22, 23, 24, 25, 26, 27, 28, 29, 30, 31, 33, 34,
         35, 36, 37, 38, 39, 40, 41, 42, 43, 44, 46, 47, 48, 49, 50]


def merged():
    order, at = [], 0
    for step, until in zip(FRONT, MERGE):
        order += BACK[at:until] + [step]
        at = max(at, until)
    return order + BACK[at:]


STEPS = merged()


def build_tower(nc: bass.Bass, ids: bass.AP, table: bass.AP, weights: bass.AP, out: bass.AP):
    fp32, bf16 = mybir.dt.float32, mybir.dt.bfloat16
    i32, u32 = mybir.dt.int32, mybir.dt.uint32
    ALU, ACT, AX = mybir.AluOpType, mybir.ActivationFunctionType, mybir.AxisListType

    qk_scr = nc.dram_tensor("qk_scr", (2, 3, 64, S), bf16, kind="Internal").ap()
    d_scr = nc.dram_tensor("d_scr", (2, 3, 128, S), bf16, kind="Internal").ap()

    ctx = ExitStack()
    with ctx:
        def sb(name, shape, dt=fp32):
            return ctx.enter_context(nc.sbuf_tensor(name, shape, dt))

        wts = sb("wts", [128, WCOLS])

        def w(name, rows=slice(0, 128), cols=None):
            at, width = AT[name]
            lo, hi = cols if cols else (0, width)
            return wts[rows, at + lo:at + hi]

        ident = sb("ident", [128, 128])
        identb = sb("identb", [128, 128], bf16)
        centre = sb("centre", [128, 128])
        halfmean = sb("halfmean", [128, 2])
        sel_den = sb("sel_den", [128, 128])
        sel_dn = sb("sel_dn", [96, 4, 128], bf16)
        sel_y = sb("sel_y", [128, 4, 32])
        sel_m = sb("sel_m", [96, NT * E, 64], bf16)
        wo3 = sb("wo3", [128, 3, 64], bf16)
        wo_r = sb("wo_r", [128, 2, 64])
        neg_half = sb("neg_half", [128, 4])
        e_base = sb("e_base", [128, 4])
        a_neg = sb("a_neg", [128, GROUPS])
        a_exp = sb("a_exp", [128, GROUPS])
        gate = sb("gate", [128, 4])
        gpool = sb("gpool", [128, 4])
        zero = sb("zero", [128, HALF])
        ids_all = sb("ids_all", [128, NB * NT], i32)

        ids_c = sb("ids_c", [128, NT], i32)
        valid = sb("valid", [128, NT])
        rows = sb("rows", [128, NT, ROW])
        vis = sb("vis", [VIS, S])
        embp = sb("embp", [128, HALF])
        cat1 = sb("cat1", [128, S])
        eg = cat1
        cat2 = sb("cat2", [64, S])
        f0 = sb("f0", [128, HALF])
        h0, h1, h2, h2b, h3, h4 = (sb(f"h{i}", [128, HALF]) for i in ("0", "1", "2", "2b", "3", "4"))
        ln_sq = sb("ln_sq", [128, 2, HALF])
        tok_a, tok_m = f0, ln_sq[:, 0, :]
        ln_xc = sb("ln_xc", [128, 2, HALF])
        ln_ve = sb("ln_ve", [128, 2, NT])
        ln_rs = sb("ln_rs", [128, 2, NT])
        ln_o = sb("ln_o", [128, NLN, HALF])
        qkf = sb("qkf", [128, S])
        qkr = sb("qkr", [128, S])
        part = sb("part", [128, 3, S], bf16)
        QS = sb("QS", [128, NH, S], bf16)
        KS = sb("KS", [128, NH, S], bf16)
        vsb = sb("vsb", [128, NT, 128])
        nmax = sb("nmax", [128, 4 * NH])
        nmax_r = sb("nmax_r", [128, 2, 4 * NH])
        M = sb("M", [128, 4 * NH, 32], bf16)
        P = sb("P", [128, 4, 2, S])
        osb, rec = qkr, qkf
        obf = sb("obf", [128, S], bf16)
        lg = sb("lg", [128, 2, NT, E])
        top = sb("top", [128, 2, NT, 8])
        idx = sb("idx", [128, 2, NT, 8], u32)
        idxf = sb("idxf", [128, 2, NT, 2])
        eq = sb("eq", [128, 2, 2, NT, E])
        dlt = sb("dlt", [128, 2, NT])
        ex2 = sb("ex2", [128, 2, NT])
        ssum = sb("ssum", [128, 2, NT])
        w12 = sb("w12", [128, 2, 2, NT])
        mk = sb("mk", [128, 2, 3, NT * E])
        mk_r = sb("mk_r", [128, 2, 2, NT * E])
        mk3 = sb("mk3", [128, 2, 3, NT * E], bf16)
        mt = sb("mt", [96, 2, 128], bf16)
        mbc = sb("mbc", [128, 2, E, HALF])
        hid = sb("hid", [128, 4, 2, HALF])
        ye = sb("ye", [128, 2, HALF])
        acc = sb("acc", [128, 2, HALF])
        hidb = sb("hidb", [128, 4, 2, HALF])
        yeb = sb("yeb", [128, 2, HALF])
        accb = sb("accb", [128, 2, HALF])
        xip = sb("xip", [128, DC - 1 + S])
        sz = sb("sz", [128, S])
        cv = sb("cv", [128, 2, S])
        u = sb("u", [128, S])
        dtl = sb("dtl", [DTR, S])
        Br = sb("Br", [128, S])
        Cr = sb("Cr", [128, S])
        sp = sb("sp", [128, 6, S])
        dd = sb("dd", [128, 2, S])
        dd_r = cv
        dp = sb("dp", [128, 2, 3, S], bf16)
        T = sb("T", [96, 2, 4 * S], bf16)
        dA = sb("dA", [128, 2, S])
        dBu = sb("dBu", [128, 2, S])
        hst = sb("hst", [128, 2, S])
        hc = sp[:, 0:4, :]
        y1, y2 = sp[:, 4, :], sp[:, 5, :]
        (sres, yl), (ff, s2), (yy, x6) = ([sp[:, i, 0:HALF], sp[:, i, HALF:S]] for i in range(3))
        outs = sb("outs", [128, 2, 128])

        F = ctx.enter_context(nc.psum_tensor("F", [128, 5, 512], fp32))
        G = ctx.enter_context(nc.psum_tensor("G", [128, 3, 512], fp32))
        turned = F[:, 0:2, :].bitcast(bf16).rearrange("p k (i q) -> p (k i) q", q=S)

        sem = {name: ctx.enter_context(nc.semaphore(name)) for name in PER}
        s_w = ctx.enter_context(nc.semaphore("weights_in"))
        s_ids = ctx.enter_context(nc.semaphore("ids_in"))
        s_c = ctx.enter_context(nc.semaphore("consts_pool"))
        s_v = ctx.enter_context(nc.semaphore("consts_dve"))
        s_ae = ctx.enter_context(nc.semaphore("a_exp_ready"))
        made = {}
        block = ctx.enter_context(nc.Block())

        def nth(name, b, k=None):
            return PER[name] * b + (PER[name] if k is None else k)

        def not_first(b):
            return not (isinstance(b, int) and b == 0)

        def turns(eng, steps):
            def turn(front, back):
                for name in STEPS:
                    row = front if name in FRONT else back
                    fn, arg = steps.get(name, (None, None)) if "_" not in name else (steps.get(name.split("_")[0] + "_", (None, None))[0], int(name.split("_")[1]))
                    if fn is not None and row is not None:
                        if arg is None:
                            fn(row)
                        else:
                            fn(row, arg)
            turn(0, None)
            turn(1, 0)
            with eng.Fori(2, NB) as b:
                turn(b, b - 1)
            turn(None, NB - 1)

        def half(x):
            return slice(64 * x, 64 * x + 64)

        def ln_of(j):
            return ("lnF", j, F[:, 4, :], 0) if j < 3 else ("lnB", j - 3, G[:, 2, :], 1)

        @block.sync
        def _(sp_):
            sp_.dma_start(ids_all[:, :], ids).then_inc(s_ids, 16)
            sp_.dma_start(wts[:, :], weights).then_inc(s_w, 16)

            def split(b):
                sp_.wait_ge(sem["qk_lo"], nth("qk_lo", b))
                for i in range(2):
                    sp_.dma_start(qk_scr[i].rearrange("p r c -> r p c"), part[64 * i:64 * i + 64, :, :]).then_inc(sem["parts_out"], 16)
                sp_.wait_ge(sem["parts_out"], nth("parts_out", b))
                flat = qk_scr.rearrange("i p (d h) c -> i p d (h c)", h=NH)
                qrow = flat[0].rearrange("p d n -> (p d) n")
                for lo, hi in ((0, 48), (48, 80), (80, 96)):
                    sp_.dma_start(QS[lo:hi, :, :].rearrange("p h c -> p (h c)"), qrow[0:hi - lo]).then_inc(sem["stack_in"], 16)
                for lo, p, times in ((0, 0, 3), (48, 1, 2), (80, 2, 1)):
                    src = flat[1, p:p + 1].to_broadcast([times, DH, NH * S]) if times > 1 else flat[1, p]
                    sp_.dma_start(KS[lo:lo + DH * times, :, :].rearrange("p h c -> p (h c)"), src).then_inc(sem["stack_in"], 16)

            def dsplit(b):
                sp_.wait_ge(sem["d_lo"], nth("d_lo", b))
                sp_.dma_start(d_scr.rearrange("i p r c -> r (i p) c"), dp[:, :, :, :].rearrange("r i p c -> r (i p) c")).then_inc(sem["dparts_out"], 16)
                sp_.wait_ge(sem["dparts_out"], nth("dparts_out", b))
                sp_.dma_start(T[:, :, :], d_scr.rearrange("i p (j r) c -> (p j) i (r c)", r=4)).then_inc(sem["dstack_in"], 16)

            def store(b):
                sp_.wait_ge(sem["out_ready"], nth("out_ready", b))
                bs = bass.ds(b, 1) if not isinstance(b, int) else slice(b, b + 1)
                for c in range(2):
                    dst = out[bs, :, :].rearrange("o (x c p) d -> c p (o x) d", x=2, c=2)[c]
                    sp_.dma_start(dst, outs[:, c, :].rearrange("p (x d) -> p x d", x=2)).then_inc(sem["stored"], 16)

            turns(sp_, {"split": (split, None), "dsplit": (dsplit, None), "turn": (store, None)})
            sp_.wait_ge(sem["stored"], 32 * NB)

        @block.gpsimd
        def _(g):
            cnt = [0]

            def link(ins):
                cnt[0] += 1
                ins.then_inc(s_c, 1)
                g.wait_ge(s_c, cnt[0])

            def select(t, fill, base, pattern, mult):
                link(g.affine_select(out=t, in_=t, compare_op=ALU.not_equal, fill=fill, base=base,
                                     pattern=pattern, channel_multiplier=mult))

            link(g.memset(ident[:, :], 0.0))
            select(ident[:, :], 1.0, 0, [[-1, 128]], 1)
            link(g.memset(centre[:, :], 0.0))
            for x in range(2):
                link(g.memset(centre[half(x), half(x)], -1.0 / D))
            select(centre[:, :], 1.0 - 1.0 / D, 0, [[-1, 128]], 1)
            link(g.memset(halfmean[:, :], 0.0))
            for x in range(2):
                link(g.memset(halfmean[half(x), x:x + 1], 1.0 / D))
            link(g.memset(sel_den[:, :], 0.0))
            v = sel_den[:, :].rearrange("p (h i) -> p h i", i=32)
            select(v, 1.0, -16, [[-32, 4], [0, 32]], 1)
            link(g.memset(sel_dn[:, :, :], 0.0))
            link(g.memset(sel_m[:, :, :], 0.0))
            for p in range(3):
                q = slice(32 * p, 32 * p + 32)
                v = sel_dn[q, :, :].rearrange("p s (j n) -> p s j n", n=NS)
                select(v, 1.0, 0, [[-8, 4], [-1, 8], [0, NS]], 1)
                select(sel_m[q, :, :], 1.0, 0, [[-1, NT * E], [0, 64]], 1)
            link(g.memset(neg_half[:, :], -0.5))
            link(g.memset(e_base[:, :], float(np.e)))
            link(g.memset(M[:, :, :], 0.0))
            link(g.memset(KS[96:128, :, :], 1.0))
            link(g.memset(xip[:, 0:DC - 1], 0.0))
            link(g.memset(gpool[:, :], 0.0))
            link(g.memset(zero[:, :], 0.0))
            made["pool"] = cnt[0]

            def rstd(j):
                def fn(b):
                    side, i, _, n = ln_of(j)
                    g.wait_ge(sem[side + "_vareps"], nth(side + "_vareps", b, i + 1))
                    g.tensor_tensor(ln_rs[:, n, :], ln_ve[:, n, :], neg_half[:, :], ALU.pow).then_inc(sem[side + "_rstd"], 1)
                return fn

            def gather(b):
                if not_first(b):
                    g.wait_ge(sem["valid_bc"], nth("valid_bc", b, 0))
                g.wait_ge(sem["ids_clipped"], nth("ids_clipped", b))
                g.tensor_tensor(gpool[:, :], neg_half[:, :], neg_half[:, :], ALU.add)
                for t in range(NT):
                    g.indirect_dma_start(rows[:, t, :], None, table[:, :], bass.IndirectOffsetOnAxis(ap=ids_c[:, t:t + 1], axis=0)).then_inc(sem["rows_in"], 16)

            def router(n):
                def fn(b):
                    g.wait_ge(sem[f"r{n}"], nth(f"r{n}", b, 1))
                    g.tensor_tensor(ex2[:, n, :], e_base[:, :], dlt[:, n, :], ALU.pow).then_inc(sem[f"e{n}"], 1)
                return fn

            def ffn(b, e):
                i = e - 2
                if i < 0:
                    return
                g.wait_ge(sem["y0"], nth("y0", b, i + 2))
                if i:
                    g.wait_ge(sem["acc0"], nth("acc0", b, i))
                if i == 7 and not_first(b):
                    g.wait_ge(sem["h2_taken"], nth("h2_taken", b, 0))
                o = h2[:, :] if i == 7 else acc[:, (i + 1) % 2, :]
                g.tensor_tensor(o, acc[:, i % 2, :], ye[:, i % 2, :], ALU.add).then_inc(sem["acc0"], 1)

            def take(b):
                g.wait_ge(sem["acc0"], nth("acc0", b))
                if not_first(b):
                    g.wait_ge(sem["h3_ready"], nth("h3_ready", b, 0))
                g.tensor_tensor(h2b[:, :], h2[:, :], zero[:, :], ALU.add).then_inc(sem["h2_taken"], 1)

            def grp(b, k):
                if k == GROUPS:
                    return
                g.wait_ge(sem["scanned"], nth("scanned", b, k + 1))
                if k == 0:
                    g.wait_ge(sem["cr_ready"], nth("cr_ready", b))
                if k >= 4:
                    g.wait_ge(sem["y_sum"], nth("y_sum", b, k // 4))
                g.tensor_tensor(hc[:, k % 4, :], hst[:, k % 2, :], Cr[:, :], ALU.mult).then_inc(sem["hc_ready"], 1)

            def exp(b, i):
                for e in range(2 * i - 2, 2 * i):
                    if e < 0:
                        continue
                    g.wait_ge(sem["y1e"], nth("y1e", b, e + 1))
                    if e:
                        g.wait_ge(sem["acc1"], nth("acc1", b, e))
                    o = h4[:, :] if e == 7 else accb[:, (e + 1) % 2, :]
                    a = h3[:, :] if e == 0 else accb[:, e % 2, :]
                    g.tensor_tensor(o, a, yeb[:, e % 2, :], ALU.add).then_inc(sem["acc1"], 1)

            steps = {f"ln{j}b": (rstd(j), None) for j in range(NLN)}
            steps |= {"gather": (gather, None), "router0": (router(0), None), "router1": (router(1), None), "ffn_": (ffn, 0),
                      "take": (take, None), "grp_": (grp, 0), "exp_": (exp, 0)}
            turns(g, steps)

        @block.scalar
        def _(a):
            act = nc.scalar.activation
            a.wait_ge(s_w, 16)
            act(a_exp[:, :], w("a_log"), ACT.Exp).then_inc(s_ae, 1)

            def ln(j):
                def fn(b):
                    side, i, bank, n = ln_of(j)
                    a.wait_ge(sem[side + "_centred"], nth(side + "_centred", b, i + 1))
                    act(ln_xc[:, n, :], bank[:, 0:HALF], ACT.Copy).then_inc(sem[side + "_kept"], 1)
                    act(ln_sq[:, n, :], bank[:, 0:HALF], ACT.Square).then_inc(sem[side + "_squared"], 1)
                return fn

            def tok(b):
                a.wait_ge(sem["tok_transposed"], nth("tok_transposed", b))
                act(eg[:, :], F[:, 0, :], ACT.Copy).then_inc(sem["eg_ready"], 1)

            def feat(b):
                a.wait_ge(sem["feat_done"], nth("feat_done", b))
                act(cat1[:, :], F[:, 3, :], ACT.Gelu, bias=w("b_eg")).then_inc(sem["cat_ready"], 1)
                act(cat2[:, :], F[0:64, 4, :], ACT.Gelu, bias=w("b_vis", slice(0, 64))).then_inc(sem["cat_ready"], 1)

            def fuse(b):
                a.wait_ge(sem["fuse_done"], nth("fuse_done", b))
                act(f0[:, :], F[:, 1, 0:HALF], ACT.Gelu, bias=w("b_f")).then_inc(sem["fuse_act"], 1)

            def qkv(b):
                a.wait_ge(sem["qk_done"], nth("qk_done", b))
                act(qkf[:, :].rearrange("p (x c) -> p x c", x=2), F[:, 0:2, 0:HALF], ACT.Identity, bias=w("b_qk")).then_inc(sem["qk_full"], 1)

            def split(b):
                if not_first(b):
                    a.wait_ge(sem["parts_out"], nth("parts_out", b, 0))
                a.wait_ge(sem["qk_full"], nth("qk_full", b))
                act(part[:, 0, :], qkf[:, :], ACT.Copy).then_inc(sem["qk_hi"], 1)
                a.wait_ge(sem["qk_r"], nth("qk_r", b))
                act(part[:, 1, :], qkr[:, :], ACT.Copy).then_inc(sem["qk_mid"], 1)

            def s2_(b, n):
                a.wait_ge(sem["s2_done"], nth("s2_done", b, n + 1))
                if n >= 4:
                    a.wait_ge(sem["pv_done"], nth("pv_done", b, (n - 4) // 2 + 1))
                act(P[:, n % 4, :, :], F[:, 2 * (n % 2):2 * (n % 2) + 2, :], ACT.Exp, scale=DH ** -0.5).then_inc(sem["exp_done"], 1)

            def mask0(b):
                a.wait_ge(sem["mt0_done"], nth("mt0_done", b))
                act(mt[:, 0, :], F[0:96, 4, 0:64].bitcast(bf16), ACT.Copy).then_inc(sem["mt0_in"], 1)
                a.wait_ge(sem["mbc0_done"], nth("mbc0_done", b))
                act(mbc[:, 0, :, :], F[:, 0:4, :].rearrange("p k (i c) -> p (k i) c", i=2), ACT.Copy).then_inc(sem["mbc0_in"], 1)

            def mask1(b):
                a.wait_ge(sem["mt1_done"], nth("mt1_done", b))
                act(mt[:, 1, :], G[0:96, 2, 0:64].bitcast(bf16), ACT.Copy).then_inc(sem["mt1_in"], 1)
                for i in range(2):
                    a.wait_ge(sem["mbc1_done"], nth("mbc1_done", b, i + 1))
                    act(mbc[:, 1, 4 * i:4 * i + 4, :], G[:, 0:2, :].rearrange("p k (i c) -> p (k i) c", i=2), ACT.Copy).then_inc(sem["mbc1_in"], 1)

            def ffn(b, e):
                if e == 9:
                    return
                a.wait_ge(sem["hid0_done"], nth("hid0_done", b, e + 1))
                if e >= 2:
                    a.wait_ge(sem["w2_0_done"], nth("w2_0_done", b, e - 1))
                p = 2 * (e % 2)
                for ch in range(2):
                    act(hid[:, p + ch, :, :], F[:, p:p + 2, HALF * ch:HALF * ch + HALF], ACT.Gelu,
                        bias=w("b1_0", cols=(2 * e + ch, 2 * e + ch + 1))).then_inc(sem["gelu0"], 1)

            def inproj(b):
                a.wait_ge(sem["in_done"], nth("in_done", b))
                act(xip[:, DC - 1:].rearrange("p (x c) -> p x c", x=2), G[:, 0:2, 0:HALF], ACT.Identity, bias=w("b_inx")).then_inc(sem["xi_ready"], 1)
                act(sz[:, :].rearrange("p (x c) -> p x c", x=2), G[:, 0:2, HALF:S], ACT.Silu, bias=w("b_inz")).then_inc(sem["sz_ready"], 1)

            def conv(b):
                a.wait_ge(sem["conv"], nth("conv", b))
                act(u[:, :], cv[:, 1, :], ACT.Silu, bias=w("conv_b")).then_inc(sem["u_ready"], 1)

            def xproj(b):
                a.wait_ge(sem["xp_done"], nth("xp_done", b))
                act(dtl[:, :], G[0:DTR, 0, :], ACT.Copy).then_inc(sem["dtl_ready"], 1)
                act(Br[:, :], G[:, 1, :], ACT.Copy).then_inc(sem["br_ready"], 1)

            def softplus(b):
                a.wait_ge(sem["dtp_done"], nth("dtp_done", b))
                act(sp[:, 0, :], G[:, 0, :], ACT.Abs, bias=w("b_dt")).then_inc(sem["sp_abs"], 1)
                act(sp[:, 1, :], G[:, 0, :], ACT.Relu, bias=w("b_dt")).then_inc(sem["sp_relu"], 1)
                a.wait_ge(sem["sp_abs"], nth("sp_abs", b))
                act(sp[:, 2, :], sp[:, 0, :], ACT.Exp, scale=-1.0).then_inc(sem["sp_exp"], 1)
                a.wait_ge(sem["sp_u1"], nth("sp_u1", b))
                act(sp[:, 4, :], sp[:, 3, :], ACT.Ln).then_inc(sem["sp_ln"], 1)

            def dsplit(b):
                for i, ready in ((0, "dt_ready"), (1, "dx_ready")):
                    a.wait_ge(sem[ready], nth(ready, b))
                    act(dp[:, i, 0, :], dd[:, i, :], ACT.Copy).then_inc(sem["d_hi"], 1)
                for i in range(2):
                    a.wait_ge(sem["d_r"], nth("d_r", b, i + 1))
                    act(dp[:, i, 1, :], dd_r[:, i, :], ACT.Copy).then_inc(sem["d_mid"], 1)

            def grp(b, k):
                if k == GROUPS:
                    return
                a.wait_ge(sem["spread"], nth("spread", b, k + 1))
                if k >= 2:
                    a.wait_ge(sem["scanned"], nth("scanned", b, k - 1))
                act(dA[:, k % 2, :], G[:, 0, :], ACT.Exp, scale=a_neg[:, k:k + 1]).then_inc(sem["da_ready"], 1)

            def fc1(b):
                a.wait_ge(sem["fc1_done"], nth("fc1_done", b))
                for ch in range(2):
                    act(hidb[:, ch, :, :], G[:, 0:2, HALF * ch:HALF * ch + HALF], ACT.Gelu, bias=w("b_fc1", cols=(ch, ch + 1))).then_inc(sem["fc1_act"], 1)

            def fc2(b):
                a.wait_ge(sem["fc2_done"], nth("fc2_done", b))
                act(ff[:, :], G[:, 2, 0:HALF], ACT.Gelu, bias=w("b_fc2")).then_inc(sem["ff_ready"], 1)

            def exp(b, i):
                if i == E // 2:
                    return
                a.wait_ge(sem["hid1_done"], nth("hid1_done", b, i + 1))
                if i >= 2:
                    a.wait_ge(sem["w2_1_done"], nth("w2_1_done", b, i - 1))
                for n in range(2):
                    e = 2 * i + n
                    act(hidb[:, 2 * (i % 2) + n, :, :], G[:, 0:2, HALF * n:HALF * n + HALF], ACT.Gelu,
                        bias=w("b1_1", cols=(e, e + 1))).then_inc(sem["gelu1"], 1)

            steps = {f"ln{j}a": (ln(j), None) for j in range(NLN)}
            steps |= {"tok": (tok, None), "feat": (feat, None), "fuse": (fuse, None), "qkv": (qkv, None), "split": (split, None),
                      "s2_": (s2_, 0), "mask0": (mask0, None), "mask1": (mask1, None), "ffn_": (ffn, 0), "inproj": (inproj, None),
                      "conv": (conv, None), "xproj": (xproj, None), "softplus": (softplus, None), "dsplit": (dsplit, None),
                      "grp_": (grp, 0), "fc1": (fc1, None), "fc2": (fc2, None), "exp_": (exp, 0)}
            turns(a, steps)

        @block.vector
        def _(v):
            tt, ts, stt = nc.vector.tensor_tensor, nc.vector.tensor_scalar, nc.vector.scalar_tensor_tensor
            cnt = [0]

            def link(ins):
                cnt[0] += 1
                ins.then_inc(s_v, 1)
                v.wait_ge(s_v, cnt[0])

            v.wait_ge(s_c, made["pool"])
            link(v.tensor_copy(identb[:, :], ident[:, :]))
            v.wait_ge(s_w, 16)
            link(v.tensor_copy(wo3[:, 0, :], w("w_o")))
            link(tt(wo_r[:, 0, :], w("w_o"), wo3[:, 0, :], ALU.subtract))
            link(v.tensor_copy(wo3[:, 1, :], wo_r[:, 0, :]))
            link(tt(wo_r[:, 1, :], wo_r[:, 0, :], wo3[:, 1, :], ALU.subtract))
            link(v.tensor_copy(wo3[:, 2, :], wo_r[:, 1, :]))
            link(v.memset(sel_y[:, :, :], 0.0))
            for r in range(4):
                link(v.tensor_reduce(sel_y[:, r, r::4], ident[:, :].rearrange("p (j n) -> p j n", n=NS), AX.X, ALU.add))
            v.wait_ge(s_ae, 1)
            link(ts(a_neg[:, :], a_exp[:, :], -1.0, None, ALU.mult))
            made["dve"] = cnt[0]
            v.wait_ge(s_ids, 16)

            def ln_b(j):
                def fn(b):
                    side, i, bank, n = ln_of(j)
                    v.wait_ge(sem[side + "_var"], nth(side + "_var", b, i + 1))
                    ts(ln_ve[:, n, :], bank[:, HALF:HALF + NT], LN_EPS, None, ALU.add).then_inc(sem[side + "_vareps"], 1)
                return fn

            def ln_c(j):
                def fn(b):
                    side, i, bank, n = ln_of(j)
                    v.wait_ge(sem[side + "_bc"], nth(side + "_bc", b, i + 1))
                    v.wait_ge(sem[side + "_kept"], nth(side + "_kept", b, i + 1))
                    tt(ln_o[:, j, :], bank[:, HALF:S], ln_xc[:, n, :], ALU.mult).then_inc(sem[side + "_out"], 1)
                    after = {0: tok_out, 4: ln4_out, 5: ln5_out, 7: ln7_out}.get(j)
                    if after:
                        v.wait_ge(sem[side + "_out"], nth(side + "_out", b, i + 1))
                        after(b)
                return fn

            def gather(b):
                src = ids_all[:, bass.ds(b * NT, NT)] if not isinstance(b, int) else ids_all[:, b * NT:b * NT + NT]
                if not_first(b):
                    v.wait_ge(sem["rows_in"], nth("rows_in", b, 0))
                    v.wait_ge(sem["valid_bc"], nth("valid_bc", b, 0))
                ts(ids_c[:, :], src, 0, N_ITEMS - 1, ALU.max, ALU.min).then_inc(sem["ids_clipped"], 1)
                ts(valid[:, :], src, 0, None, ALU.not_equal).then_inc(sem["valid_ready"], 1)

            def tok(b):
                v.wait_ge(sem["tok_transposed"], nth("tok_transposed", b))
                v.tensor_copy(vis[:, :], F[0:VIS, 1, :]).then_inc(sem["vis_ready"], 1)
                v.tensor_copy(embp[:, :], F[:, 2, 0:HALF]).then_inc(sem["embp_ready"], 1)

            def tok_out(b):
                ts(tok_a[:, :], ln_o[:, 0, :], w("g_t"), w("be_t"), ALU.mult, ALU.add).then_inc(sem["tok_affine"], 1)
                v.wait_ge(sem["valid_bc"], nth("valid_bc", b))
                v.wait_ge(sem["tok_affine"], nth("tok_affine", b))
                tt(tok_m[:, :], F[:, 2, 0:HALF], tok_a[:, :], ALU.mult).then_inc(sem["tok_masked"], 1)
                v.wait_ge(sem["tok_masked"], nth("tok_masked", b))
                stt(out=h0[:, :], in0=tok_m[:, :], scalar=0.1, in1=embp[:, :], op0=ALU.mult, op1=ALU.add).then_inc(sem["h0_ready"], 1)

            def qkv(b):
                v.wait_ge(sem["v_done"], nth("v_done", b))
                tt(vsb[:, :, :], F[:, 2:4, 0:HALF].rearrange("p x (c n) -> p x c n", c=2), w("bv").unsqueeze(1).to_broadcast([128, NT, 128]), ALU.add).then_inc(sem["v_ready"], 1)

            def split(b):
                v.wait_ge(sem["qk_hi"], nth("qk_hi", b))
                tt(qkr[:, :], qkf[:, :], part[:, 0, :], ALU.subtract).then_inc(sem["qk_r"], 1)
                v.wait_ge(sem["qk_mid"], nth("qk_mid", b))
                tt(part[:, 2, :], qkr[:, :], part[:, 1, :], ALU.subtract).then_inc(sem["qk_lo"], 1)

            def s1_(b, n):
                v.wait_ge(sem["s1_done"], nth("s1_done", b, n + 1))
                p = 2 * (n % 2)
                v.tensor_reduce(nmax[:, 2 * n:2 * n + 2], F[:, p:p + 2, :], AX.X, ALU.max, negate=True).then_inc(sem["max_done"], 1)

            def msplit(b):
                v.wait_ge(sem["max_done"], nth("max_done", b))
                v.tensor_copy(M[:, :, 0], nmax[:, :]).then_inc(sem["max_split"], 1)
                v.wait_ge(sem["max_split"], nth("max_split", b, 1))
                tt(nmax_r[:, 0, :], nmax[:, :], M[:, :, 0], ALU.subtract).then_inc(sem["max_split"], 1)
                v.wait_ge(sem["max_split"], nth("max_split", b, 2))
                v.tensor_copy(M[:, :, 1], nmax_r[:, 0, :]).then_inc(sem["max_split"], 1)
                v.wait_ge(sem["max_split"], nth("max_split", b, 3))
                tt(nmax_r[:, 1, :], nmax_r[:, 0, :], M[:, :, 1], ALU.subtract).then_inc(sem["max_split"], 1)
                v.wait_ge(sem["max_split"], nth("max_split", b, 4))
                v.tensor_copy(M[:, :, 2], nmax_r[:, 1, :]).then_inc(sem["max_split"], 1)
                v.wait_ge(sem["max_turned"], nth("max_turned", b))
                v.tensor_copy(QS[96:128, :, :], turned[96:128, :, :]).then_inc(sem["max_in"], 1)

            def den(b):
                v.wait_ge(sem["pv_done"], nth("pv_done", b))
                v.tensor_copy(osb[:, :], F[:, 4, :]).then_inc(sem["o_ready"], 1)
                v.wait_ge(sem["den_done"], nth("den_done", b))
                v.reciprocal(rec[:, :], F[:, 0, :]).then_inc(sem["rec_ready"], 1)
                v.wait_ge(sem["rec_ready"], nth("rec_ready", b))
                tt(obf[:, :], osb[:, :], rec[:, :], ALU.mult).then_inc(sem["o_bf"], 1)

            def wo(b):
                v.wait_ge(sem["wo_done"], nth("wo_done", b))
                stt(out=h1[:, :], in0=F[:, 1, 0:HALF], scalar=w("b_o"), in1=h0[:, :], op0=ALU.add, op1=ALU.add).then_inc(sem["h1_ready"], 1)

            def router(n):
                bank, bias = (F, None) if n == 0 else (G, w("br1"))

                def fn(b):
                    v.wait_ge(sem[f"lg{n}_done"], nth(f"lg{n}_done", b))
                    lgn = lg[:, n, :, :]
                    src = bank[:, 0:2, 0:2 * E].rearrange("p x (c e) -> p x c e", e=E)
                    dst = lgn.rearrange("p (x c) e -> p x c e", x=2)
                    if bias is None:
                        v.tensor_copy(dst, src).then_inc(sem[f"lg{n}_in"], 1)
                    else:
                        tt(dst, src, bias.rearrange("p (x c e) -> p x c e", x=2, e=E), ALU.add).then_inc(sem[f"lg{n}_in"], 1)
                    v.wait_ge(sem[f"lg{n}_in"], nth(f"lg{n}_in", b))
                    v.memset(gate[:, 2 * n:2 * n + 1], 0.0)
                    for t in range(NT):
                        v.max(top[:, n, t, :], lgn[:, t, :]).then_inc(sem[f"top{n}"], 1)
                    v.wait_ge(sem[f"top{n}"], nth(f"top{n}", b))
                    v.memset(gate[:, 2 * n + 1:2 * n + 2], 0.0)
                    for t in range(NT):
                        v.max_index(idx[:, n, t, :], top[:, n, t, :], lgn[:, t, :]).then_inc(sem[f"idx{n}"], 1)
                    r = f"r{n}"
                    tt(dlt[:, n, :], top[:, n, :, 1], top[:, n, :, 0], ALU.subtract).then_inc(sem[r], 1)
                    v.wait_ge(sem[f"idx{n}"], nth(f"idx{n}", b))
                    v.tensor_copy(idxf[:, n, :, :], idx[:, n, :, 0:2]).then_inc(sem[r], 1)
                    v.wait_ge(sem[r], nth(r, b, 2))
                    iota = w("iota").rearrange("p (t e) -> p t e", e=E)
                    for i in range(2):
                        tt(eq[:, n, i, :, :], iota, idxf[:, n, :, i:i + 1].to_broadcast([128, NT, E]), ALU.is_equal).then_inc(sem[r], 1)
                    v.wait_ge(sem[f"e{n}"], nth(f"e{n}", b))
                    ts(ssum[:, n, :], ex2[:, n, :], 1.0, None, ALU.add).then_inc(sem[r], 1)
                    v.wait_ge(sem[r], nth(r, b, 5))
                    v.reciprocal(w12[:, n, 0, :], ssum[:, n, :]).then_inc(sem[r], 1)
                    v.wait_ge(sem[r], nth(r, b, 6))
                    tt(w12[:, n, 1, :], w12[:, n, 0, :], ex2[:, n, :], ALU.mult).then_inc(sem[r], 1)
                    v.wait_ge(sem[r], nth(r, b, 7))
                    for i in range(2):
                        tt(mk[:, n, i, :].rearrange("p (t e) -> p t e", e=E), eq[:, n, i, :, :],
                           w12[:, n, i, :].unsqueeze(2).to_broadcast([128, NT, E]), ALU.mult).then_inc(sem[r], 1)
                    v.wait_ge(sem[r], nth(r, b, 9))
                    tt(mk[:, n, 2, :], mk[:, n, 0, :], mk[:, n, 1, :], ALU.add).then_inc(sem[f"mask{n}"], 1)
                    m = f"mp{n}"
                    v.wait_ge(sem[f"mask{n}"], nth(f"mask{n}", b))
                    v.tensor_copy(mk3[:, n, 0, :], mk[:, n, 2, :]).then_inc(sem[m], 1)
                    v.wait_ge(sem[m], nth(m, b, 1))
                    tt(mk_r[:, n, 0, :], mk[:, n, 2, :], mk3[:, n, 0, :], ALU.subtract).then_inc(sem[m], 1)
                    v.wait_ge(sem[m], nth(m, b, 2))
                    v.tensor_copy(mk3[:, n, 1, :], mk_r[:, n, 0, :]).then_inc(sem[m], 1)
                    v.wait_ge(sem[m], nth(m, b, 3))
                    tt(mk_r[:, n, 1, :], mk_r[:, n, 0, :], mk3[:, n, 1, :], ALU.subtract).then_inc(sem[m], 1)
                    v.wait_ge(sem[m], nth(m, b, 4))
                    v.tensor_copy(mk3[:, n, 2, :], mk_r[:, n, 1, :]).then_inc(sem[m], 1)
                return fn

            def ffn(b, e):
                e = e - 1
                if e < 0:
                    return
                v.wait_ge(sem["w2_0_done"], nth("w2_0_done", b, e + 1))
                src = F[:, 4, 0:HALF]
                bias = w("b2_0", cols=(e, e + 1))
                if e == 0:
                    v.wait_ge(sem["h1_ready"], nth("h1_ready", b))
                    stt(out=acc[:, 0, :], in0=src, scalar=bias, in1=h1[:, :], op0=ALU.add, op1=ALU.add).then_inc(sem["y0"], 1)
                else:
                    if e == 1:
                        v.wait_ge(sem["mbc0_in"], nth("mbc0_in", b))
                    if e >= 3:
                        v.wait_ge(sem["acc0"], nth("acc0", b, e - 2))
                    stt(out=ye[:, (e - 1) % 2, :], in0=src, scalar=bias, in1=mbc[:, 0, e - 1, :], op0=ALU.add, op1=ALU.mult).then_inc(sem["y0"], 1)

            def conv(b):
                v.wait_ge(sem["xi_ready"], nth("xi_ready", b))
                cw = [w("conv_w", cols=(i, i + 1)) for i in range(DC)]
                ts(cv[:, 0, :], xip[:, 0:S], cw[0], None, ALU.mult).then_inc(sem["conv"], 1)
                for i in range(1, DC):
                    v.wait_ge(sem["conv"], nth("conv", b, i))
                    stt(out=cv[:, i % 2, :], in0=xip[:, i:i + S], scalar=cw[i], in1=cv[:, (i - 1) % 2, :], op0=ALU.mult, op1=ALU.add).then_inc(sem["conv"], 1)

            def xproj(b):
                v.wait_ge(sem["xp_done"], nth("xp_done", b))
                v.tensor_copy(Cr[:, :], G[:, 2, :]).then_inc(sem["cr_ready"], 1)

            def softplus(b):
                v.wait_ge(sem["sp_exp"], nth("sp_exp", b))
                ts(sp[:, 3, :], sp[:, 2, :], 1.0, None, ALU.add).then_inc(sem["sp_u1"], 1)
                v.wait_ge(sem["sp_u1"], nth("sp_u1", b))
                stt(out=sp[:, 5, :], in0=sp[:, 3, :], scalar=1.0, in1=sp[:, 2, :], op0=ALU.subtract, op1=ALU.subtract).then_inc(sem["sp_r"], 1)
                v.wait_ge(sem["sp_r"], nth("sp_r", b))
                v.wait_ge(sem["sp_relu"], nth("sp_relu", b))
                tt(sp[:, 0, :], sp[:, 1, :], sp[:, 5, :], ALU.subtract).then_inc(sem["sp_t"], 1)
                v.wait_ge(sem["sp_ln"], nth("sp_ln", b))
                v.wait_ge(sem["sp_t"], nth("sp_t", b))
                tt(dd[:, 0, :], sp[:, 4, :], sp[:, 0, :], ALU.add).then_inc(sem["dt_ready"], 1)
                v.wait_ge(sem["u_ready"], nth("u_ready", b))
                v.wait_ge(sem["dt_ready"], nth("dt_ready", b))
                tt(dd[:, 1, :], dd[:, 0, :], u[:, :], ALU.mult).then_inc(sem["dx_ready"], 1)

            def dsplit(b):
                for i in range(2):
                    v.wait_ge(sem["d_hi"], nth("d_hi", b, i + 1))
                    tt(dd_r[:, i, :], dd[:, i, :], dp[:, i, 0, :], ALU.subtract).then_inc(sem["d_r"], 1)
                for i in range(2):
                    v.wait_ge(sem["d_mid"], nth("d_mid", b, i + 1))
                    tt(dp[:, i, 2, :], dd_r[:, i, :], dp[:, i, 1, :], ALU.subtract).then_inc(sem["d_lo"], 1)

            def grp(b, k):
                if k == GROUPS:
                    return
                v.wait_ge(sem["spread"], nth("spread", b, k + 1))
                if k == 0:
                    v.wait_ge(sem["br_ready"], nth("br_ready", b))
                if k >= 2:
                    v.wait_ge(sem["scanned"], nth("scanned", b, k - 1))
                tt(dBu[:, k % 2, :], G[:, 1, :], Br[:, :], ALU.mult).then_inc(sem["dbu_ready"], 1)
                v.wait_ge(sem["dbu_ready"], nth("dbu_ready", b, k + 1))
                v.wait_ge(sem["da_ready"], nth("da_ready", b, k + 1))
                if k >= 2:
                    v.wait_ge(sem["hc_ready"], nth("hc_ready", b, k - 1))
                v.tensor_tensor_scan(hst[:, k % 2, :], dA[:, k % 2, :], dBu[:, k % 2, :], 0.0, ALU.mult, ALU.add).then_inc(sem["scanned"], 1)

            def yout(b):
                v.wait_ge(sem["y_sum"], nth("y_sum", b))
                stt(out=y1, in0=u[:, :], scalar=w("d_ssm"), in1=G[:, 2, :], op0=ALU.mult, op1=ALU.add).then_inc(sem["y1"], 1)
                v.wait_ge(sem["y1"], nth("y1", b))
                v.wait_ge(sem["sz_ready"], nth("sz_ready", b))
                tt(y2, y1, sz[:, :], ALU.mult).then_inc(sem["y2"], 1)
                v.wait_ge(sem["out_done"], nth("out_done", b))
                stt(out=sres[:, :], in0=G[:, 0, 0:HALF], scalar=w("b_out"), in1=ln_o[:, 3, :], op0=ALU.add, op1=ALU.add).then_inc(sem["s_ready"], 1)

            def ln4_out(b):
                ts(yl[:, :], ln_o[:, 4, :], w("g1"), w("be1"), ALU.mult, ALU.add).then_inc(sem["yln"], 1)

            def fc2(b):
                v.wait_ge(sem["yln"], nth("yln", b))
                v.wait_ge(sem["ff_ready"], nth("ff_ready", b))
                tt(s2[:, :], yl[:, :], ff[:, :], ALU.add).then_inc(sem["s2_ready"], 1)

            def ln5_out(b):
                ts(yy[:, :], ln_o[:, 5, :], w("g2"), w("be2"), ALU.mult, ALU.add).then_inc(sem["yy"], 1)
                v.wait_ge(sem["yy"], nth("yy", b))
                v.wait_ge(sem["h2_taken"], nth("h2_taken", b))
                tt(h3[:, :], yy[:, :], h2b[:, :], ALU.add).then_inc(sem["h3_ready"], 1)

            def ln7_out(b):
                ts(x6[:, :], ln_o[:, 7, :], w("g_m"), w("be_m"), ALU.mult, ALU.add).then_inc(sem["x6_ready"], 1)

            def exp(b, i):
                for e in range(2 * i - 2, 2 * i):
                    if e < 0:
                        continue
                    v.wait_ge(sem["w2_1_done"], nth("w2_1_done", b, e // 2 + 1))
                    if e == 0:
                        v.wait_ge(sem["mbc1_in"], nth("mbc1_in", b))
                    if e >= 2:
                        v.wait_ge(sem["acc1"], nth("acc1", b, e - 1))
                    stt(out=yeb[:, e % 2, :], in0=G[:, 2, HALF * (e % 2):HALF * (e % 2) + HALF], scalar=w("b2_1", cols=(e, e + 1)),
                        in1=mbc[:, 1, e, :], op0=ALU.add, op1=ALU.mult).then_inc(sem["y1e"], 1)

            def turn(b):
                v.wait_ge(sem["out_turned"], nth("out_turned", b))
                if not_first(b):
                    v.wait_ge(sem["stored"], nth("stored", b, 0))
                v.tensor_copy(outs[:, :, :], G[:, 0, 0:256].rearrange("p (c n) -> p c n", c=2)).then_inc(sem["out_ready"], 1)

            steps = {f"ln{j}b": (ln_b(j), None) for j in range(NLN)} | {f"ln{j}c": (ln_c(j), None) for j in range(NLN)}
            steps |= {"gather": (gather, None), "tok": (tok, None), "qkv": (qkv, None), "split": (split, None), "s1_": (s1_, 0), "msplit": (msplit, None),
                      "den": (den, None), "wo": (wo, None), "router0": (router(0), None), "router1": (router(1), None),
                      "ffn_": (ffn, 0), "conv": (conv, None), "xproj": (xproj, None), "softplus": (softplus, None), "dsplit": (dsplit, None),
                      "grp_": (grp, 0), "yout": (yout, None), "fc2": (fc2, None), "exp_": (exp, 0), "turn": (turn, None)}
            turns(v, steps)

        @block.tensor
        def _(pe):
            mm = nc.tensor.matmul
            pe.wait_ge(s_w, 16)
            pe.wait_ge(s_c, made["pool"])
            pe.wait_ge(s_v, made["dve"])

            def ln_a(j, x, ready, k=None):
                def fn(b):
                    side, i, bank, n = ln_of(j)
                    pe.wait_ge(sem[ready], nth(ready, b, k))
                    mm(bank[:, 0:HALF], centre[:, :], x, start=True, stop=True).then_inc(sem[side + "_centred"], 1)
                return fn

            def ln_b(j):
                def fn(b):
                    side, i, bank, n = ln_of(j)
                    pe.wait_ge(sem[side + "_squared"], nth(side + "_squared", b, i + 1))
                    for c in range(2):
                        last = mm(bank[:, HALF + 2 * c:HALF + 2 * c + 2], ln_sq[:, n, 128 * c:128 * c + 128], halfmean[:, :], start=True, stop=True)
                    last.then_inc(sem[side + "_var"], 1)
                return fn

            def ln_c(j):
                def fn(b):
                    side, i, bank, n = ln_of(j)
                    pe.wait_ge(sem[side + "_rstd"], nth(side + "_rstd", b, i + 1))
                    for c in range(2):
                        for x_ in range(2):
                            last = mm(bank[half(x_), HALF + 128 * c:HALF + 128 * c + 128],
                                      ln_rs[:, n, 2 * c + x_:2 * c + x_ + 1].to_broadcast([128, 64]), ident[:, :], start=True, stop=True)
                    last.then_inc(sem[side + "_bc"], 1)
                return fn

            def tok(b):
                pe.wait_ge(sem["rows_in"], nth("rows_in", b))
                for x_ in range(2):
                    for c in range(2):
                        t = 2 * x_ + c
                        nc.tensor.transpose(F[:, 0, 128 * t:128 * t + 128], rows[:, t, 0:128], ident[:, :])
                        nc.tensor.transpose(F[0:VIS, 1, 128 * t:128 * t + 128], rows[:, t, 128:ROW], ident[:, :])
                for c in range(2):
                    for x_ in range(2):
                        last = mm(F[half(x_), 2, 128 * c:128 * c + 128], rows[:, 2 * x_ + c, 0:64], ident[:, :], start=True, stop=True)
                last.then_inc(sem["tok_transposed"], 1)

            def feat(b):
                pe.wait_ge(sem["eg_ready"], nth("eg_ready", b))
                mm(F[:, 3, :], w("w_eg"), eg[:, :], start=True, stop=True)
                pe.wait_ge(sem["vis_ready"], nth("vis_ready", b))
                mm(F[0:64, 4, :], w("w_vis", slice(0, VIS)), vis[:, :], start=True, stop=True).then_inc(sem["feat_done"], 1)
                pe.wait_ge(sem["embp_ready"], nth("embp_ready", b))
                pe.wait_ge(sem["valid_ready"], nth("valid_ready", b))
                for c in range(2):
                    for x_ in range(2):
                        t = 2 * x_ + c
                        last = mm(F[half(x_), 2, 128 * c:128 * c + 128], valid[:, t:t + 1].to_broadcast([128, 64]), ident[:, :], start=True, stop=True)
                last.then_inc(sem["valid_bc"], 1)

            def fuse(b):
                pe.wait_ge(sem["cat_ready"], nth("cat_ready", b))
                for x_ in range(2):
                    mm(F[half(x_), 1, 0:HALF], w("w_f1"), cat1[:, HALF * x_:HALF * x_ + HALF], start=True, stop=False)
                for x_ in range(2):
                    last = mm(F[half(x_), 1, 0:HALF], w("w_f2", slice(0, 64)), cat2[:, HALF * x_:HALF * x_ + HALF], start=False, stop=True)
                last.then_inc(sem["fuse_done"], 1)

            def qkv(b):
                x1 = ln_o[:, 1, :]
                pe.wait_ge(sem["lnF_out"], nth("lnF_out", b, 2))
                for x_ in range(2):
                    last = mm(F[:, x_, 0:HALF], w("w_qk", half(x_)), x1[half(x_), :], start=True, stop=True)
                last.then_inc(sem["qk_done"], 1)
                for x_ in range(2):
                    for c in range(2):
                        last = mm(F[:, 2 + x_, 128 * c:128 * c + 128], x1[half(x_), 128 * c:128 * c + 128], w("w_v", half(x_)), start=True, stop=True)
                last.then_inc(sem["v_done"], 1)

            def s1_(b, n):
                if n == 0:
                    pe.wait_ge(sem["qk_full"], nth("qk_full", b))
                    pe.wait_ge(sem["stack_in"], nth("stack_in", b))
                if n == 1:
                    pe.wait_ge(sem["v_ready"], nth("v_ready", b))
                if n >= 2:
                    pe.wait_ge(sem["max_done"], nth("max_done", b, n - 1))
                for i in range(2):
                    h = 2 * (n % 2) + i
                    last = mm(F[:, h, :], QS[0:96, h, 128 * (n // 2):128 * (n // 2) + 128], KS[0:96, h, :], start=True, stop=True)
                last.then_inc(sem["s1_done"], 1)

            def msplit(b):
                pe.wait_ge(sem["max_split"], nth("max_split", b))
                for t in range(NT):
                    for h in range(NH):
                        last = nc.tensor.transpose(turned[96:128, h, 128 * t:128 * t + 128], M[:, NH * t + h, :], identb[:, :])
                last.then_inc(sem["max_turned"], 1)

            def s2_(b, n):
                if n == 0:
                    pe.wait_ge(sem["max_in"], nth("max_in", b))
                if n >= 2:
                    pe.wait_ge(sem["exp_done"], nth("exp_done", b, n - 1))
                kt = n // 2
                for i in range(2):
                    h = 2 * (n % 2) + i
                    last = mm(F[:, h, :], KS[:, h, 128 * kt:128 * kt + 128], QS[:, h, :], start=True, stop=True)
                last.then_inc(sem["s2_done"], 1)
                if n >= 3 and n % 2 == 1:
                    pv(b, (n - 3) // 2)

            def pv(b, kt):
                pe.wait_ge(sem["exp_done"], nth("exp_done", b, 2 * kt + 2))
                for h in range(NH):
                    last = mm(F[32 * h:32 * h + 32, 4, :], vsb[:, kt, 32 * h:32 * h + 32], P[:, (2 * kt + h // 2) % 4, h % 2, :],
                              start=(kt == 0), stop=(kt == NT - 1))
                last.then_inc(sem["pv_done"], 1)

            def den(b):
                pv(b, NT - 1)
                pe.wait_ge(sem["o_ready"], nth("o_ready", b))
                mm(F[:, 0, :], sel_den[:, :], osb[:, :], start=True, stop=True).then_inc(sem["den_done"], 1)

            def wo(b):
                pe.wait_ge(sem["o_bf"], nth("o_bf", b))
                for p in range(3):
                    for x_ in range(2):
                        last = mm(F[half(x_), 1, 0:HALF], wo3[:, p, :], obf[:, HALF * x_:HALF * x_ + HALF], start=(p == 0), stop=(p == 2))
                last.then_inc(sem["wo_done"], 1)

            def logit(n, x, wr, bank, ready, k=None):
                def fn(b):
                    pe.wait_ge(sem[ready], nth(ready, b, k))
                    for x_ in range(2):
                        for c in range(2):
                            last = mm(bank[:, x_, E * c:E * c + E], x[half(x_), 128 * c:128 * c + 128], wr[half(x_), :], start=True, stop=True)
                    last.then_inc(sem[f"lg{n}_done"], 1)
                return fn

            def mask_bc(n, e, out_):
                for c in range(2):
                    for x_ in range(2):
                        last = mm(out_[half(x_), 128 * c:128 * c + 128], sel_m[:, E * (2 * x_ + c) + e, :], mt[:, n, :], start=True, stop=True)
                return last

            def mask0(b):
                pe.wait_ge(sem["mp0"], nth("mp0", b))
                nc.tensor.transpose(F[0:96, 4, 0:64].bitcast(bf16), mk3[:, 0, :, :].rearrange("p i t -> p (i t)"), identb[:, :]).then_inc(sem["mt0_done"], 1)
                pe.wait_ge(sem["mt0_in"], nth("mt0_in", b))
                for e in range(E):
                    last = mask_bc(0, e, F[:, e // 2, HALF * (e % 2):HALF * (e % 2) + HALF])
                last.then_inc(sem["mbc0_done"], 1)

            def mask1(b):
                pe.wait_ge(sem["mp1"], nth("mp1", b))
                nc.tensor.transpose(G[0:96, 2, 0:64].bitcast(bf16), mk3[:, 1, :, :].rearrange("p i t -> p (i t)"), identb[:, :]).then_inc(sem["mt1_done"], 1)
                pe.wait_ge(sem["mt1_in"], nth("mt1_in", b))
                for i in range(2):
                    if i:
                        pe.wait_ge(sem["mbc1_in"], nth("mbc1_in", b, 1))
                    for e in range(4):
                        last = mask_bc(1, 4 * i + e, G[:, e // 2, HALF * (e % 2):HALF * (e % 2) + HALF])
                    last.then_inc(sem["mbc1_done"], 1)

            def ffn(b, e):
                x2 = ln_o[:, 2, :]
                if e < 9:
                    if e == 0:
                        pe.wait_ge(sem["mbc0_in"], nth("mbc0_in", b))
                    if e >= 2:
                        pe.wait_ge(sem["gelu0"], nth("gelu0", b, 2 * (e - 1)))
                    for ch in range(2):
                        for x_ in range(2):
                            last = mm(F[:, 2 * (e % 2) + x_, HALF * ch:HALF * ch + HALF], w("w1_0", half(x_), (128 * (2 * e + ch), 128 * (2 * e + ch) + 128)),
                                      x2[half(x_), :], start=True, stop=True)
                    last.then_inc(sem["hid0_done"], 1)
                e = e - 1
                if e < 0:
                    return
                pe.wait_ge(sem["gelu0"], nth("gelu0", b, 2 * e + 2))
                if e >= 1:
                    pe.wait_ge(sem["y0"], nth("y0", b, e))
                for ch in range(2):
                    for x_ in range(2):
                        last = mm(F[half(x_), 4, 0:HALF], w("w2_0", cols=(64 * (2 * e + ch), 64 * (2 * e + ch) + 64)),
                                  hid[:, 2 * (e % 2) + ch, x_, :], start=(ch == 0), stop=(ch == 1), skip_group_check=True)
                last.then_inc(sem["w2_0_done"], 1)

            def inproj(b):
                x3 = ln_o[:, 3, :]
                pe.wait_ge(sem["lnB_out"], nth("lnB_out", b, 1))
                for x_ in range(2):
                    mm(G[:, x_, 0:HALF], w("w_inx", half(x_)), x3[half(x_), :], start=True, stop=True)
                    last = mm(G[:, x_, HALF:S], w("w_inz", half(x_)), x3[half(x_), :], start=True, stop=True)
                last.then_inc(sem["in_done"], 1)

            def xproj(b):
                pe.wait_ge(sem["sz_ready"], nth("sz_ready", b))
                pe.wait_ge(sem["u_ready"], nth("u_ready", b))
                mm(G[0:DTR, 0, :], w("w_xdt"), u[:, :], start=True, stop=True)
                mm(G[:, 1, :], w("w_xb"), u[:, :], start=True, stop=True)
                mm(G[:, 2, :], w("w_xc"), u[:, :], start=True, stop=True).then_inc(sem["xp_done"], 1)

            def dtproj(b):
                pe.wait_ge(sem["dtl_ready"], nth("dtl_ready", b))
                mm(G[:, 0, :], w("w_dt", slice(0, DTR)), dtl[:, :], start=True, stop=True).then_inc(sem["dtp_done"], 1)

            def ysum(b, r):
                pe.wait_ge(sem["hc_ready"], nth("hc_ready", b, 4 * r + 4))
                for s in range(4):
                    last = mm(G[32 * s:32 * s + 32, 2, :], sel_y[:, r, :], hc[:, s, :], start=(r == 0), stop=(r == 3))
                last.then_inc(sem["y_sum"], 1)

            def grp(b, k):
                if k < GROUPS:
                    s, r = k % 4, k // 4
                    if k == 0:
                        pe.wait_ge(sem["br_ready"], nth("br_ready", b))
                        pe.wait_ge(sem["cr_ready"], nth("cr_ready", b))
                        pe.wait_ge(sem["sp_relu"], nth("sp_relu", b))
                        pe.wait_ge(sem["dstack_in"], nth("dstack_in", b))
                    else:
                        pe.wait_ge(sem["da_ready"], nth("da_ready", b, k))
                        pe.wait_ge(sem["dbu_ready"], nth("dbu_ready", b, k))
                    mm(G[:, 0, :], sel_dn[:, s, :], T[:, 0, S * r:S * r + S], start=True, stop=True)
                    mm(G[:, 1, :], sel_dn[:, s, :], T[:, 1, S * r:S * r + S], start=True, stop=True).then_inc(sem["spread"], 1)
                    if k >= 5 and k % 4 == 1:
                        ysum(b, (k - 5) // 4)
                else:
                    ysum(b, 3)

            def yout(b):
                pe.wait_ge(sem["y2"], nth("y2", b))
                for x_ in range(2):
                    last = mm(G[half(x_), 0, 0:HALF], w("w_out"), sp[:, 5, HALF * x_:HALF * x_ + HALF], start=True, stop=True)
                last.then_inc(sem["out_done"], 1)

            def fc1(b):
                pe.wait_ge(sem["yln"], nth("yln", b))
                for ch in range(2):
                    for x_ in range(2):
                        last = mm(G[:, x_, HALF * ch:HALF * ch + HALF], w("fc1", half(x_), (128 * ch, 128 * ch + 128)), yl[half(x_), :], start=True, stop=True)
                last.then_inc(sem["fc1_done"], 1)

            def fc2(b):
                pe.wait_ge(sem["fc1_act"], nth("fc1_act", b))
                for ch in range(2):
                    for x_ in range(2):
                        last = mm(G[half(x_), 2, 0:HALF], w("fc2", cols=(64 * ch, 64 * ch + 64)), hidb[:, ch, x_, :], start=(ch == 0), stop=(ch == 1))
                last.then_inc(sem["fc2_done"], 1)

            def exp(b, i):
                if i < E // 2:
                    if i == 0:
                        pe.wait_ge(sem["mbc1_in"], nth("mbc1_in", b))
                    else:
                        pe.wait_ge(sem["gelu1"], nth("gelu1", b, 2 * i))
                    for n in range(2):
                        e = 2 * i + n
                        for x_ in range(2):
                            last = mm(G[:, x_, HALF * n:HALF * n + HALF], w("w1_1", half(x_), (128 * e, 128 * e + 128)), x6[half(x_), :], start=True, stop=True)
                    last.then_inc(sem["hid1_done"], 1)
                i = i - 1
                if i < 0:
                    return
                pe.wait_ge(sem["gelu1"], nth("gelu1", b, 2 * i + 2))
                if i >= 1:
                    pe.wait_ge(sem["y1e"], nth("y1e", b, 2 * i))
                for n in range(2):
                    e = 2 * i + n
                    for x_ in range(2):
                        last = mm(G[half(x_), 2, HALF * n:HALF * n + HALF], w("w2_1", cols=(64 * e, 64 * e + 64)),
                                  hidb[:, 2 * (i % 2) + n, x_, :], start=True, stop=True)
                last.then_inc(sem["w2_1_done"], 1)

            def turn(b):
                pe.wait_ge(sem["acc1"], nth("acc1", b))
                for c in range(2):
                    last = nc.tensor.transpose(G[:, 0, 128 * c:128 * c + 128], h4[:, 128 * c:128 * c + 128], ident[:, :])
                last.then_inc(sem["out_turned"], 1)

            steps = {f"ln{j}b": (ln_b(j), None) for j in range(NLN)} | {f"ln{j}c": (ln_c(j), None) for j in range(NLN)}
            steps |= {"ln0a": (ln_a(0, f0[:, :], "fuse_act"), None), "ln1a": (ln_a(1, h0[:, :], "h0_ready"), None),
                      "ln2a": (ln_a(2, h1[:, :], "h1_ready"), None), "ln3a": (ln_a(3, h2b[:, :], "h2_taken"), None),
                      "ln4a": (ln_a(4, sres[:, :], "s_ready"), None), "ln5a": (ln_a(5, s2[:, :], "s2_ready"), None),
                      "ln6a": (ln_a(6, h3[:, :], "h3_ready"), None), "ln7a": (ln_a(7, ln_o[:, 6, :], "lnB_out", 4), None),
                      "tok": (tok, None), "feat": (feat, None), "fuse": (fuse, None), "qkv": (qkv, None), "s1_": (s1_, 0),
                      "msplit": (msplit, None), "s2_": (s2_, 0), "den": (den, None), "wo": (wo, None),
                      "logit0": (logit(0, ln_o[:, 2, :], w("wr0"), F, "lnF_out", 3), None), "mask0": (mask0, None), "ffn_": (ffn, 0),
                      "inproj": (inproj, None), "xproj": (xproj, None), "dtproj": (dtproj, None), "grp_": (grp, 0), "yout": (yout, None),
                      "fc1": (fc1, None), "fc2": (fc2, None), "logit1": (logit(1, x6[:, :], w("wr1"), G, "x6_ready"), None),
                      "mask1": (mask1, None), "exp_": (exp, 0), "turn": (turn, None)}
            turns(pe, steps)


def kernel(**inputs):
    import concourse.bacc as bacc
    from concourse.bass_utils import run_bass_kernel_spmd

    p = {k: np.asarray(v) for k, v in inputs.items()}
    wts = np.zeros((128, WCOLS), np.float32)

    def put(name, a, row=0, col=0):
        a = a if a.ndim == 2 else a[:, None]
        at = AT[name][0] + col
        wts[row:row + a.shape[0], at:at + a.shape[1]] = a

    def twice(name, a, col=0):
        put(name, a, 0, col)
        put(name, a, 64, col)

    put("w_eg", p["L0_tok_w_item"]); put("w_eg", p["L0_tok_w_geo"], 64, 64)
    put("b_eg", p["L0_tok_b_item"]); put("b_eg", p["L0_tok_b_geo"], 64)
    put("w_vis", p["L0_tok_w_visit"]); put("b_vis", p["L0_tok_b_visit"])
    put("w_f1", p["L0_tok_w_fuse"][:128]); put("w_f2", p["L0_tok_w_fuse"][128:])
    twice("b_f", p["L0_tok_b_fuse"]); twice("g_t", p["L0_tok_ln_gamma"]); twice("be_t", p["L0_tok_ln_beta"])
    dh = np.arange(NH * DH).reshape(NH, DH).T.reshape(-1)
    twice("w_qk", p["L0_attn_Wq"][dh].T); twice("w_qk", p["L0_attn_Wk"][dh].T, 64)
    put("b_qk", p["L0_attn_bq"][dh]); put("b_qk", p["L0_attn_bk"][dh], 64)
    for h in range(NH):
        hs = slice(DH * h, DH * h + DH)
        twice("w_v", p["L0_attn_Wv"][hs].T, 32 * h)
        put("w_o", p["L0_attn_Wo"][:, hs].T, 32 * h)
        put("bv", np.tile(p["L0_attn_bv"][hs], (128, 1)), 0, 32 * h)
        put("bv", np.ones((128, 1), np.float32), 0, 32 * h + DH)
    twice("b_o", p["L0_attn_bo"])
    twice("wr0", p["L0_ffn_Wr"]); twice("wr1", p["L1_ffn_Wr"])
    for e in range(9):
        w1 = p["L0_ffn_W1s"] if e == 0 else p["L0_ffn_W1p"][e - 1]
        b1 = p["L0_ffn_b1s"] if e == 0 else p["L0_ffn_b1p"][e - 1]
        w2 = p["L0_ffn_W2s"] if e == 0 else p["L0_ffn_W2p"][e - 1]
        b2 = p["L0_ffn_b2s"] if e == 0 else p["L0_ffn_b2p"][e - 1]
        twice("w1_0", w1, F0 * e)
        for ch in range(2):
            put("w2_0", w2[128 * ch:128 * ch + 128], 0, 64 * (2 * e + ch))
            put("b1_0", b1[128 * ch:128 * ch + 128], 0, 2 * e + ch)
        twice("b2_0", b2, e)
    twice("w_inx", p["L1_attn_in_proj_w"][:DI].T); twice("w_inz", p["L1_attn_in_proj_w"][DI:].T)
    put("b_inx", p["L1_attn_in_proj_b"][:DI]); put("b_inz", p["L1_attn_in_proj_b"][DI:])
    put("conv_w", p["L1_attn_conv_w"]); put("conv_b", p["L1_attn_conv_b"])
    xp = p["L1_attn_x_proj_w"]
    put("w_xdt", xp[:DTR].T)
    put("w_xb", np.tile(xp[DTR:DTR + NS].T, (1, 8))); put("w_xc", np.tile(xp[DTR + NS:].T, (1, 8)))
    put("w_dt", p["L1_attn_dt_proj_w"].T); put("b_dt", p["L1_attn_dt_proj_b"])
    put("a_log", p["L1_attn_A_log"].reshape(4, 8, 4, NS).transpose(1, 3, 2, 0).reshape(128, GROUPS))
    put("d_ssm", p["L1_attn_D_ssm"]); put("w_out", p["L1_attn_out_proj_w"].T); twice("b_out", p["L1_attn_out_proj_b"])
    twice("g1", p["L1_attn_ln1_g"]); twice("be1", p["L1_attn_ln1_b"])
    twice("g2", p["L1_attn_ln2_g"]); twice("be2", p["L1_attn_ln2_b"])
    twice("fc1", p["L1_attn_fc1_w"].T)
    for ch in range(2):
        put("fc2", p["L1_attn_fc2_w"].T[128 * ch:128 * ch + 128], 0, 64 * ch)
        put("b_fc1", p["L1_attn_fc1_b"][128 * ch:128 * ch + 128], 0, ch)
    twice("b_fc2", p["L1_attn_fc2_b"])
    twice("g_m", p["L1_ffn_gamma"]); twice("be_m", p["L1_ffn_beta"])
    put("br1", np.tile(p["L1_ffn_br"], (128, NT)))
    put("iota", np.tile(np.arange(E, dtype=np.float32), (128, NT)))
    for e in range(E):
        twice("w1_1", p["L1_ffn_W1"][e], F1 * e)
        put("w2_1", p["L1_ffn_W2"][e], 0, 64 * e)
        put("b1_1", p["L1_ffn_b1"][e], 0, e)
        twice("b2_1", p["L1_ffn_b2"][e], e)
    arrays = {
        "ids": np.ascontiguousarray(p["x"].reshape(NB * NT, 128).T),
        "table": np.concatenate([p["L0_tok_emb_table"], p["L0_tok_geo_table"], p["L0_tok_visit_table"]], axis=1),
        "weights": wts,
    }
    nc = bacc.Bacc("TRN2", target_bir_lowering=False, num_devices=1)
    args = [nc.dram_tensor(f"in_{n}", a.shape, mybir.dt.from_np(a.dtype), kind="ExternalInput").ap() for n, a in arrays.items()]
    args.append(nc.dram_tensor("out_h", (NB, S, D), mybir.dt.float32, kind="ExternalOutput").ap())
    build_tower(nc, *args)
    r = run_bass_kernel_spmd(nc, [{f"in_{n}": a for n, a in arrays.items()}], core_ids=[0])
    return r.results[0]["out_h"]
```

```python
from contextlib import ExitStack

import numpy as np
import concourse.bass as bass
from concourse import mybir

NB, S, D = 8, 512, 64
HALF = S // 2
NT = S // 128
NH, DH = 4, 16
F0, E, F1 = 256, 8, 128
DI, NS, DC, DTR = 128, 16, 4, 16
VIS = 24
ROW = 2 * D + VIS
LN_EPS = 1e-5
NLN = 8
GROUPS = DI * NS // 128
N_ITEMS = 25001

EARLY = [
    ("w_eg", 128), ("w_vis", 64), ("w_f1", 64), ("w_f2", 64), ("iota", NT * E), ("br1", NT * E), ("bv", 128), ("w_o", 64),
    ("b_eg", 1), ("b_vis", 1), ("b_f", 1), ("g_t", 1), ("be_t", 1), ("b_qk", 1), ("b_o", 1),
    ("b1_0", 18), ("b2_0", 9), ("b_inx", 1), ("b_inz", 1), ("conv_w", DC), ("conv_b", 1), ("b_dt", 1),
    ("a_log", GROUPS), ("d_ssm", 1), ("b_out", 1), ("g1", 1), ("be1", 1), ("b_fc1", 2), ("b_fc2", 1),
    ("g2", 1), ("be2", 1), ("g_m", 1), ("be_m", 1), ("b1_1", E), ("b2_1", E),
]
WIDTHS = EARLY + [
    ("w_qk", 128), ("w_v", 128), ("wr0", E), ("w1_0", 9 * F0), ("w2_0", 18 * D),
    ("w_inx", 128), ("w_inz", 128), ("w_xdt", 16), ("w_xb", 128), ("w_xc", 128), ("w_dt", 128), ("w_out", 64),
    ("fc1", 256), ("fc2", 128), ("wr1", E), ("w1_1", E * F1), ("w2_1", E * D),
]
AT = {name: (sum(w for _, w in WIDTHS[:n]), width) for n, (name, width) in enumerate(WIDTHS)}
WCOLS = sum(w for _, w in WIDTHS)
WEARLY = sum(w for _, w in EARLY)

PER = {
    "ids_clipped": 1, "valid_ready": 1, "rows_in": 16 * NT, "tok_transposed": 1, "eg_ready": 1, "vis_ready": 1,
    "emb_turned": 1, "ev_ready": 1, "feat_done": 2, "cat_ready": 2, "fuse_done": 1, "fuse_act": 1, 
    "tok_affine": 1, "tok_masked": 1, "h0_ready": 1,
    "lnA_centred": 2, "lnA_squared": 2, "lnA_kept": 2, "lnA_var": 2, "lnA_vareps": 2, "lnA_rstd": 2, "lnA_bc": 2, "lnA_out": 2,
    "lnB_centred": 2, "lnB_squared": 2, "lnB_kept": 2, "lnB_var": 2, "lnB_vareps": 2, "lnB_rstd": 2, "lnB_bc": 2, "lnB_out": 2,
    "lnC_centred": 4, "lnC_squared": 4, "lnC_kept": 4, "lnC_var": 4, "lnC_vareps": 4, "lnC_rstd": 4, "lnC_bc": 4, "lnC_out": 4,
    "qk_done": 1, "v_done": 1, "qk_full": 1, "qk_hi": 1, "qk_r": 1, "qk_mid": 1, "qk_lo": 1, "v_ready": 1,
    "parts_out": 32, "stack_in": 96, "s1_done": 16, "max_done": 16, "max_split": 5, "max_turned": 1, "max_in": 1,
    "s2_done": 16, "exp_done": 16, "pv_done": NT, "o_ready": 1, "den_done": 1, "rec_ready": 1, "o_bf": 1,
    "wo_done": 1, "h1_ready": 1,
    "lg0_done": 1, "lg0_in": 1, "top0": NT, "idx0": NT, "r0": 9, "e0": 1, "mask0": 1, "mp0": 5, "mt0_done": 1, "mt0_in": 1, "mbc0_done": 2, "mbc0_in": 2,
    "lg1_done": 1, "lg1_in": 1, "top1": NT, "idx1": NT, "r1": 9, "e1": 1, "mask1": 1, "mp1": 5, "mt1_done": 1, "mt1_in": 1, "mbc1_done": 2, "mbc1_in": 2,
    "hid0_done": 18, "gelu0": 18, "w2_0_done": 9, "y0": 9, "acc0": 8,
    "h2_taken": 1,
    "in_done": 1, "xi_ready": 1, "sz_ready": 1, "conv": 4, "u_ready": 1, "xp_done": 1, "dtl_ready": 1, "br_ready": 1,
    "cr_ready": 1, "dtp_done": 1, "sp_abs": 1, "sp_exp": 1, "sp_relu": 1, "sp_u1": 1, "sp_ln": 1, "sp_r": 1, "sp_t": 1,
    "dt_ready": 1, "dx_ready": 1, "d_hi": 2, "d_r": 2, "d_mid": 2, "d_lo": 2, "dparts_out": 16, "dstack_in": 16,
    "spread": GROUPS, "da_ready": GROUPS, "dbu_ready": GROUPS, "scanned": GROUPS,
    "hc_ready": GROUPS, "y_sum": 4, "y1": 1, "y2": 1, "out_done": 1, "s_ready": 1, "yln": 1,
    "fc1_done": 1, "fc1_act": 2, "fc2_done": 1, "ff_ready": 1, "s2_ready": 1, "yy": 1, "h3_ready": 1, "x6_ready": 1,
    "hid1_done": E, "gelu1": E, "w2_1_done": E // 2, "y1e": E, "acc1": E, "out_turned": 1, "out_ready": 1, "stored": 32,
}

STAGES = (
    ["gather", "tok", "feat", "fuse", "ln0a", "ln0b", "ln0c", "ln1a", "ln1b", "ln1c", "qkv", "split"]
    + [f"s1_{n}" for n in range(8)] + ["msplit"] + [f"s2_{n}" for n in range(8)] + ["den", "wo"],
    ["ln2a", "ln2b", "ln2c", "logit0", "router0", "mask0"] + [f"ffn_{e}" for e in range(10)]
    + ["ln3a", "ln3b", "ln3c", "inproj", "conv", "xproj", "dtproj", "softplus", "dsplit"],
    ["take"] + [f"grp_{k}" for k in range(GROUPS + 1)] + ["yout", "ln4a", "ln4b", "ln4c", "fc1", "fc2", "ln5a", "ln5b", "ln5c"]
    + ["ln6a", "ln6b", "ln6c", "ln7a", "ln7b", "ln7c", "logit1", "router1", "mask1"] + [f"exp_{i}" for i in range(E // 2 + 1)] + ["turn"])
ORDER = {
    "SP": ("AABBC"),
    "Pool": ("CACACBCCCCCBCCCBACCBCCACCCBBBCBBCBBBCBCCCCCCCCCCCCCCC"),
    "Activation": ("BCCCCCCACCAAACACBCBCBCBCBBACCBCBBBAABABBBBBBCBABBBBCBBCBBBBCBBACBABAAAAAACAABBAABACBACABACAABBAABAAB"
           "ACBBCCCC"),
    "DVE": ("ACCCCCBCCCCACCBCCCBACCBBBBBBBCBBBBBBBBCCCCACCCCACCAAACACACACCBACBAABACCCBBAACAAACABCAAAAAAACAABABAAA"
           "CAAAAAAAAACBACCBCBCBBCCBBCCBBCCCCCCCCCCCBCCCCBBBBCBBBCBBBACCACCCCACCCCCAC"),
    "PE": ("BCCBCCACBCCACCABAACACCABCBCBACBCBCCAABBCABABBBCBBBCBBACBABCABBAACBABCABAACBABABCAABACABABBCABACBACAB"
           "ACABCABACCAACBABCCAACAAACAAAAACCACCCCCACC"),
}


def build_tower(nc: bass.Bass, ids: bass.AP, table: bass.AP, weights: bass.AP, out: bass.AP):
    fp32, bf16 = mybir.dt.float32, mybir.dt.bfloat16
    i32, u32 = mybir.dt.int32, mybir.dt.uint32
    ALU, ACT, AX = mybir.AluOpType, mybir.ActivationFunctionType, mybir.AxisListType

    qk_scr = nc.dram_tensor("qk_scr", (2, 3, 64, S), bf16, kind="Internal").ap()
    d_scr = nc.dram_tensor("d_scr", (2, 3, 128, S), bf16, kind="Internal").ap()

    ctx = ExitStack()
    with ctx:
        def sb(name, shape, dt=fp32):
            return ctx.enter_context(nc.sbuf_tensor(name, shape, dt))

        wts = sb("wts", [128, WCOLS])

        def w(name, rows=slice(0, 128), cols=None):
            at, width = AT[name]
            lo, hi = cols if cols else (0, width)
            return wts[rows, at + lo:at + hi]

        ident = sb("ident", [128, 128])
        identb = sb("identb", [128, 128], bf16)
        centre = sb("centre", [128, 128])
        halfmean = sb("halfmean", [128, 2])
        sel_den = sb("sel_den", [128, 128])
        sel_dn = sb("sel_dn", [128, 4, 128], bf16)
        sel_y = sb("sel_y", [128, 4, 32])
        sel_m = sb("sel_m", [128, NT * E, 64], bf16)
        wo3 = sb("wo3", [128, 3, 64], bf16)
        wo_r = sb("wo_r", [128, 2, 64])
        neg_half = sb("neg_half", [128, 4])
        e_base = sb("e_base", [128, 4])
        a_neg = sb("a_neg", [128, GROUPS])
        a_exp = sb("a_exp", [128, GROUPS])
        gate = sb("gate", [128, 4])
        gpool = sb("gpool", [128, 4])
        zero = sb("zero", [128, HALF])
        ids_all = sb("ids_all", [128, NB * NT], i32)

        ids_c = sb("ids_c", [128, NT], i32)
        valid = sb("valid", [128, NT])
        rows = sb("rows", [128, NT, ROW])
        vis = sb("vis", [128, S])
        ev = sb("ev", [128, 2, HALF])
        cat1 = sb("cat1", [128, S])
        eg = cat1
        cat2 = sb("cat2", [128, S])
        f0 = sb("f0", [128, HALF])
        h0, h1, h2, h2b, h3, h4 = (sb(f"h{i}", [128, HALF]) for i in ("0", "1", "2", "2b", "3", "4"))
        ln_sq = sb("ln_sq", [128, 3, HALF])
        tok_a, tok_m = f0, ln_sq[:, 0, :]
        ln_xc = sb("ln_xc", [128, 3, HALF])
        ln_ve = sb("ln_ve", [128, 3, NT])
        ln_rs = sb("ln_rs", [128, 3, NT])
        lno = sb("lno", [128, 5, HALF])
        ln_o = {j: lno[:, max(j - 3, 0), :] for j in (0, 4, 5, 6, 7)}
        xz = sb("xz", [128, 5, 2, HALF])
        x1z, x2z, x3z, ylz, x6z = (xz[:, i, :, :] for i in range(5))
        qkf = sb("qkf", [128, S])
        qkr = sb("qkr", [128, S])
        part = sb("part", [128, 3, S], bf16)
        QS = sb("QS", [128, NH, S], bf16)
        KS = sb("KS", [128, NH, S], bf16)
        vsb = sb("vsb", [128, NT, 128])
        nmax = sb("nmax", [128, 4 * NH])
        nmax_r = sb("nmax_r", [128, 2, 4 * NH])
        M = sb("M", [128, 4 * NH, 32], bf16)
        P = sb("P", [128, 8, S])
        osb, rec = qkr, qkf
        obf = sb("obf", [128, S], bf16)
        lg = sb("lg", [128, 2, NT, E])
        top = sb("top", [128, 2, NT, 8])
        idx = sb("idx", [128, 2, NT, 8], u32)
        idxf = sb("idxf", [128, 2, NT, 2])
        eq = sb("eq", [128, 2, 2, NT, E])
        dlt = sb("dlt", [128, 2, NT])
        ex2 = sb("ex2", [128, 2, NT])
        ssum = sb("ssum", [128, 2, NT])
        w12 = sb("w12", [128, 2, 2, NT])
        mk = sb("mk", [128, 2, 3, NT * E])
        mk_r = sb("mk_r", [128, 2, 2, NT * E])
        mk3 = sb("mk3", [128, 2, 3, NT * E], bf16)
        mt = sb("mt", [128, 2, 128], bf16)
        mbc = sb("mbc", [128, 2, E, HALF])
        hid = sb("hid", [128, 2, 2, S])
        ye = sb("ye", [128, 2, HALF])
        acc = sb("acc", [128, 2, HALF])
        yeb = sb("yeb", [128, 2, HALF])
        accb = sb("accb", [128, 2, HALF])
        xip = sb("xip", [128, DC - 1 + S])
        sz = sb("sz", [128, S])
        cv = sb("cv", [128, 2, S])
        u = sb("u", [128, S])
        dtl = sb("dtl", [128, S])
        Br = sb("Br", [128, S])
        Cr = sb("Cr", [128, S])
        sp = sb("sp", [128, 2, S])
        dd = sb("dd", [128, 2, S])
        dd_r = cv
        dp = sb("dp", [128, 2, 3, S], bf16)
        T = sb("T", [128, 2, 4 * S], bf16)
        dA = sb("dA", [128, 2, S])
        dBu = sb("dBu", [128, 2, S])
        hst = sb("hst", [128, 2, S])
        hc = sb("hc", [128, 4, S])
        hidb = hc[:, :, :].rearrange("p (i n) c -> p i n c", n=2)
        y1, y2 = dBu[:, 0, :], dBu[:, 1, :]
        sres, ff, s2, yy = (dA[:, i // 2, HALF * (i % 2):HALF * (i % 2) + HALF] for i in range(4))
        outs = sb("outs", [128, 2, 128])

        pA, pB, pC = (ctx.enter_context(nc.psum_tensor(f"p{c}", [128, k, 512], fp32)) for c, k in (("A", 2), ("B", 3), ("C", 3)))
        turned = pA[:, 0:2, :].bitcast(bf16).rearrange("p k (i q) -> p (k i) q", q=S)

        sem = {name: ctx.enter_context(nc.semaphore(name)) for name in PER}
        s_w = ctx.enter_context(nc.semaphore("weights_in"))
        s_wr = ctx.enter_context(nc.semaphore("rest_of_weights_in"))
        s_ids = ctx.enter_context(nc.semaphore("ids_in"))
        s_c = ctx.enter_context(nc.semaphore("consts_pool"))
        s_v = ctx.enter_context(nc.semaphore("consts_dve"))
        s_ae = ctx.enter_context(nc.semaphore("a_exp_ready"))
        made = {}
        block = ctx.enter_context(nc.Block())

        def nth(name, b, k=None):
            return PER[name] * b + (PER[name] if k is None else k)

        def not_first(b):
            return not (isinstance(b, int) and b == 0)

        def turns(eng, name, steps):
            def pieces(stage, row):
                for step in STAGES[stage]:
                    kind, _, n = step.partition("_")
                    if kind in steps:
                        yield from (steps[kind](row, int(n)) if n else steps[kind](row)) or ()
                        yield

            def turn(*row_of):
                stages = [pieces(stage, row) for stage, row in enumerate(row_of)]
                for c in ORDER[name]:
                    if row_of["ABC".index(c)] is not None:
                        next(stages["ABC".index(c)])
            turn(0, None, None)
            turn(1, 0, None)
            with eng.Fori(2, NB) as b:
                turn(b, b - 1, b - 2)
            turn(None, NB - 1, NB - 2)
            turn(None, None, NB - 1)

        def half(x):
            return slice(64 * x, 64 * x + 64)

        def ln_of(j):
            return (("lnA", j, pA[:, 1, :], 0) if j < 2 else ("lnB", j - 2, pB[:, 2, :], 1) if j < 4 else
                    ("lnC", j - 4, pC[:, 2, :], 2))

        @block.sync
        def _(sp_):
            sp_.dma_start(ids_all[:, :], ids).then_inc(s_ids, 16)
            sp_.dma_start(wts[:, 0:WEARLY], weights[:, 0:WEARLY]).then_inc(s_w, 16)
            sp_.wait_ge(sem["rows_in"], nth("rows_in", 0))
            sp_.dma_start(wts[:, WEARLY:], weights[:, WEARLY:]).then_inc(s_wr, 16)

            def split(b):
                sp_.wait_ge(sem["qk_lo"], nth("qk_lo", b))
                for i in range(2):
                    sp_.dma_start(qk_scr[i].rearrange("p r c -> r p c"), part[64 * i:64 * i + 64, :, :]).then_inc(sem["parts_out"], 16)
                yield
                sp_.wait_ge(sem["parts_out"], nth("parts_out", b))
                flat = qk_scr.rearrange("i p (d h) c -> i p d (h c)", h=NH)
                qrow = flat[0].rearrange("p d n -> (p d) n")
                for lo, hi in ((0, 48), (48, 80), (80, 96)):
                    sp_.dma_start(QS[lo:hi, :, :].rearrange("p h c -> p (h c)"), qrow[0:hi - lo]).then_inc(sem["stack_in"], 16)
                for lo, p, times in ((0, 0, 3), (48, 1, 2), (80, 2, 1)):
                    src = flat[1, p:p + 1].to_broadcast([times, DH, NH * S]) if times > 1 else flat[1, p]
                    sp_.dma_start(KS[lo:lo + DH * times, :, :].rearrange("p h c -> p (h c)"), src).then_inc(sem["stack_in"], 16)

            def dsplit(b):
                sp_.wait_ge(sem["d_lo"], nth("d_lo", b))
                sp_.dma_start(d_scr.rearrange("i p r c -> r (i p) c"), dp[:, :, :, :].rearrange("r i p c -> r (i p) c")).then_inc(sem["dparts_out"], 16)
                yield
                sp_.wait_ge(sem["dparts_out"], nth("dparts_out", b))
                sp_.dma_start(T[0:96, :, :], d_scr.rearrange("i p (j r) c -> (p j) i (r c)", r=4)).then_inc(sem["dstack_in"], 16)

            def store(b):
                sp_.wait_ge(sem["out_ready"], nth("out_ready", b))
                bs = bass.ds(b, 1) if not isinstance(b, int) else slice(b, b + 1)
                for c in range(2):
                    dst = out[bs, :, :].rearrange("o (x c p) d -> c p (o x) d", x=2, c=2)[c]
                    sp_.dma_start(dst, outs[:, c, :].rearrange("p (x d) -> p x d", x=2)).then_inc(sem["stored"], 16)

            turns(sp_, "SP", {"split": split, "dsplit": dsplit, "turn": store})
            sp_.wait_ge(sem["stored"], 32 * NB)

        @block.gpsimd
        def _(g):
            cnt = [0]

            def link(ins):
                cnt[0] += 1
                ins.then_inc(s_c, 1)
                g.wait_ge(s_c, cnt[0])

            def select(t, fill, base, pattern, mult):
                link(g.affine_select(out=t, in_=t, compare_op=ALU.not_equal, fill=fill, base=base,
                                     pattern=pattern, channel_multiplier=mult))

            link(g.memset(neg_half[:, :], -0.5))

            link(g.memset(ident[:, :], 0.0))
            select(ident[:, :], 1.0, 0, [[-1, 128]], 1)
            link(g.memset(centre[:, :], 0.0))
            for x in range(2):
                link(g.memset(centre[half(x), half(x)], -1.0 / D))
            select(centre[:, :], 1.0 - 1.0 / D, 0, [[-1, 128]], 1)
            link(g.memset(halfmean[:, :], 0.0))
            for x in range(2):
                link(g.memset(halfmean[half(x), x:x + 1], 1.0 / D))
            made["early"] = cnt[0]

            def constants():
                link(g.memset(sel_den[:, :], 0.0))
                v = sel_den[:, :].rearrange("p (h i) -> p h i", i=32)
                select(v, 1.0, -16, [[-32, 4], [0, 32]], 1)
                link(g.memset(sel_dn[:, :, :], 0.0))
                link(g.memset(sel_m[:, :, :], 0.0))
                for p in range(3):
                    q = slice(32 * p, 32 * p + 32)
                    v = sel_dn[q, :, :].rearrange("p s (j n) -> p s j n", n=NS)
                    select(v, 1.0, 0, [[-8, 4], [-1, 8], [0, NS]], 1)
                    select(sel_m[q, :, :], 1.0, 0, [[-1, NT * E], [0, 64]], 1)
                link(g.memset(zero[:, :], 0.0))
                link(g.memset(e_base[:, :], float(np.e)))
                made["pool"] = cnt[0]

            def rstd(j):
                def fn(b):
                    side, i, _, n = ln_of(j)
                    g.wait_ge(sem[side + "_vareps"], nth(side + "_vareps", b, i + 1))
                    g.tensor_tensor(ln_rs[:, n, :], ln_ve[:, n, :], neg_half[:, :], ALU.pow).then_inc(sem[side + "_rstd"], 1)
                return fn

            def gather(b):
                if not_first(b):
                    g.wait_ge(sem["emb_turned"], nth("emb_turned", b, 0))
                g.wait_ge(sem["ids_clipped"], nth("ids_clipped", b))
                g.tensor_tensor(gpool[:, :], neg_half[:, :], neg_half[:, :], ALU.add)
                for t in range(NT):
                    g.indirect_dma_start(rows[:, t, :], None, table[:, :], bass.IndirectOffsetOnAxis(ap=ids_c[:, t:t + 1], axis=0)).then_inc(sem["rows_in"], 16)
                yield
                if not not_first(b):
                    g.wait_ge(sem["rows_in"], nth("rows_in", b))
                    constants()

            def router(n):
                def fn(b):
                    g.wait_ge(sem[f"r{n}"], nth(f"r{n}", b, 1))
                    g.tensor_tensor(ex2[:, n, :], e_base[:, :], dlt[:, n, :], ALU.pow).then_inc(sem[f"e{n}"], 1)
                return fn

            def ffn(b, e):
                i = e - 2
                if i < 0:
                    return
                g.wait_ge(sem["y0"], nth("y0", b, i + 2))
                if i:
                    g.wait_ge(sem["acc0"], nth("acc0", b, i))
                if i == 7 and not_first(b):
                    g.wait_ge(sem["h2_taken"], nth("h2_taken", b, 0))
                o = h2[:, :] if i == 7 else acc[:, (i + 1) % 2, :]
                g.tensor_tensor(o, acc[:, i % 2, :], ye[:, i % 2, :], ALU.add).then_inc(sem["acc0"], 1)

            def take(b):
                g.wait_ge(sem["acc0"], nth("acc0", b))
                if not_first(b):
                    g.wait_ge(sem["h3_ready"], nth("h3_ready", b, 0))
                g.tensor_tensor(h2b[:, :], h2[:, :], zero[:, :], ALU.add).then_inc(sem["h2_taken"], 1)

            def grp(b, k):
                if k == GROUPS:
                    return
                g.wait_ge(sem["scanned"], nth("scanned", b, k + 1))
                if k == 0:
                    g.wait_ge(sem["cr_ready"], nth("cr_ready", b))
                if k >= 4:
                    g.wait_ge(sem["y_sum"], nth("y_sum", b, k // 4))
                g.tensor_tensor(hc[:, k % 4, :], hst[:, k % 2, :], Cr[:, :], ALU.mult).then_inc(sem["hc_ready"], 1)

            def exp(b, i):
                for e in range(2 * i - 2, 2 * i):
                    if e < 0:
                        continue
                    yield
                    g.wait_ge(sem["y1e"], nth("y1e", b, e + 1))
                    if e:
                        g.wait_ge(sem["acc1"], nth("acc1", b, e))
                    o = h4[:, :] if e == 7 else accb[:, (e + 1) % 2, :]
                    a = h3[:, :] if e == 0 else accb[:, e % 2, :]
                    g.tensor_tensor(o, a, yeb[:, e % 2, :], ALU.add).then_inc(sem["acc1"], 1)

            steps = {f"ln{j}b": rstd(j) for j in range(NLN)}
            steps |= {"gather": gather, "router0": router(0), "router1": router(1), "ffn": ffn,
                      "take": take, "grp": grp, "exp": exp}
            turns(g, "Pool", steps)

        @block.scalar
        def _(a):
            act = nc.scalar.activation
            a.wait_ge(s_w, 16)
            act(a_exp[:, :], w("a_log"), ACT.Exp).then_inc(s_ae, 1)

            def ln(j):
                def fn(b):
                    side, i, bank, n = ln_of(j)
                    a.wait_ge(sem[side + "_centred"], nth(side + "_centred", b, i + 1))
                    act(ln_xc[:, n, :], bank[:, 0:HALF], ACT.Copy).then_inc(sem[side + "_kept"], 1)
                    act(ln_sq[:, n, :], bank[:, 0:HALF], ACT.Square).then_inc(sem[side + "_squared"], 1)
                return fn

            def tok(b):
                a.wait_ge(sem["tok_transposed"], nth("tok_transposed", b))
                act(eg[:, :], pA[:, 0, :], ACT.Copy).then_inc(sem["eg_ready"], 1)

            def feat(b):
                a.wait_ge(sem["feat_done"], nth("feat_done", b, 1))
                act(cat1[:, :], pA[:, 1, :], ACT.Gelu, bias=w("b_eg")).then_inc(sem["cat_ready"], 1)
                yield
                a.wait_ge(sem["feat_done"], nth("feat_done", b, 2))
                act(cat2[0:64, :], pA[0:64, 0, :], ACT.Gelu, bias=w("b_vis", slice(0, 64))).then_inc(sem["cat_ready"], 1)

            def fuse(b):
                a.wait_ge(sem["fuse_done"], nth("fuse_done", b))
                act(f0[:, :], pA[:, 1, 0:HALF], ACT.Gelu, bias=w("b_f")).then_inc(sem["fuse_act"], 1)

            def qkv(b):
                a.wait_ge(sem["qk_done"], nth("qk_done", b))
                act(qkf[:, :], pA[:, 0, :], ACT.Identity, bias=w("b_qk")).then_inc(sem["qk_full"], 1)

            def split(b):
                if not_first(b):
                    a.wait_ge(sem["parts_out"], nth("parts_out", b, 0))
                a.wait_ge(sem["qk_full"], nth("qk_full", b))
                act(part[:, 0, :], qkf[:, :], ACT.Copy).then_inc(sem["qk_hi"], 1)
                yield
                a.wait_ge(sem["qk_r"], nth("qk_r", b))
                act(part[:, 1, :], qkr[:, :], ACT.Copy).then_inc(sem["qk_mid"], 1)

            def s2_(b, n):
                for k in (2 * n, 2 * n + 1):
                    yield
                    a.wait_ge(sem["s2_done"], nth("s2_done", b, k + 1))
                    if k >= 8:
                        a.wait_ge(sem["pv_done"], nth("pv_done", b, k // 4 - 1))
                    act(P[:, k % 8, :], pA[:, 0, :], ACT.Exp, scale=DH ** -0.5).then_inc(sem["exp_done"], 1)

            def mask0(b):
                a.wait_ge(sem["mt0_done"], nth("mt0_done", b))
                act(mt[0:96, 0, :], pB[0:96, 2, 0:64].bitcast(bf16), ACT.Copy).then_inc(sem["mt0_in"], 1)
                for i in range(2):
                    yield
                    a.wait_ge(sem["mbc0_done"], nth("mbc0_done", b, i + 1))
                    act(mbc[:, 0, 4 * i:4 * i + 4, :], pB[:, 0:2, :].rearrange("p k (i c) -> p (k i) c", i=2), ACT.Copy).then_inc(sem["mbc0_in"], 1)

            def mask1(b):
                a.wait_ge(sem["mt1_done"], nth("mt1_done", b))
                act(mt[0:96, 1, :], pC[0:96, 2, 0:64].bitcast(bf16), ACT.Copy).then_inc(sem["mt1_in"], 1)
                for i in range(2):
                    yield
                    a.wait_ge(sem["mbc1_done"], nth("mbc1_done", b, i + 1))
                    act(mbc[:, 1, 4 * i:4 * i + 4, :], pC[:, 0:2, :].rearrange("p k (i c) -> p (k i) c", i=2), ACT.Copy).then_inc(sem["mbc1_in"], 1)

            def ffn(b, e):
                if e == 9:
                    return
                for ch in range(2):
                    yield
                    a.wait_ge(sem["hid0_done"], nth("hid0_done", b, 2 * e + ch + 1))
                    if e >= 2 and ch == 0:
                        a.wait_ge(sem["w2_0_done"], nth("w2_0_done", b, e - 1))
                    act(hid[:, e % 2, ch, :], pB[:, ch, :], ACT.Gelu, bias=w("b1_0", cols=(2 * e + ch, 2 * e + ch + 1))).then_inc(sem["gelu0"], 1)

            def inproj(b):
                a.wait_ge(sem["in_done"], nth("in_done", b))
                act(xip[:, DC - 1:], pB[:, 0, :], ACT.Identity, bias=w("b_inx")).then_inc(sem["xi_ready"], 1)
                act(sz[:, :], pB[:, 1, :], ACT.Silu, bias=w("b_inz")).then_inc(sem["sz_ready"], 1)

            def conv(b):
                a.wait_ge(sem["conv"], nth("conv", b))
                act(u[:, :], cv[:, 1, :], ACT.Silu, bias=w("conv_b")).then_inc(sem["u_ready"], 1)

            def xproj(b):
                a.wait_ge(sem["xp_done"], nth("xp_done", b))
                act(dtl[0:DTR, :], pB[0:DTR, 0, :], ACT.Copy).then_inc(sem["dtl_ready"], 1)
                act(Br[:, :], pB[:, 1, :], ACT.Copy).then_inc(sem["br_ready"], 1)

            def softplus(b):
                a.wait_ge(sem["dtp_done"], nth("dtp_done", b))
                act(cv[:, 1, :], pB[:, 0, :], ACT.Abs, bias=w("b_dt")).then_inc(sem["sp_abs"], 1)
                act(sp[:, 0, :], pB[:, 0, :], ACT.Relu, bias=w("b_dt")).then_inc(sem["sp_relu"], 1)
                yield
                a.wait_ge(sem["sp_abs"], nth("sp_abs", b))
                act(sp[:, 1, :], cv[:, 1, :], ACT.Exp, scale=-1.0).then_inc(sem["sp_exp"], 1)
                yield
                a.wait_ge(sem["sp_u1"], nth("sp_u1", b))
                act(dd[:, 1, :], cv[:, 1, :], ACT.Ln).then_inc(sem["sp_ln"], 1)

            def dsplit(b):
                for i, ready in ((0, "dt_ready"), (1, "dx_ready")):
                    yield
                    a.wait_ge(sem[ready], nth(ready, b))
                    act(dp[:, i, 0, :], dd[:, i, :], ACT.Copy).then_inc(sem["d_hi"], 1)
                for i in range(2):
                    yield
                    a.wait_ge(sem["d_r"], nth("d_r", b, i + 1))
                    act(dp[:, i, 1, :], dd_r[:, i, :], ACT.Copy).then_inc(sem["d_mid"], 1)

            def grp(b, k):
                if k == GROUPS:
                    return
                a.wait_ge(sem["spread"], nth("spread", b, k + 1))
                if k >= 2:
                    a.wait_ge(sem["scanned"], nth("scanned", b, k - 1))
                act(dA[:, k % 2, :], pC[:, 0, :], ACT.Exp, scale=a_neg[:, k:k + 1]).then_inc(sem["da_ready"], 1)

            def fc1(b):
                a.wait_ge(sem["fc1_done"], nth("fc1_done", b))
                for ch in range(2):
                    act(hidb[:, 0, ch, :], pC[:, ch, :], ACT.Gelu, bias=w("b_fc1", cols=(ch, ch + 1))).then_inc(sem["fc1_act"], 1)

            def fc2(b):
                a.wait_ge(sem["fc2_done"], nth("fc2_done", b))
                act(ff[:, :], pC[:, 2, 0:HALF], ACT.Gelu, bias=w("b_fc2")).then_inc(sem["ff_ready"], 1)

            def exp(b, i):
                if i == E // 2:
                    return
                for n in range(2):
                    e = 2 * i + n
                    a.wait_ge(sem["hid1_done"], nth("hid1_done", b, e + 1))
                    if i >= 2 and n == 0:
                        a.wait_ge(sem["w2_1_done"], nth("w2_1_done", b, i - 1))
                    act(hidb[:, i % 2, n, :], pC[:, n, :], ACT.Gelu, bias=w("b1_1", cols=(e, e + 1))).then_inc(sem["gelu1"], 1)

            steps = {f"ln{j}a": ln(j) for j in range(NLN)}
            steps |= {"tok": tok, "feat": feat, "fuse": fuse, "qkv": qkv, "split": split,
                      "s2": s2_, "mask0": mask0, "mask1": mask1, "ffn": ffn, "inproj": inproj,
                      "conv": conv, "xproj": xproj, "softplus": softplus, "dsplit": dsplit,
                      "grp": grp, "fc1": fc1, "fc2": fc2, "exp": exp}
            turns(a, "Activation", steps)

        @block.vector
        def _(v):
            tt, ts, stt = nc.vector.tensor_tensor, nc.vector.tensor_scalar, nc.vector.scalar_tensor_tensor
            cnt = [0]

            def link(ins):
                cnt[0] += 1
                ins.then_inc(s_v, 1)
                v.wait_ge(s_v, cnt[0])

            def constants():
                link(v.memset(xz[:, :, :, :], 0.0))
                link(v.memset(M[:, :, :], 0.0))
                for t in (vis[:, :], cat2[:, :], dtl[:, :], T[96:128, :, :], mt[96:128, :, :]):
                    link(v.memset(t, 0.0))
                link(v.memset(KS[96:128, :, :], 1.0))
                link(v.memset(xip[:, 0:DC - 1], 0.0))
                v.wait_ge(s_c, made["early"])
                link(v.tensor_copy(identb[:, :], ident[:, :]))
                v.wait_ge(s_w, 16)
                link(v.tensor_copy(wo3[:, 0, :], w("w_o")))
                link(tt(wo_r[:, 0, :], w("w_o"), wo3[:, 0, :], ALU.subtract))
                link(v.tensor_copy(wo3[:, 1, :], wo_r[:, 0, :]))
                link(tt(wo_r[:, 1, :], wo_r[:, 0, :], wo3[:, 1, :], ALU.subtract))
                link(v.tensor_copy(wo3[:, 2, :], wo_r[:, 1, :]))
                link(v.memset(sel_y[:, :, :], 0.0))
                for r in range(4):
                    link(v.tensor_reduce(sel_y[:, r, r::4], ident[:, :].rearrange("p (j n) -> p j n", n=NS), AX.X, ALU.add))
                v.wait_ge(s_ae, 1)
                link(ts(a_neg[:, :], a_exp[:, :], -1.0, None, ALU.mult))
                made["dve"] = cnt[0]

            v.wait_ge(s_ids, 16)

            def ln_b(j):
                def fn(b):
                    side, i, bank, n = ln_of(j)
                    v.wait_ge(sem[side + "_var"], nth(side + "_var", b, i + 1))
                    ts(ln_ve[:, n, :], bank[:, HALF:HALF + NT], LN_EPS, None, ALU.add).then_inc(sem[side + "_vareps"], 1)
                return fn

            def ln_c(j):
                def fn(b):
                    side, i, bank, n = ln_of(j)
                    v.wait_ge(sem[side + "_bc"], nth(side + "_bc", b, i + 1))
                    v.wait_ge(sem[side + "_kept"], nth(side + "_kept", b, i + 1))
                    if j == 3 and not_first(b):
                        v.wait_ge(sem["s_ready"], nth("s_ready", b, 0))
                    if j in (1, 2, 3):
                        for x_ in range(2):
                            last = tt(xz[half(x_), j - 1, x_, :], bank[half(x_), HALF:S], ln_xc[half(x_), n, :], ALU.mult)
                    else:
                        last = tt(ln_o[j], bank[:, HALF:S], ln_xc[:, n, :], ALU.mult)
                    last.then_inc(sem[side + "_out"], 1)
                    after = {0: tok_out, 4: ln4_out, 5: ln5_out, 7: ln7_out}.get(j)
                    yield
                    if after:
                        v.wait_ge(sem[side + "_out"], nth(side + "_out", b, i + 1))
                        yield from after(b) or ()
                return fn

            def gather(b):
                src = ids_all[:, bass.ds(b * NT, NT)] if not isinstance(b, int) else ids_all[:, b * NT:b * NT + NT]
                if not_first(b):
                    v.wait_ge(sem["rows_in"], nth("rows_in", b, 0))
                    v.wait_ge(sem["emb_turned"], nth("emb_turned", b, 0))
                ts(ids_c[:, :], src, 0, N_ITEMS - 1, ALU.max, ALU.min).then_inc(sem["ids_clipped"], 1)
                ts(valid[:, :], src, 0, None, ALU.not_equal).then_inc(sem["valid_ready"], 1)
                if not not_first(b):
                    constants()

            def tok(b):
                v.wait_ge(sem["tok_transposed"], nth("tok_transposed", b))
                v.tensor_copy(vis[0:VIS, :], pA[0:VIS, 1, :]).then_inc(sem["vis_ready"], 1)

            def feat(b):
                v.wait_ge(sem["emb_turned"], nth("emb_turned", b))
                v.tensor_copy(ev[:, :, :], pA[:, 0, :].rearrange("p (i c) -> p i c", i=2)).then_inc(sem["ev_ready"], 1)

            def tok_out(b):
                ts(tok_a[:, :], ln_o[0], w("g_t"), w("be_t"), ALU.mult, ALU.add).then_inc(sem["tok_affine"], 1)
                yield
                v.wait_ge(sem["ev_ready"], nth("ev_ready", b))
                v.wait_ge(sem["tok_affine"], nth("tok_affine", b))
                tt(tok_m, ev[:, 1, :], tok_a[:, :], ALU.mult).then_inc(sem["tok_masked"], 1)
                yield
                v.wait_ge(sem["tok_masked"], nth("tok_masked", b))
                stt(out=h0[:, :], in0=tok_m, scalar=0.1, in1=ev[:, 0, :], op0=ALU.mult, op1=ALU.add).then_inc(sem["h0_ready"], 1)

            def qkv(b):
                v.wait_ge(sem["v_done"], nth("v_done", b))
                tt(vsb[:, :, :], pA[:, 1, :].rearrange("p (t n) -> p t n", n=128), w("bv").unsqueeze(1).to_broadcast([128, NT, 128]), ALU.add).then_inc(sem["v_ready"], 1)

            def split(b):
                v.wait_ge(sem["qk_hi"], nth("qk_hi", b))
                tt(qkr[:, :], qkf[:, :], part[:, 0, :], ALU.subtract).then_inc(sem["qk_r"], 1)
                yield
                v.wait_ge(sem["qk_mid"], nth("qk_mid", b))
                tt(part[:, 2, :], qkr[:, :], part[:, 1, :], ALU.subtract).then_inc(sem["qk_lo"], 1)

            def s1_(b, n):
                for i in range(2):
                    yield
                    v.wait_ge(sem["s1_done"], nth("s1_done", b, 2 * n + i + 1))
                    v.tensor_reduce(nmax[:, 2 * n + i:2 * n + i + 1], pA[:, i, :], AX.X, ALU.max, negate=True).then_inc(sem["max_done"], 1)

            def msplit(b):
                v.wait_ge(sem["max_done"], nth("max_done", b))
                v.tensor_copy(M[:, :, 0], nmax[:, :]).then_inc(sem["max_split"], 1)
                yield
                v.wait_ge(sem["max_split"], nth("max_split", b, 1))
                tt(nmax_r[:, 0, :], nmax[:, :], M[:, :, 0], ALU.subtract).then_inc(sem["max_split"], 1)
                yield
                v.wait_ge(sem["max_split"], nth("max_split", b, 2))
                v.tensor_copy(M[:, :, 1], nmax_r[:, 0, :]).then_inc(sem["max_split"], 1)
                yield
                v.wait_ge(sem["max_split"], nth("max_split", b, 3))
                tt(nmax_r[:, 1, :], nmax_r[:, 0, :], M[:, :, 1], ALU.subtract).then_inc(sem["max_split"], 1)
                yield
                v.wait_ge(sem["max_split"], nth("max_split", b, 4))
                v.tensor_copy(M[:, :, 2], nmax_r[:, 1, :]).then_inc(sem["max_split"], 1)
                yield
                v.wait_ge(sem["max_turned"], nth("max_turned", b))
                v.tensor_copy(QS[96:128, :, :], turned[96:128, :, :]).then_inc(sem["max_in"], 1)

            def den(b):
                v.wait_ge(sem["pv_done"], nth("pv_done", b))
                v.tensor_copy(osb[:, :], pA[:, 1, :]).then_inc(sem["o_ready"], 1)
                yield
                v.wait_ge(sem["den_done"], nth("den_done", b))
                v.reciprocal(rec[:, :], pA[:, 0, :]).then_inc(sem["rec_ready"], 1)
                yield
                v.wait_ge(sem["rec_ready"], nth("rec_ready", b))
                tt(obf[:, :], osb[:, :], rec[:, :], ALU.mult).then_inc(sem["o_bf"], 1)

            def wo(b):
                v.wait_ge(sem["wo_done"], nth("wo_done", b))
                if not_first(b):
                    v.wait_ge(sem["y0"], nth("y0", b - 1, 1))
                stt(out=h1[:, :], in0=pA[:, 1, 0:HALF], scalar=w("b_o"), in1=h0[:, :], op0=ALU.add, op1=ALU.add).then_inc(sem["h1_ready"], 1)

            def router(n):
                bank, bias = (pB, None) if n == 0 else (pC, w("br1"))

                def fn(b):
                    v.wait_ge(sem[f"lg{n}_done"], nth(f"lg{n}_done", b))
                    lgn = lg[:, n, :, :]
                    src = bank[:, 0, 0:NT * E].rearrange("p (t e) -> p t e", e=E)
                    if bias is None:
                        v.tensor_copy(lgn, src).then_inc(sem[f"lg{n}_in"], 1)
                    else:
                        tt(lgn, src, bias.rearrange("p (t e) -> p t e", e=E), ALU.add).then_inc(sem[f"lg{n}_in"], 1)
                    yield
                    v.wait_ge(sem[f"lg{n}_in"], nth(f"lg{n}_in", b))
                    v.memset(gate[:, 2 * n:2 * n + 1], 0.0)
                    for t in range(NT):
                        v.max(top[:, n, t, :], lgn[:, t, :]).then_inc(sem[f"top{n}"], 1)
                    yield
                    v.wait_ge(sem[f"top{n}"], nth(f"top{n}", b))
                    v.memset(gate[:, 2 * n + 1:2 * n + 2], 0.0)
                    for t in range(NT):
                        v.max_index(idx[:, n, t, :], top[:, n, t, :], lgn[:, t, :]).then_inc(sem[f"idx{n}"], 1)
                    r = f"r{n}"
                    tt(dlt[:, n, :], top[:, n, :, 1], top[:, n, :, 0], ALU.subtract).then_inc(sem[r], 1)
                    yield
                    v.wait_ge(sem[f"idx{n}"], nth(f"idx{n}", b))
                    v.tensor_copy(idxf[:, n, :, :], idx[:, n, :, 0:2]).then_inc(sem[r], 1)
                    yield
                    v.wait_ge(sem[r], nth(r, b, 2))
                    iota = w("iota").rearrange("p (t e) -> p t e", e=E)
                    for i in range(2):
                        tt(eq[:, n, i, :, :], iota, idxf[:, n, :, i:i + 1].to_broadcast([128, NT, E]), ALU.is_equal).then_inc(sem[r], 1)
                    yield
                    v.wait_ge(sem[f"e{n}"], nth(f"e{n}", b))
                    ts(ssum[:, n, :], ex2[:, n, :], 1.0, None, ALU.add).then_inc(sem[r], 1)
                    yield
                    v.wait_ge(sem[r], nth(r, b, 5))
                    v.reciprocal(w12[:, n, 0, :], ssum[:, n, :]).then_inc(sem[r], 1)
                    yield
                    v.wait_ge(sem[r], nth(r, b, 6))
                    tt(w12[:, n, 1, :], w12[:, n, 0, :], ex2[:, n, :], ALU.mult).then_inc(sem[r], 1)
                    yield
                    v.wait_ge(sem[r], nth(r, b, 7))
                    for i in range(2):
                        tt(mk[:, n, i, :].rearrange("p (t e) -> p t e", e=E), eq[:, n, i, :, :],
                           w12[:, n, i, :].unsqueeze(2).to_broadcast([128, NT, E]), ALU.mult).then_inc(sem[r], 1)
                    yield
                    v.wait_ge(sem[r], nth(r, b, 9))
                    tt(mk[:, n, 2, :], mk[:, n, 0, :], mk[:, n, 1, :], ALU.add).then_inc(sem[f"mask{n}"], 1)
                    m = f"mp{n}"
                    yield
                    v.wait_ge(sem[f"mask{n}"], nth(f"mask{n}", b))
                    v.tensor_copy(mk3[:, n, 0, :], mk[:, n, 2, :]).then_inc(sem[m], 1)
                    yield
                    v.wait_ge(sem[m], nth(m, b, 1))
                    tt(mk_r[:, n, 0, :], mk[:, n, 2, :], mk3[:, n, 0, :], ALU.subtract).then_inc(sem[m], 1)
                    yield
                    v.wait_ge(sem[m], nth(m, b, 2))
                    v.tensor_copy(mk3[:, n, 1, :], mk_r[:, n, 0, :]).then_inc(sem[m], 1)
                    yield
                    v.wait_ge(sem[m], nth(m, b, 3))
                    tt(mk_r[:, n, 1, :], mk_r[:, n, 0, :], mk3[:, n, 1, :], ALU.subtract).then_inc(sem[m], 1)
                    yield
                    v.wait_ge(sem[m], nth(m, b, 4))
                    v.tensor_copy(mk3[:, n, 2, :], mk_r[:, n, 1, :]).then_inc(sem[m], 1)
                return fn

            def ffn(b, e):
                e = e - 1
                if e < 0:
                    return
                v.wait_ge(sem["w2_0_done"], nth("w2_0_done", b, e + 1))
                src = pB[:, 2, 0:HALF]
                bias = w("b2_0", cols=(e, e + 1))
                if e == 0:
                    v.wait_ge(sem["h1_ready"], nth("h1_ready", b))
                    stt(out=acc[:, 0, :], in0=src, scalar=bias, in1=h1[:, :], op0=ALU.add, op1=ALU.add).then_inc(sem["y0"], 1)
                else:
                    if e == 1:
                        v.wait_ge(sem["mbc0_in"], nth("mbc0_in", b))
                    if e >= 3:
                        v.wait_ge(sem["acc0"], nth("acc0", b, e - 2))
                    stt(out=ye[:, (e - 1) % 2, :], in0=src, scalar=bias, in1=mbc[:, 0, e - 1, :], op0=ALU.add, op1=ALU.mult).then_inc(sem["y0"], 1)

            def conv(b):
                v.wait_ge(sem["xi_ready"], nth("xi_ready", b))
                cw = [w("conv_w", cols=(i, i + 1)) for i in range(DC)]
                ts(cv[:, 0, :], xip[:, 0:S], cw[0], None, ALU.mult).then_inc(sem["conv"], 1)
                for i in range(1, DC):
                    yield
                    v.wait_ge(sem["conv"], nth("conv", b, i))
                    stt(out=cv[:, i % 2, :], in0=xip[:, i:i + S], scalar=cw[i], in1=cv[:, (i - 1) % 2, :], op0=ALU.mult, op1=ALU.add).then_inc(sem["conv"], 1)

            def xproj(b):
                v.wait_ge(sem["xp_done"], nth("xp_done", b))
                v.tensor_copy(Cr[:, :], pB[:, 2, :]).then_inc(sem["cr_ready"], 1)

            def softplus(b):
                v.wait_ge(sem["sp_exp"], nth("sp_exp", b))
                ts(cv[:, 1, :], sp[:, 1, :], 1.0, None, ALU.add).then_inc(sem["sp_u1"], 1)
                yield
                v.wait_ge(sem["sp_u1"], nth("sp_u1", b))
                stt(out=cv[:, 0, :], in0=cv[:, 1, :], scalar=1.0, in1=sp[:, 1, :], op0=ALU.subtract, op1=ALU.subtract).then_inc(sem["sp_r"], 1)
                yield
                v.wait_ge(sem["sp_r"], nth("sp_r", b))
                v.wait_ge(sem["sp_relu"], nth("sp_relu", b))
                tt(sp[:, 0, :], sp[:, 0, :], cv[:, 0, :], ALU.subtract).then_inc(sem["sp_t"], 1)
                yield
                v.wait_ge(sem["sp_ln"], nth("sp_ln", b))
                v.wait_ge(sem["sp_t"], nth("sp_t", b))
                tt(dd[:, 0, :], dd[:, 1, :], sp[:, 0, :], ALU.add).then_inc(sem["dt_ready"], 1)
                yield
                v.wait_ge(sem["u_ready"], nth("u_ready", b))
                v.wait_ge(sem["dt_ready"], nth("dt_ready", b))
                tt(dd[:, 1, :], dd[:, 0, :], u[:, :], ALU.mult).then_inc(sem["dx_ready"], 1)

            def dsplit(b):
                for i in range(2):
                    yield
                    v.wait_ge(sem["d_hi"], nth("d_hi", b, i + 1))
                    tt(dd_r[:, i, :], dd[:, i, :], dp[:, i, 0, :], ALU.subtract).then_inc(sem["d_r"], 1)
                for i in range(2):
                    yield
                    v.wait_ge(sem["d_mid"], nth("d_mid", b, i + 1))
                    tt(dp[:, i, 2, :], dd_r[:, i, :], dp[:, i, 1, :], ALU.subtract).then_inc(sem["d_lo"], 1)

            def grp(b, k):
                if k == GROUPS:
                    return
                v.wait_ge(sem["spread"], nth("spread", b, k + 1))
                if k == 0:
                    v.wait_ge(sem["br_ready"], nth("br_ready", b))
                if k >= 2:
                    v.wait_ge(sem["scanned"], nth("scanned", b, k - 1))
                tt(dBu[:, k % 2, :], pC[:, 1, :], Br[:, :], ALU.mult).then_inc(sem["dbu_ready"], 1)
                yield
                v.wait_ge(sem["dbu_ready"], nth("dbu_ready", b, k + 1))
                v.wait_ge(sem["da_ready"], nth("da_ready", b, k + 1))
                if k >= 2:
                    v.wait_ge(sem["hc_ready"], nth("hc_ready", b, k - 1))
                v.tensor_tensor_scan(hst[:, k % 2, :], dA[:, k % 2, :], dBu[:, k % 2, :], 0.0, ALU.mult, ALU.add).then_inc(sem["scanned"], 1)

            def yout(b):
                v.wait_ge(sem["y_sum"], nth("y_sum", b))
                stt(out=y1, in0=u[:, :], scalar=w("d_ssm"), in1=pC[:, 2, :], op0=ALU.mult, op1=ALU.add).then_inc(sem["y1"], 1)
                yield
                v.wait_ge(sem["y1"], nth("y1", b))
                v.wait_ge(sem["sz_ready"], nth("sz_ready", b))
                tt(y2, y1, sz[:, :], ALU.mult).then_inc(sem["y2"], 1)
                yield
                v.wait_ge(sem["out_done"], nth("out_done", b))
                for x_ in range(2):
                    last = stt(out=sres[half(x_), :], in0=pC[half(x_), 0, 0:HALF], scalar=w("b_out", half(x_)), in1=x3z[half(x_), x_, :], op0=ALU.add, op1=ALU.add)
                last.then_inc(sem["s_ready"], 1)

            def ln4_out(b):
                for x_ in range(2):
                    last = ts(ylz[half(x_), x_, :], ln_o[4][half(x_), :], w("g1", half(x_)), w("be1", half(x_)), ALU.mult, ALU.add)
                last.then_inc(sem["yln"], 1)

            def fc2(b):
                v.wait_ge(sem["yln"], nth("yln", b))
                v.wait_ge(sem["ff_ready"], nth("ff_ready", b))
                for x_ in range(2):
                    last = tt(s2[half(x_), :], ylz[half(x_), x_, :], ff[half(x_), :], ALU.add)
                last.then_inc(sem["s2_ready"], 1)

            def ln5_out(b):
                ts(yy[:, :], ln_o[5], w("g2"), w("be2"), ALU.mult, ALU.add).then_inc(sem["yy"], 1)
                yield
                v.wait_ge(sem["yy"], nth("yy", b))
                v.wait_ge(sem["h2_taken"], nth("h2_taken", b))
                tt(h3[:, :], yy[:, :], h2b[:, :], ALU.add).then_inc(sem["h3_ready"], 1)

            def ln7_out(b):
                for x_ in range(2):
                    last = ts(x6z[half(x_), x_, :], ln_o[7][half(x_), :], w("g_m", half(x_)), w("be_m", half(x_)), ALU.mult, ALU.add)
                last.then_inc(sem["x6_ready"], 1)

            def exp(b, i):
                for e in range(2 * i - 2, 2 * i):
                    if e < 0:
                        continue
                    yield
                    v.wait_ge(sem["w2_1_done"], nth("w2_1_done", b, e // 2 + 1))
                    if e == 0:
                        v.wait_ge(sem["mbc1_in"], nth("mbc1_in", b))
                    if e >= 2:
                        v.wait_ge(sem["acc1"], nth("acc1", b, e - 1))
                    stt(out=yeb[:, e % 2, :], in0=pC[:, 2, HALF * (e % 2):HALF * (e % 2) + HALF], scalar=w("b2_1", cols=(e, e + 1)),
                        in1=mbc[:, 1, e, :], op0=ALU.add, op1=ALU.mult).then_inc(sem["y1e"], 1)

            def turn(b):
                v.wait_ge(sem["out_turned"], nth("out_turned", b))
                if not_first(b):
                    v.wait_ge(sem["stored"], nth("stored", b, 0))
                v.tensor_copy(outs[:, :, :], pC[:, 0, 0:256].rearrange("p (c n) -> p c n", c=2)).then_inc(sem["out_ready"], 1)

            steps = {f"ln{j}b": ln_b(j) for j in range(NLN)} | {f"ln{j}c": ln_c(j) for j in range(NLN)}
            steps |= {"gather": gather, "tok": tok, "feat": feat, "qkv": qkv, "split": split, "s1": s1_, "msplit": msplit,
                      "den": den, "wo": wo, "router0": router(0), "router1": router(1),
                      "ffn": ffn, "conv": conv, "xproj": xproj, "softplus": softplus, "dsplit": dsplit,
                      "grp": grp, "yout": yout, "fc2": fc2, "exp": exp, "turn": turn}
            turns(v, "DVE", steps)

        @block.tensor
        def _(pe):
            mm = nc.tensor.matmul
            pe.wait_ge(s_w, 16)
            pe.wait_ge(s_c, made["early"])

            def ln_a(j, x, ready, k=None):
                def fn(b):
                    side, i, bank, n = ln_of(j)
                    pe.wait_ge(sem[ready], nth(ready, b, k))
                    if j == 2 and not_first(b):
                        pe.wait_ge(sem["cr_ready"], nth("cr_ready", b, 0))
                        pe.wait_ge(sem["sp_relu"], nth("sp_relu", b, 0))
                    mm(bank[:, 0:HALF], centre[:, :], x, start=True, stop=True).then_inc(sem[side + "_centred"], 1)
                return fn

            def ln_b(j):
                def fn(b):
                    side, i, bank, n = ln_of(j)
                    pe.wait_ge(sem[side + "_squared"], nth(side + "_squared", b, i + 1))
                    for c in range(2):
                        last = mm(bank[:, HALF + 2 * c:HALF + 2 * c + 2], ln_sq[:, n, 128 * c:128 * c + 128], halfmean[:, :], start=True, stop=True)
                    last.then_inc(sem[side + "_var"], 1)
                return fn

            def ln_c(j):
                def fn(b):
                    side, i, bank, n = ln_of(j)
                    pe.wait_ge(sem[side + "_rstd"], nth(side + "_rstd", b, i + 1))
                    for c in range(2):
                        for x_ in range(2):
                            last = mm(bank[half(x_), HALF + 128 * c:HALF + 128 * c + 128],
                                      ln_rs[:, n, 2 * c + x_:2 * c + x_ + 1].to_broadcast([128, 64]), ident[:, :], start=True, stop=True)
                    last.then_inc(sem[side + "_bc"], 1)
                return fn

            def tok(b):
                if not_first(b):
                    pe.wait_ge(sem["h1_ready"], nth("h1_ready", b, 0))
                pe.wait_ge(sem["rows_in"], nth("rows_in", b))
                for t in range(NT):
                    nc.tensor.transpose(pA[:, 0, 128 * t:128 * t + 128], rows[:, t, 0:128], ident[:, :])
                    last = nc.tensor.transpose(pA[0:VIS, 1, 128 * t:128 * t + 128], rows[:, t, 128:ROW], ident[:, :])
                last.then_inc(sem["tok_transposed"], 1)

            def feat(b):
                pe.wait_ge(sem["eg_ready"], nth("eg_ready", b))
                pe.wait_ge(sem["valid_ready"], nth("valid_ready", b))
                for c in range(2):
                    for x_ in range(2):
                        t = 2 * x_ + c
                        mm(pA[half(x_), 0, 128 * c:128 * c + 128], rows[:, t, 0:64], ident[:, :], start=True, stop=True)
                for c in range(2):
                    for x_ in range(2):
                        t = 2 * x_ + c
                        last = mm(pA[half(x_), 0, HALF + 128 * c:HALF + 128 * c + 128], valid[:, t:t + 1].to_broadcast([128, 64]), ident[:, :], start=True, stop=True)
                last.then_inc(sem["emb_turned"], 1)
                yield
                pe.wait_ge(sem["vis_ready"], nth("vis_ready", b))
                mm(pA[:, 1, :], w("w_eg"), eg[:, :], start=True, stop=True).then_inc(sem["feat_done"], 1)
                yield
                pe.wait_ge(sem["ev_ready"], nth("ev_ready", b))
                mm(pA[0:64, 0, :], w("w_vis"), vis[:, :], start=True, stop=True).then_inc(sem["feat_done"], 1)

            def fuse(b):
                pe.wait_ge(sem["cat_ready"], nth("cat_ready", b))
                for x_ in range(2):
                    mm(pA[half(x_), 1, 0:HALF], w("w_f1"), cat1[:, HALF * x_:HALF * x_ + HALF], start=True, stop=False)
                for x_ in range(2):
                    last = mm(pA[half(x_), 1, 0:HALF], w("w_f2"), cat2[:, HALF * x_:HALF * x_ + HALF], start=False, stop=True)
                last.then_inc(sem["fuse_done"], 1)

            def qkv(b):
                if not not_first(b):
                    pe.wait_ge(s_wr, 16)
                    pe.wait_ge(s_c, made["pool"])
                    pe.wait_ge(s_v, made["dve"])
                pe.wait_ge(sem["lnA_out"], nth("lnA_out", b, 2))
                mm(pA[:, 0, :], w("w_qk"), x1z, start=True, stop=True).then_inc(sem["qk_done"], 1)
                for t in range(NT):
                    last = mm(pA[:, 1, 128 * t:128 * t + 128], x1z[:, t // 2, 128 * (t % 2):128 * (t % 2) + 128], w("w_v"), start=True, stop=True)
                last.then_inc(sem["v_done"], 1)

            def s1_(b, n):
                if n == 0:
                    pe.wait_ge(sem["qk_full"], nth("qk_full", b))
                    pe.wait_ge(sem["v_ready"], nth("v_ready", b))
                    pe.wait_ge(sem["stack_in"], nth("stack_in", b))
                for i in range(2):
                    if i:
                        yield
                    if n >= 1:
                        pe.wait_ge(sem["max_done"], nth("max_done", b, 2 * n + i - 1))
                    h = 2 * (n % 2) + i
                    mm(pA[:, i, :], QS[0:96, h, 128 * (n // 2):128 * (n // 2) + 128], KS[0:96, h, :], start=True, stop=True).then_inc(sem["s1_done"], 1)

            def msplit(b):
                pe.wait_ge(sem["max_split"], nth("max_split", b))
                for t in range(NT):
                    for h in range(NH):
                        last = nc.tensor.transpose(turned[96:128, h, 128 * t:128 * t + 128], M[:, NH * t + h, :], identb[:, :])
                last.then_inc(sem["max_turned"], 1)

            def s2_(b, n):
                if n == 0:
                    pe.wait_ge(sem["max_in"], nth("max_in", b))
                for k in (2 * n, 2 * n + 1):
                    if k > 2 * n:
                        yield
                    if k:
                        pe.wait_ge(sem["exp_done"], nth("exp_done", b, k))
                    kt, h = k // NH, k % NH
                    mm(pA[:, 0, :], KS[:, h, 128 * kt:128 * kt + 128], QS[:, h, :], start=True, stop=True).then_inc(sem["s2_done"], 1)
                if n >= 3 and n % 2 == 1:
                    yield
                    pv(b, (n - 3) // 2)

            def pv(b, kt):
                pe.wait_ge(sem["exp_done"], nth("exp_done", b, NH * kt + NH))
                for h in range(NH):
                    last = mm(pA[32 * h:32 * h + 32, 1, :], vsb[:, kt, 32 * h:32 * h + 32], P[:, (NH * kt + h) % 8, :],
                              start=(kt == 0), stop=(kt == NT - 1))
                last.then_inc(sem["pv_done"], 1)

            def den(b):
                pv(b, NT - 1)
                yield
                pe.wait_ge(sem["o_ready"], nth("o_ready", b))
                mm(pA[:, 0, :], sel_den[:, :], osb[:, :], start=True, stop=True).then_inc(sem["den_done"], 1)

            def wo(b):
                pe.wait_ge(sem["o_bf"], nth("o_bf", b))
                for p in range(3):
                    for x_ in range(2):
                        last = mm(pA[half(x_), 1, 0:HALF], wo3[:, p, :], obf[:, HALF * x_:HALF * x_ + HALF], start=(p == 0), stop=(p == 2))
                last.then_inc(sem["wo_done"], 1)

            def logit(n, x, wr, bank, ready, k=None):
                def fn(b):
                    pe.wait_ge(sem[ready], nth(ready, b, k))
                    for t in range(NT):
                        last = mm(bank[:, 0, E * t:E * t + E], x[:, t // 2, 128 * (t % 2):128 * (t % 2) + 128], wr, start=True, stop=True)
                    last.then_inc(sem[f"lg{n}_done"], 1)
                return fn

            def mask_bc(n, e, out_):
                for c in range(2):
                    for x_ in range(2):
                        last = mm(out_[half(x_), 128 * c:128 * c + 128], sel_m[:, E * (2 * x_ + c) + e, :], mt[:, n, :], start=True, stop=True)
                return last

            def mask(n, bank):
                def fn(b):
                    pe.wait_ge(sem[f"mp{n}"], nth(f"mp{n}", b))
                    nc.tensor.transpose(bank[0:96, 2, 0:64].bitcast(bf16), mk3[:, n, :, :].rearrange("p i t -> p (i t)"), identb[:, :]).then_inc(sem[f"mt{n}_done"], 1)
                    yield
                    pe.wait_ge(sem[f"mt{n}_in"], nth(f"mt{n}_in", b))
                    for i in range(2):
                        if i:
                            yield
                        if i:
                            pe.wait_ge(sem[f"mbc{n}_in"], nth(f"mbc{n}_in", b, 1))
                        for e in range(4):
                            last = mask_bc(n, 4 * i + e, bank[:, e // 2, HALF * (e % 2):HALF * (e % 2) + HALF])
                        last.then_inc(sem[f"mbc{n}_done"], 1)
                return fn

            def ffn(b, e):
                if e < 9:
                    if e == 0:
                        pe.wait_ge(sem["mbc0_in"], nth("mbc0_in", b))
                    for ch in range(2):
                        if ch:
                            yield
                        if e >= 1:
                            pe.wait_ge(sem["gelu0"], nth("gelu0", b, 2 * e - 1 + ch))
                        mm(pB[:, ch, :], w("w1_0", cols=(128 * (2 * e + ch), 128 * (2 * e + ch) + 128)), x2z, start=True, stop=True).then_inc(sem["hid0_done"], 1)
                e = e - 1
                if e < 0:
                    return
                yield
                pe.wait_ge(sem["gelu0"], nth("gelu0", b, 2 * e + 2))
                if e >= 1:
                    pe.wait_ge(sem["y0"], nth("y0", b, e))
                for ch in range(2):
                    for x_ in range(2):
                        last = mm(pB[half(x_), 2, 0:HALF], w("w2_0", cols=(64 * (2 * e + ch), 64 * (2 * e + ch) + 64)),
                                  hid[:, e % 2, ch, HALF * x_:HALF * x_ + HALF], start=(ch == 0), stop=(ch == 1), skip_group_check=True)
                last.then_inc(sem["w2_0_done"], 1)

            def inproj(b):
                pe.wait_ge(sem["lnB_out"], nth("lnB_out", b, 2))
                mm(pB[:, 0, :], w("w_inx"), x3z, start=True, stop=True)
                mm(pB[:, 1, :], w("w_inz"), x3z, start=True, stop=True).then_inc(sem["in_done"], 1)

            def xproj(b):
                pe.wait_ge(sem["sz_ready"], nth("sz_ready", b))
                pe.wait_ge(sem["u_ready"], nth("u_ready", b))
                mm(pB[0:DTR, 0, :], w("w_xdt"), u[:, :], start=True, stop=True)
                mm(pB[:, 1, :], w("w_xb"), u[:, :], start=True, stop=True)
                mm(pB[:, 2, :], w("w_xc"), u[:, :], start=True, stop=True).then_inc(sem["xp_done"], 1)

            def dtproj(b):
                pe.wait_ge(sem["dtl_ready"], nth("dtl_ready", b))
                mm(pB[:, 0, :], w("w_dt"), dtl[:, :], start=True, stop=True).then_inc(sem["dtp_done"], 1)

            def ysum(b, r):
                pe.wait_ge(sem["hc_ready"], nth("hc_ready", b, 4 * r + 4))
                for s in range(4):
                    last = mm(pC[32 * s:32 * s + 32, 2, :], sel_y[:, r, :], hc[:, s, :], start=(r == 0), stop=(r == 3))
                last.then_inc(sem["y_sum"], 1)

            def grp(b, k):
                if k < GROUPS:
                    s, r = k % 4, k // 4
                    if k == 0:
                        pe.wait_ge(sem["br_ready"], nth("br_ready", b))
                        pe.wait_ge(sem["cr_ready"], nth("cr_ready", b))
                        pe.wait_ge(sem["dstack_in"], nth("dstack_in", b))
                        if not_first(b):
                            pe.wait_ge(sem["out_ready"], nth("out_ready", b, 0))
                    else:
                        pe.wait_ge(sem["da_ready"], nth("da_ready", b, k))
                        pe.wait_ge(sem["dbu_ready"], nth("dbu_ready", b, k))
                    mm(pC[:, 0, :], sel_dn[:, s, :], T[:, 0, S * r:S * r + S], start=True, stop=True)
                    mm(pC[:, 1, :], sel_dn[:, s, :], T[:, 1, S * r:S * r + S], start=True, stop=True).then_inc(sem["spread"], 1)
                    if k >= 5 and k % 4 == 1:
                        yield
                        ysum(b, (k - 5) // 4)
                else:
                    ysum(b, 3)

            def yout(b):
                pe.wait_ge(sem["y2"], nth("y2", b))
                for x_ in range(2):
                    last = mm(pC[half(x_), 0, 0:HALF], w("w_out"), y2[:, HALF * x_:HALF * x_ + HALF], start=True, stop=True)
                last.then_inc(sem["out_done"], 1)

            def fc1(b):
                pe.wait_ge(sem["yln"], nth("yln", b))
                for ch in range(2):
                    last = mm(pC[:, ch, :], w("fc1", cols=(128 * ch, 128 * ch + 128)), ylz, start=True, stop=True)
                last.then_inc(sem["fc1_done"], 1)

            def fc2(b):
                pe.wait_ge(sem["fc1_act"], nth("fc1_act", b))
                for ch in range(2):
                    for x_ in range(2):
                        last = mm(pC[half(x_), 2, 0:HALF], w("fc2", cols=(64 * ch, 64 * ch + 64)), hidb[:, 0, ch, HALF * x_:HALF * x_ + HALF], start=(ch == 0), stop=(ch == 1))
                last.then_inc(sem["fc2_done"], 1)

            def exp(b, i):
                if i < E // 2:
                    if i == 0:
                        pe.wait_ge(sem["mbc1_in"], nth("mbc1_in", b))
                    for n in range(2):
                        e = 2 * i + n
                        if i:
                            pe.wait_ge(sem["gelu1"], nth("gelu1", b, 2 * i - 1 + n))
                        mm(pC[:, n, :], w("w1_1", cols=(128 * e, 128 * e + 128)), x6z, start=True, stop=True).then_inc(sem["hid1_done"], 1)
                i = i - 1
                if i < 0:
                    return
                yield
                pe.wait_ge(sem["gelu1"], nth("gelu1", b, 2 * i + 2))
                if i >= 1:
                    pe.wait_ge(sem["y1e"], nth("y1e", b, 2 * i))
                for n in range(2):
                    e = 2 * i + n
                    for x_ in range(2):
                        last = mm(pC[half(x_), 2, HALF * n:HALF * n + HALF], w("w2_1", cols=(64 * e, 64 * e + 64)),
                                  hidb[:, i % 2, n, HALF * x_:HALF * x_ + HALF], start=True, stop=True)
                last.then_inc(sem["w2_1_done"], 1)

            def turn(b):
                pe.wait_ge(sem["acc1"], nth("acc1", b))
                for c in range(2):
                    last = nc.tensor.transpose(pC[:, 0, 128 * c:128 * c + 128], h4[:, 128 * c:128 * c + 128], ident[:, :])
                last.then_inc(sem["out_turned"], 1)

            steps = {f"ln{j}b": ln_b(j) for j in range(NLN)} | {f"ln{j}c": ln_c(j) for j in range(NLN)}
            steps |= {"ln0a": ln_a(0, f0[:, :], "fuse_act"), "ln1a": ln_a(1, h0[:, :], "h0_ready"),
                      "ln2a": ln_a(2, h1[:, :], "h1_ready"), "ln3a": ln_a(3, h2[:, :], "acc0"),
                      "ln4a": ln_a(4, sres[:, :], "s_ready"), "ln5a": ln_a(5, s2[:, :], "s2_ready"),
                      "ln6a": ln_a(6, h3[:, :], "h3_ready"), "ln7a": ln_a(7, ln_o[6], "lnC_out", 3),
                      "tok": tok, "feat": feat, "fuse": fuse, "qkv": qkv, "s1": s1_,
                      "msplit": msplit, "s2": s2_, "den": den, "wo": wo,
                      "logit0": logit(0, x2z, w("wr0"), pB, "lnB_out", 1), "mask0": mask(0, pB), "ffn": ffn,
                      "inproj": inproj, "xproj": xproj, "dtproj": dtproj, "grp": grp, "yout": yout,
                      "fc1": fc1, "fc2": fc2, "logit1": logit(1, x6z, w("wr1"), pC, "x6_ready"),
                      "mask1": mask(1, pC), "exp": exp, "turn": turn}
            turns(pe, "PE", steps)


def kernel(**inputs):
    import concourse.bacc as bacc
    from concourse.bass_utils import run_bass_kernel_spmd

    p = {k: np.asarray(v) for k, v in inputs.items()}
    wts = np.zeros((128, WCOLS), np.float32)

    def put(name, a, row=0, col=0):
        a = a if a.ndim == 2 else a[:, None]
        at = AT[name][0] + col
        wts[row:row + a.shape[0], at:at + a.shape[1]] = a

    def twice(name, a, col=0):
        put(name, a, 0, col)
        put(name, a, 64, col)

    put("w_eg", p["L0_tok_w_item"]); put("w_eg", p["L0_tok_w_geo"], 64, 64)
    put("b_eg", p["L0_tok_b_item"]); put("b_eg", p["L0_tok_b_geo"], 64)
    put("w_vis", p["L0_tok_w_visit"]); put("b_vis", p["L0_tok_b_visit"])
    put("w_f1", p["L0_tok_w_fuse"][:128]); put("w_f2", p["L0_tok_w_fuse"][128:])
    twice("b_f", p["L0_tok_b_fuse"]); twice("g_t", p["L0_tok_ln_gamma"]); twice("be_t", p["L0_tok_ln_beta"])
    dh = np.arange(NH * DH).reshape(NH, DH).T.reshape(-1)
    twice("w_qk", p["L0_attn_Wq"][dh].T); twice("w_qk", p["L0_attn_Wk"][dh].T, 64)
    put("b_qk", p["L0_attn_bq"][dh]); put("b_qk", p["L0_attn_bk"][dh], 64)
    for h in range(NH):
        hs = slice(DH * h, DH * h + DH)
        twice("w_v", p["L0_attn_Wv"][hs].T, 32 * h)
        put("w_o", p["L0_attn_Wo"][:, hs].T, 32 * h)
        put("bv", np.tile(p["L0_attn_bv"][hs], (128, 1)), 0, 32 * h)
        put("bv", np.ones((128, 1), np.float32), 0, 32 * h + DH)
    twice("b_o", p["L0_attn_bo"])
    twice("wr0", p["L0_ffn_Wr"]); twice("wr1", p["L1_ffn_Wr"])
    for e in range(9):
        w1 = p["L0_ffn_W1s"] if e == 0 else p["L0_ffn_W1p"][e - 1]
        b1 = p["L0_ffn_b1s"] if e == 0 else p["L0_ffn_b1p"][e - 1]
        w2 = p["L0_ffn_W2s"] if e == 0 else p["L0_ffn_W2p"][e - 1]
        b2 = p["L0_ffn_b2s"] if e == 0 else p["L0_ffn_b2p"][e - 1]
        twice("w1_0", w1, F0 * e)
        for ch in range(2):
            put("w2_0", w2[128 * ch:128 * ch + 128], 0, 64 * (2 * e + ch))
            put("b1_0", b1[128 * ch:128 * ch + 128], 0, 2 * e + ch)
        twice("b2_0", b2, e)
    twice("w_inx", p["L1_attn_in_proj_w"][:DI].T); twice("w_inz", p["L1_attn_in_proj_w"][DI:].T)
    put("b_inx", p["L1_attn_in_proj_b"][:DI]); put("b_inz", p["L1_attn_in_proj_b"][DI:])
    put("conv_w", p["L1_attn_conv_w"]); put("conv_b", p["L1_attn_conv_b"])
    xp = p["L1_attn_x_proj_w"]
    put("w_xdt", xp[:DTR].T)
    put("w_xb", np.tile(xp[DTR:DTR + NS].T, (1, 8))); put("w_xc", np.tile(xp[DTR + NS:].T, (1, 8)))
    put("w_dt", p["L1_attn_dt_proj_w"].T); put("b_dt", p["L1_attn_dt_proj_b"])
    put("a_log", p["L1_attn_A_log"].reshape(4, 8, 4, NS).transpose(1, 3, 2, 0).reshape(128, GROUPS))
    put("d_ssm", p["L1_attn_D_ssm"]); put("w_out", p["L1_attn_out_proj_w"].T); twice("b_out", p["L1_attn_out_proj_b"])
    twice("g1", p["L1_attn_ln1_g"]); twice("be1", p["L1_attn_ln1_b"])
    twice("g2", p["L1_attn_ln2_g"]); twice("be2", p["L1_attn_ln2_b"])
    twice("fc1", p["L1_attn_fc1_w"].T)
    for ch in range(2):
        put("fc2", p["L1_attn_fc2_w"].T[128 * ch:128 * ch + 128], 0, 64 * ch)
        put("b_fc1", p["L1_attn_fc1_b"][128 * ch:128 * ch + 128], 0, ch)
    twice("b_fc2", p["L1_attn_fc2_b"])
    twice("g_m", p["L1_ffn_gamma"]); twice("be_m", p["L1_ffn_beta"])
    put("br1", np.tile(p["L1_ffn_br"], (128, NT)))
    put("iota", np.tile(np.arange(E, dtype=np.float32), (128, NT)))
    for e in range(E):
        twice("w1_1", p["L1_ffn_W1"][e], F1 * e)
        put("w2_1", p["L1_ffn_W2"][e], 0, 64 * e)
        put("b1_1", p["L1_ffn_b1"][e], 0, e)
        twice("b2_1", p["L1_ffn_b2"][e], e)
    arrays = {
        "ids": np.ascontiguousarray(p["x"].reshape(NB * NT, 128).T),
        "table": np.concatenate([p["L0_tok_emb_table"], p["L0_tok_geo_table"], p["L0_tok_visit_table"]], axis=1),
        "weights": wts,
    }
    nc = bacc.Bacc("TRN2", target_bir_lowering=False, num_devices=1)
    args = [nc.dram_tensor(f"in_{n}", a.shape, mybir.dt.from_np(a.dtype), kind="ExternalInput").ap() for n, a in arrays.items()]
    args.append(nc.dram_tensor("out_h", (NB, S, D), mybir.dt.float32, kind="ExternalOutput").ap())
    build_tower(nc, *args)
    r = run_bass_kernel_spmd(nc, [{f"in_{n}": a for n, a in arrays.items()}], core_ids=[0])
    return r.results[0]["out_h"]
```
